# Optimizing a Trainium2 kernel written in Bass

```python
import numpy as np
import jax
import jax.numpy as jnp

def _softmax(x, axis=-1):
    return jax.nn.softmax(x, axis=axis)

def _gelu(x):
    return jax.nn.gelu(x, approximate=True)

def _silu(x):
    return jax.nn.silu(x)

def _sigmoid(x):
    return jax.nn.sigmoid(x)

def _layernorm(x, axis=-1, eps=1e-05):
    m = jnp.mean(x, axis=axis, keepdims=True)
    v = jnp.var(x, axis=axis, keepdims=True)
    return (x - m) / jnp.sqrt(v + eps)

def _scatter_add(tgt, idx, src, axis=0):
    return tgt.at[idx].add(src)

def _segment_sum(src, seg, n):
    return jax.ops.segment_sum(src, seg, n)
kernel_name = 'mk_adaln_ffn_d2_seqx_r4_6b02e6'

def setup_inputs(seed: int=0):
    np.random.seed(seed)
    _w = jnp.asarray

    def _rec_inputs():
        import jax
        import jax.numpy as jnp
        _rk = jax.random.key(seed)
        x = -7.109e-05 + 0.9999 * jax.random.normal(jax.random.fold_in(_rk, 1), (32, 64, 512), jnp.float32)
        _lenS = 64 - jax.random.randint(jax.random.fold_in(_rk, 7), (32,), 0, max(1, 64 // 4) + 1, jnp.int32)
        _lenS2 = 64 - jax.random.randint(jax.random.fold_in(_rk, 8), (32,), 0, max(1, 64 // 4) + 1, jnp.int32)
        itok_B_0_7 = jax.random.randint(jax.random.fold_in(_rk, 11), (32,), 0, 8, jnp.int32)
        itok_Bx257_0_4111 = jax.random.randint(jax.random.fold_in(_rk, 12), (32, 257), 0, 1028, jnp.int32)
        itok_B_37_3939 = jax.random.randint(jax.random.fold_in(_rk, 13), (32,), 37, 985, jnp.int32)
        return (x, itok_B_0_7, itok_Bx257_0_4111, itok_B_37_3939)
    x, itok_B_0_7, itok_Bx257_0_4111, itok_B_37_3939 = _rec_inputs()

    def _L0_cond_setup():
        import jax, jax.numpy as jnp
        import numpy as np
        B, C, D, T, N_SUBJECTS = (128, 64, 64, 512, 8)
        key = jax.random.key(seed)
        kx, ks, kw = jax.random.split(key, 3)
        x = jax.random.normal(kx, (B, C, T), dtype=jnp.float32)
        subjects = jax.random.randint(ks, (B,), 0, N_SUBJECTS, dtype=jnp.int64)
        weights = jax.random.normal(kw, (N_SUBJECTS, C, D), dtype=jnp.float32) * (1.0 / C ** 0.5)
        return {'x': x, 'subjects': subjects, 'weights': weights}
    _L0_cond_all = _L0_cond_setup()
    _L0_cond_in = {k: v for k, v in _L0_cond_all.items() if k in ('weights',)}
    del _L0_cond_all

    def _L0_ffn_setup():
        import jax, jax.numpy as jnp
        import numpy as np
        HIDDEN = 512
        INTER = 1408
        B, S = (2, 512)

        def _ternary(key, shape):
            return jax.random.randint(key, shape, -1, 2).astype(jnp.float32)
        key = jax.random.key(seed)
        ks = jax.random.split(key, 7)
        x = jax.random.normal(ks[0], (B, S, HIDDEN), dtype=jnp.float32)
        gate_w = _ternary(ks[1], (INTER, HIDDEN))
        up_w = _ternary(ks[2], (INTER, HIDDEN))
        down_w = _ternary(ks[3], (HIDDEN, INTER))
        gate_s = jax.random.uniform(ks[4], (INTER,), minval=0.01, maxval=0.1, dtype=jnp.float32)
        up_s = jax.random.uniform(ks[5], (INTER,), minval=0.01, maxval=0.1, dtype=jnp.float32)
        down_s = jax.random.uniform(ks[6], (HIDDEN,), minval=0.01, maxval=0.1, dtype=jnp.float32)
        return {'x': x, 'gate_w': gate_w, 'up_w': up_w, 'down_w': down_w, 'gate_s': gate_s, 'up_s': up_s, 'down_s': down_s}
    _L0_ffn_all = _L0_ffn_setup()
    _L0_ffn_in = {k: v for k, v in _L0_ffn_all.items() if k in ('gate_w', 'up_w', 'down_w', 'gate_s', 'up_s', 'down_s')}
    del _L0_ffn_all

    def _L1_cond_setup():
        import jax, jax.numpy as jnp
        import numpy as np
        H, G, HD = (8, 4, 64)
        GSZ = H // G
        BLOCK = 16
        WINDOW = 256
        SCALE = 256.0 ** (-0.5)
        EPS = 1e-06
        THETA = 10000.0
        B, T, D = (16, 4, 512)
        NBLK = 257

        def _rms(x, scale):
            var = jnp.mean(x * x, axis=-1, keepdims=True)
            return x * jax.lax.rsqrt(var + EPS) * (1.0 + scale)

        def _rope(x, pos):
            half = HD // 2
            inv = 1.0 / THETA ** (jnp.arange(half, dtype=jnp.float32) / half)
            ang = pos[:, :, None].astype(jnp.float32) * inv
            cos = jnp.cos(ang)[:, None, :, :]
            sin = jnp.sin(ang)[:, None, :, :]
            x1, x2 = (x[..., :half], x[..., half:])
            return jnp.concatenate([x1 * cos - x2 * sin, x2 * cos + x1 * sin], axis=-1)
        key = jax.random.key(seed)
        ks = jax.random.split(key, 10)
        inv_d = 1.0 / np.sqrt(D)
        return {'x': jax.random.normal(ks[0], (B, T, D), jnp.float32), 'Wq': jax.random.normal(ks[1], (H * HD, D), jnp.float32) * inv_d, 'Wk': jax.random.normal(ks[2], (G * HD, D), jnp.float32) * inv_d, 'Wv': jax.random.normal(ks[3], (G * HD, D), jnp.float32) * inv_d, 'Wo': jax.random.normal(ks[4], (D, H * HD), jnp.float32) * inv_d, 'q_norm_scale': jax.random.normal(ks[5], (HD,), jnp.float32) * 0.02, 'k_norm_scale': jax.random.normal(ks[6], (HD,), jnp.float32) * 0.02, 'k_blocks': jax.random.normal(ks[7], (B * NBLK, G, BLOCK, HD), jnp.float32), 'v_blocks': jax.random.normal(ks[8], (B * NBLK, G, BLOCK, HD), jnp.float32), 'block_tables': jnp.arange(B * NBLK, dtype=jnp.int32).reshape(B, NBLK), 'kv_lens': jax.random.randint(ks[9], (B,), 0, 1024, dtype=jnp.int32)}
    _L1_cond_all = _L1_cond_setup()
    _L1_cond_in = {k: v for k, v in _L1_cond_all.items() if k in ('Wq', 'Wk', 'Wv', 'Wo', 'q_norm_scale', 'k_norm_scale', 'k_blocks', 'v_blocks')}
    del _L1_cond_all

    def _L1_ffn_setup():
        import jax, jax.numpy as jnp
        import numpy as np
        TOP_K = 2
        key = jax.random.key(seed)
        ks = jax.random.split(key, 7)
        B, S, H = (2, 512, 512)
        E, A, NS = (8, 64, 4096)
        x = jax.random.normal(ks[0], (B, S, H), jnp.float32)
        gate_w = jax.random.normal(ks[1], (E, H), jnp.float32) * 0.01
        W = jax.random.normal(ks[2], (H, H), jnp.float32) * 0.02
        atoms = jax.random.normal(ks[3], (A, NS), jnp.float32) * 0.02
        expert_atom_weights = jax.random.normal(ks[4], (E, A), jnp.float32) * 0.1
        importance = jax.random.normal(ks[5], (E, NS), jnp.float32) * 0.1
        mask_idx = jax.random.randint(ks[6], (NS,), 0, H * H, jnp.int32)
        return dict(x=x, gate_w=gate_w, W=W, atoms=atoms, expert_atom_weights=expert_atom_weights, importance=importance, mask_idx=mask_idx)
    _L1_ffn_all = _L1_ffn_setup()
    _L1_ffn_in = {k: v for k, v in _L1_ffn_all.items() if k in ('gate_w', 'W', 'atoms', 'expert_atom_weights', 'importance', 'mask_idx')}
    del _L1_ffn_all
    return {'x': x, 'itok_B_0_7': itok_B_0_7, 'itok_Bx257_0_4111': itok_Bx257_0_4111, 'itok_B_37_3939': itok_B_37_3939, 'L0_cond_weights': _L0_cond_in['weights'], 'L0_ffn_gate_w': _L0_ffn_in['gate_w'], 'L0_ffn_up_w': _L0_ffn_in['up_w'], 'L0_ffn_down_w': _L0_ffn_in['down_w'], 'L0_ffn_gate_s': _L0_ffn_in['gate_s'], 'L0_ffn_up_s': _L0_ffn_in['up_s'], 'L0_ffn_down_s': _L0_ffn_in['down_s'], 'L1_cond_Wq': _L1_cond_in['Wq'], 'L1_cond_Wk': _L1_cond_in['Wk'], 'L1_cond_Wv': _L1_cond_in['Wv'], 'L1_cond_Wo': _L1_cond_in['Wo'], 'L1_cond_q_norm_scale': _L1_cond_in['q_norm_scale'], 'L1_cond_k_norm_scale': _L1_cond_in['k_norm_scale'], 'L1_cond_k_blocks': _L1_cond_in['k_blocks'], 'L1_cond_v_blocks': _L1_cond_in['v_blocks'], 'L1_ffn_gate_w': _L1_ffn_in['gate_w'], 'L1_ffn_W': _L1_ffn_in['W'], 'L1_ffn_atoms': _L1_ffn_in['atoms'], 'L1_ffn_expert_atom_weights': _L1_ffn_in['expert_atom_weights'], 'L1_ffn_importance': _L1_ffn_in['importance'], 'L1_ffn_mask_idx': _L1_ffn_in['mask_idx']}

def reference(x, itok_B_0_7, itok_Bx257_0_4111, itok_B_37_3939, L0_cond_weights, L0_ffn_gate_w, L0_ffn_up_w, L0_ffn_down_w, L0_ffn_gate_s, L0_ffn_up_s, L0_ffn_down_s, L1_cond_Wq, L1_cond_Wk, L1_cond_Wv, L1_cond_Wo, L1_cond_q_norm_scale, L1_cond_k_norm_scale, L1_cond_k_blocks, L1_cond_v_blocks, L1_ffn_gate_w, L1_ffn_W, L1_ffn_atoms, L1_ffn_expert_atom_weights, L1_ffn_importance, L1_ffn_mask_idx):
    import jax
    import jax.numpy as jnp

    def _L0_cond_ref(x, subjects, weights):
        import jax, jax.numpy as jnp
        import numpy as np
        B, C, D, T, N_SUBJECTS = (128, 64, 64, 512, 8)
        w = weights[subjects]
        out = jnp.einsum('bct,bcd->bdt', x, w)
        return out

    def _L0_ffn_ref(x, gate_w, up_w, down_w, gate_s, up_s, down_s):
        import jax, jax.numpy as jnp
        import numpy as np
        HIDDEN = 512
        INTER = 1408
        B, S = (2, 512)

        def _ternary(key, shape):
            return jax.random.randint(key, shape, -1, 2).astype(jnp.float32)
        b, s, h = x.shape
        xf = x.reshape(b * s, h)
        g = jnp.einsum('th,ih->ti', xf, gate_w) * gate_s
        u = jnp.einsum('th,ih->ti', xf, up_w) * up_s
        hdn = jax.nn.silu(g) * u
        out = jnp.einsum('ti,hi->th', hdn, down_w) * down_s
        return out.reshape(b, s, -1)

    def _L1_cond_ref(x, Wq, Wk, Wv, Wo, q_norm_scale, k_norm_scale, k_blocks, v_blocks, block_tables, kv_lens):
        import jax, jax.numpy as jnp
        import numpy as np
        H, G, HD = (8, 4, 64)
        GSZ = H // G
        BLOCK = 16
        WINDOW = 256
        SCALE = 256.0 ** (-0.5)
        EPS = 1e-06
        THETA = 10000.0
        B, T, D = (16, 4, 512)
        NBLK = 257

        def _rms(x, scale):
            var = jnp.mean(x * x, axis=-1, keepdims=True)
            return x * jax.lax.rsqrt(var + EPS) * (1.0 + scale)

        def _rope(x, pos):
            half = HD // 2
            inv = 1.0 / THETA ** (jnp.arange(half, dtype=jnp.float32) / half)
            ang = pos[:, :, None].astype(jnp.float32) * inv
            cos = jnp.cos(ang)[:, None, :, :]
            sin = jnp.sin(ang)[:, None, :, :]
            x1, x2 = (x[..., :half], x[..., half:])
            return jnp.concatenate([x1 * cos - x2 * sin, x2 * cos + x1 * sin], axis=-1)
        Bx, Tx, _ = x.shape
        q = jnp.einsum('btd,od->bto', x, Wq).reshape(Bx, Tx, H, HD).transpose(0, 2, 1, 3)
        k = jnp.einsum('btd,od->bto', x, Wk).reshape(Bx, Tx, G, HD).transpose(0, 2, 1, 3)
        v = jnp.einsum('btd,od->bto', x, Wv).reshape(Bx, Tx, G, HD).transpose(0, 2, 1, 3)
        q = _rms(q, q_norm_scale)
        k = _rms(k, k_norm_scale)
        pos = kv_lens[:, None] + jnp.arange(Tx, dtype=jnp.int32)
        q = _rope(q, pos)
        k = _rope(k, pos)
        slot = pos // BLOCK
        off = pos % BLOCK
        blk = jnp.take_along_axis(block_tables, slot, axis=1)
        k_blocks = k_blocks.at[blk, :, off, :].set(k.transpose(0, 2, 1, 3))
        v_blocks = v_blocks.at[blk, :, off, :].set(v.transpose(0, 2, 1, 3))
        k_all = k_blocks[block_tables].transpose(0, 2, 1, 3, 4).reshape(Bx, G, -1, HD)
        v_all = v_blocks[block_tables].transpose(0, 2, 1, 3, 4).reshape(Bx, G, -1, HD)
        S = k_all.shape[2]
        qg = q.reshape(Bx, G, GSZ, Tx, HD)
        scores = jnp.einsum('bghtd,bgsd->bghts', qg, k_all) * SCALE
        kpos = jnp.arange(S, dtype=jnp.int32)
        allowed = (kpos[None, None, :] <= pos[:, :, None]) & (kpos[None, None, :] > pos[:, :, None] - WINDOW)
        scores = jnp.where(allowed[:, None, None, :, :], scores, -jnp.inf)
        p = jax.nn.softmax(scores, axis=-1)
        o = jnp.einsum('bghts,bgsd->bghtd', p, v_all).reshape(Bx, H, Tx, HD)
        o = o.transpose(0, 2, 1, 3).reshape(Bx, Tx, H * HD)
        return jnp.einsum('bto,do->btd', o, Wo)

    def _L1_ffn_ref(x, gate_w, W, atoms, expert_atom_weights, importance, mask_idx):
        import jax, jax.numpy as jnp
        import numpy as np
        TOP_K = 2
        B, S, H = x.shape
        xt = x.reshape(-1, H)
        logits = jnp.clip(xt @ gate_w.T, -50.0, 50.0)
        top_w, top_idx = jax.lax.top_k(logits, TOP_K)
        rw = jax.nn.softmax(top_w, axis=-1)
        deltas = jax.nn.softmax(expert_atom_weights, axis=-1) @ atoms
        weighted = deltas * jax.nn.sigmoid(importance)
        rows = mask_idx // H
        cols = mask_idx % H
        vals = jnp.einsum('tk,tks->ts', rw, weighted[top_idx])
        xg = xt[:, cols]
        contrib = jax.ops.segment_sum((xg * vals).T, rows, num_segments=H)
        out = xt @ W.T + contrib.T
        return out.reshape(B, S, H)
    x = x + _L0_ffn_ref(_L0_cond_ref(x, itok_B_0_7, L0_cond_weights), L0_ffn_gate_w, L0_ffn_up_w, L0_ffn_down_w, L0_ffn_gate_s, L0_ffn_up_s, L0_ffn_down_s)
    x = x + _L1_ffn_ref(_L1_cond_ref(x, L1_cond_Wq, L1_cond_Wk, L1_cond_Wv, L1_cond_Wo, L1_cond_q_norm_scale, L1_cond_k_norm_scale, L1_cond_k_blocks, L1_cond_v_blocks, itok_Bx257_0_4111, itok_B_37_3939), L1_ffn_gate_w, L1_ffn_W, L1_ffn_atoms, L1_ffn_expert_atom_weights, L1_ffn_importance, L1_ffn_mask_idx)
    return x

_drawn_inputs = setup_inputs


def setup_inputs(seed=0):
    import zlib

    import numpy as np

    out = dict(_drawn_inputs(seed))
    spreads = {}
    factors = {'L1_cond_Wq': 5.057,
     'L1_cond_Wk': 200.0,
     'L1_cond_Wv': 163.504,
     'L1_cond_q_norm_scale': 8.0,
     'L1_cond_k_norm_scale': 200.0,
     'L1_cond_k_blocks': 7.318,
     'L1_cond_v_blocks': 3.451,
     'L1_ffn_gate_w': 8.0,
     'L1_ffn_atoms': 8.0,
     'L1_ffn_expert_atom_weights': 8.0,
     'L1_ffn_importance': 36.295}
    for name, (base, spread) in spreads.items():
        noise = np.random.default_rng([zlib.crc32(name.encode()), seed]).standard_normal(out[name].shape)
        drawn = base * np.exp(spread * noise) if base else spread * noise
        out[name] = jnp.asarray(drawn.astype(out[name].dtype))
    for name, factor in factors.items():
        out[name] = (out[name] * factor).astype(out[name].dtype)
    return out
```

```python
from contextlib import ExitStack

import numpy as np

import concourse.bass as bass
from concourse import mybir

F32 = mybir.dt.float32
F32R = mybir.dt.float32r
I32 = mybir.dt.int32
ALU = mybir.AluOpType
ACT = mybir.ActivationFunctionType
AX = mybir.AxisListType.X

P = 128
B, C, T = 32, 64, 512
TOK = B * C
KT = T // P
NSUB = 8
INTER = 1408
IT = INTER // P
GROUPS = 4
GT = TOK // GROUPS
TPG = GT // P
SPG = B // GROUPS
PAIRS = B // 2
H, G, HD = 8, 4, 64
HALF = HD // 2
NQK = H + G
BLOCK, WINDOW, NBLK = 16, 256, 257
POOL_ROWS = 16 * NBLK * BLOCK
KEYS = WINDOW + C
KCH = (128, 128, 64)
NCH = len(KCH)
SLOTS = 21
SEG = 5
NSEG = B * SEG
SCALE = 256.0 ** -0.5
EPS = 1e-6
E, A, NS = 8, 64, 4096
SCH = NS // P
TBL = T * T
SKIP = float(1 << 20)
MASKED = -1.0e30
TWO_PI = 2 * np.pi
C1 = 6.28125
C2 = float(np.floor((TWO_PI - C1) * 2**21) / 2**21)
C3 = float(np.float32(TWO_PI - C1 - C2))
MAGIC = 1.5 * 2.0**23
PI_IN = 3.1415925


class Count:

    def __init__(self, start=0):
        self.n = start

    def next(self):
        self.n += 1
        return self.n


def bass_adaln_ffn_kernel(nc, x, kv_lens, subjects, tables, cond_w, gate_t, up_t, down_t, gate_s, up_s, down_s,
                          wqkv_t, wo_t, q_norm, k_norm, kv_cache, inv_freq, route_t, w_t, atoms, expert_atom,
                          importance, mask_col, mask_row, out):
    q_dram = nc.dram_tensor("q_dram", (TOK, T), F32, kind="Internal").ap()
    kv_dram = nc.dram_tensor("kv_dram", (TOK, T), F32, kind="Internal").ap()
    x1_dram = nc.dram_tensor("x1_dram", (TOK, T), F32, kind="Internal").ap()
    table_dram = nc.dram_tensor("table_dram", (TBL + P, E), F32, kind="Internal").ap()

    sbuf_map = [(nc.sbuf_base + 31) // 32 * 32]

    def place(name, shape, dt=F32):
        off = sbuf_map[0]
        sbuf_map[0] = off + (int(np.prod(shape[1:])) * 4 + 31) // 32 * 32
        return nc.alloc_sbuf_tensor_at(name, list(shape), dt, offset=off)

    with ExitStack() as ctx:
        def sem(name):
            return ctx.enter_context(nc.semaphore(name))

        def psum(name, shape):
            return ctx.enter_context(nc.psum_tensor(name, shape, F32))

        ident = place("ident", (P, P))
        own_cache = place("own_cache", (P, B * NCH), I32)
        own_new = place("own_new", (P, B * NCH), I32)
        thr = place("thr", (P, B))
        band = place("band", (P, KEYS))
        jrow = place("jrow", (P, KEYS))
        before = place("before", (P, E, E))
        route_w = place("route_w", (P, KT, E))
        keep_at = sbuf_map[0]
        wqkv = place("wqkv", (P, KT, 2 * T))
        cos = place("cos", (P, PAIRS, HALF))
        sin = place("sin", (P, PAIRS, HALF))
        nscale = place("nscale", (P, NQK, HD))
        dscale = place("dscale", (P, T))
        gs = place("gs", (P, IT))
        us = place("us", (P, IT))
        key_addr = place("key_addr", (P, B * NCH))
        seg_lo = place("seg_lo", (P, B, SEG))
        seg_hi = place("seg_hi", (P, B, SEG))
        seg_shift = place("seg_shift", (P, B, SEG))
        tot = place("tot", (P, SCH, E))
        table_idx = place("table_idx", (P, SCH), I32)
        subj = place("subj", (1, B), I32)
        wT_sb = place("wT_sb", (P, KT, T))
        zero8 = place("zero8", (P, E))
        wexp = place("wexp", (P, T // 2, E))
        weights_at = sbuf_map[0]
        gate_w = place("gate_w", (P, KT, INTER))
        up_w = place("up_w", (P, KT, INTER))
        down_w = place("down_w", (P, IT, T))
        work_at = sbuf_map[0]

        mrow_i = place("mrow_i", (P, SCH, P), I32)
        mrow = place("mrow", (P, SCH, P))
        mcol_i = place("mcol_i", (P, SCH), I32)
        mcol = place("mcol", (P, SCH))
        mhi_i = place("mhi_i", (P, SCH), I32)
        mlo_i = place("mlo_i", (P, SCH), I32)
        mhi = place("mhi", (P, SCH))
        mlo = place("mlo", (P, SCH))
        earlier = place("earlier", (P, SCH))
        lowtri = place("lowtri", (P, P))
        dump_i = place("dump_i", (P, 1), I32)
        dump = place("dump", (P, 1))
        wt = place("wt", (P, SCH, E))
        sig = place("sig", (P, SCH, E))
        eaw = place("eaw", (E, A))
        eaw_s = place("eaw_s", (E, 4))
        eawT = place("eawT", (A, E))
        atoms_sb = place("atoms_sb", (A, SCH, P))
        oh = place("oh", (P, B, SLOTS))
        tb_f = place("tb_f", (P, B, SLOTS))
        tb_i = place("tb_i", (P, B, SLOTS), I32)
        kv_i = place("kv_i", (P, B), I32)
        kv_f = place("kv_f", (P, B))
        kvq_i = place("kvq_i", (P, B), I32)
        kvr_i = place("kvr_i", (P, B), I32)
        kvq = place("kvq", (P, B))
        kvr = place("kvr", (P, B))
        slot0 = place("slot0", (P, B))
        jcol_i = place("jcol_i", (P, NCH), I32)
        jcol = place("jcol", (P, NCH))
        posk_i = place("posk_i", (P, B, NCH), I32)
        slot_i = place("slot_i", (P, B, NCH), I32)
        off_i = place("off_i", (P, B, NCH), I32)
        rel = place("rel", (P, B, NCH))
        off_f = place("off_f", (P, B, NCH))
        kblk = place("kblk", (P, B, NCH))
        seg_rel = place("seg_rel", (P, B))
        seg_blk = place("seg_blk", (P, B, SEG))
        seg_t = place("seg_t", (P, B, SEG))
        bbase_i = place("bbase_i", (P, B), I32)
        bbase = place("bbase", (P, B))
        io21_i = place("io21_i", (P, SLOTS), I32)
        io21 = place("io21", (P, SLOTS))
        ang = place("ang", (P, PAIRS, HALF))
        turns = place("turns", (P, PAIRS, HALF))
        kvt_i = place("kvt_i", (P, PAIRS), I32)
        kvt = place("kvt", (P, PAIRS))
        tpos_i = place("tpos_i", (P, 1), I32)
        tpos = place("tpos", (P, 1))
        inv = place("inv", (P, HALF))
        qn = place("qn", (P, 2, HD))
        jrow_i = place("jrow_i", (P, KEYS), I32)
        dist_i = place("dist_i", (P, KEYS), I32)
        dist = place("dist", (P, KEYS))
        prologue_end = sbuf_map[0]

        sbuf_map[0] = work_at
        xc = place("xc", (P, TPG, T))
        xr = place("xr", (P, TPG, T))
        cw = place("cw", (P, TPG, P))
        hT = place("hT", (P, KT, GT))
        hdn = place("hdn", (P, IT, GT))
        silu = place("silu", (P, 2, GT))
        x1 = place("x1", (P, 2, T))
        x1T = place("x1T", (P, KT, GT))
        raw = place("raw", (P, 2, NQK * HD))
        sq = place("sq", (P, NQK * HD))
        q_out = place("q_out", (P, 2, T))
        kv_out = place("kv_out", (P, 2, T))
        rot_a = place("rot_a", (P, NQK, HALF))
        rot_b = place("rot_b", (P, NQK, HALF))
        ssum = place("ssum", (P, 3, NQK))
        KCOLS = 4
        own_u = place("own_u", (P, KCOLS, NSEG))
        own_m = place("own_m", (P, KCOLS, NSEG))
        owner = place("owner", (P, 2, KCOLS))
        slot_val = place("slot_val", (P, E))
        slot_idx = place("slot_idx", (P, 1), I32)
        layer0_end = sbuf_map[0]

        sbuf_map[0] = keep_at
        experts_hi = place("experts_hi", (P, KT, E, T))
        experts_lo = place("experts_lo", (P, KT, E, T))
        PIECE = T // 4
        PIECES = T // PIECE
        stage = place("stage", (P, 2, PIECE, E))
        wo = place("wo", (P, KT, T))
        kv_t = [[place(f"kv_t{u}{b}", (P, NCH, T)) for b in range(2)] for u in range(2)]
        idx_c = [place(f"idx_c{u}", (P, 2 * NCH), I32) for u in range(2)]
        idx_n = [place(f"idx_n{u}", (P, 2 * NCH), I32) for u in range(2)]
        q_t = place("q_t", (P, 2, T))
        acc = place("acc", (P, 2, T))
        qT = place("qT", (P, 2, 2, 2, C))
        kT = place("kT", (P, 2, 2, KEYS))
        mask = place("mask", (P, 2, KEYS))
        sm = place("sm", (P, 2, KEYS))
        prob = place("prob", (P, 2, KEYS))
        pT = place("pT", (P, 2, NCH, P))
        mx = place("mx", (P, 8))
        nmx = place("nmx", (P, 8))
        rsum = place("rsum", (P, 8))
        rinv = place("rinv", (P, 8))
        o_sb = place("o_sb", (P, 2, G * HD))
        oT = place("oT", (P, 2, 2, 2, C))
        yT_hi = place("yT_hi", (P, KT, P))
        yT_lo = place("yT_lo", (P, KT, P))
        lg = place("lg", (P, E))
        gtr = place("gtr", (P, E, E))
        eqr = place("eqr", (P, E, E))
        rt = place("rt", (P, 8, E))
        layer1_end = sbuf_map[0]
        assert max(prologue_end, layer0_end, layer1_end) <= nc.sbuf_usable_end, (
            prologue_end, layer0_end, layer1_end, nc.sbuf_usable_end)

        bank = [psum(f"bank{i}", [P, 2, T]) for i in range(4)]

        def bk(n):
            return bank[n // 2][:, n % 2, :]

        weights_loaded = sem("weights_loaded")

        kv_loaded = sem("kv_loaded")
        consts_loaded = sem("consts_loaded")
        tables_loaded = sem("tables_loaded")
        iotas = sem("iotas")
        sparse_loaded = sem("sparse_loaded")
        p_dve = sem("p_dve")
        eaw_max = sem("eaw_max")
        eaw_exp = sem("eaw_exp")
        eaw_norm = sem("eaw_norm")
        eaw_T = sem("eaw_T")
        eaw_Tsb = sem("eaw_Tsb")
        delta_ps = sem("delta_ps")
        sig_ready = sem("sig_ready")
        wt_ready = sem("wt_ready")
        eq_ready = sem("eq_ready")
        tot_ps = sem("tot_ps")
        sin_arg = sem("sin_arg")
        sin_done = sem("sin_done")
        ident_ready = sem("ident_ready")

        with nc.Block() as block:
            @block.sync
            def _(sp):
                sp.dma_start(kv_i[:, :], kv_lens.rearrange("(a n) -> a n", a=1).to_broadcast([P, B])).then_inc(kv_loaded, 16)
                by_half = kv_lens.rearrange("(i h) -> h i", h=2)
                for h in range(2):
                    with nc.allow_non_contiguous_dma(reason="32 lengths"):
                        sp.dma_start(kvt_i[h * C:(h + 1) * C, :], by_half[h:h + 1, :].to_broadcast([C, PAIRS])).then_inc(consts_loaded, 16)
                sp.dma_start(inv[:, :], inv_freq.to_broadcast([P, HALF])).then_inc(consts_loaded, 16)
                sp.dma_start(qn[:, 0, :], q_norm.to_broadcast([P, HD])).then_inc(consts_loaded, 16)
                sp.dma_start(qn[:, 1, :], k_norm.to_broadcast([P, HD])).then_inc(consts_loaded, 16)
                sp.dma_start(mcol_i[:, :], mask_col).then_inc(sparse_loaded, 16)
                sp.dma_start(mrow_i[:, :, :], mask_row.rearrange("(a c) p -> a c p", a=1).to_broadcast([P, SCH, P])).then_inc(sparse_loaded, 16)
                sp.dma_start(eaw[:, :], expert_atom).then_inc(sparse_loaded, 16)
                sp.dma_start(atoms_sb[:, :, :], atoms).then_inc(sparse_loaded, 16)
                sp.dma_start(sig[:, :, :], importance).then_inc(sparse_loaded, 16)
                sp.wait_ge(kv_loaded, 16)
                with sp.Fori(0, B) as b:
                    q = sp.snap(sp.value_load(kv_i[0:1, bass.ds(b, 1)], min_val=0, max_val=(NBLK - 1) * BLOCK - C - 1) >> 4)
                    first = sp.snap((q >= 16) * (q - 16)).with_bounds(min_val=0, max_val=NBLK - SLOTS)
                    sp.dma_start(tb_i[:, bass.ds(b, 1), :],
                                 tables[bass.ds(b * NBLK + first, SLOTS)].rearrange("(a n) -> a n", a=1).to_broadcast([P, SLOTS])).then_inc(tables_loaded, 16)

            @block.gpsimd
            def _(pool):
                pool.memset(ident[:, :], 0.0).then_inc(ident_ready, 1)
                pool.memset(lowtri[:, :], 1.0).then_inc(ident_ready, 1)
                pool.memset(zero8[:, :], 0.0)
                pool.memset(before[:, :, :], 1.0).then_inc(ident_ready, 1)
                pool.iota(jcol_i[:, :], [[P, NCH]], base=-WINDOW, channel_multiplier=1).then_inc(iotas, 1)
                pool.iota(io21_i[:, :], [[1, SLOTS]], base=0, channel_multiplier=0).then_inc(iotas, 1)
                pool.iota(bbase_i[:, :], [[C, B]], base=1, channel_multiplier=0).then_inc(iotas, 1)
                pool.iota(jrow_i[:, :], [[1, KEYS]], base=0, channel_multiplier=0).then_inc(iotas, 1)
                pool.iota(dump_i[:, :], [[0, 1]], base=TBL, channel_multiplier=1).then_inc(iotas, 1)
                for h in range(2):
                    pool.wait_ge(iotas, 5 + 2 * h)
                    pool.iota(tpos_i[h * C:(h + 1) * C, :], [[0, 1]], base=0, channel_multiplier=1).then_inc(iotas, 1)
                    pool.iota(dist_i[h * C:(h + 1) * C, :], [[1, KEYS]], base=0, channel_multiplier=-1).then_inc(iotas, 1)
                pool.wait_ge(ident_ready, 3)
                pool.wait_ge(iotas, 9)
                pool.affine_select(out=ident[:, :], in_=ident[:, :], compare_op=ALU.not_equal, fill=1.0,
                                   base=0, pattern=[[-1, P]], channel_multiplier=1).then_inc(ident_ready, 1)
                pool.affine_select(out=lowtri[:, :], in_=lowtri[:, :], compare_op=ALU.is_gt, fill=0.0,
                                   base=0, pattern=[[-1, P]], channel_multiplier=1).then_inc(ident_ready, 1)
                pool.affine_select(out=before[:, :, :], in_=before[:, :, :], compare_op=ALU.is_gt, fill=0.0,
                                   base=0, pattern=[[1, E], [-1, E]], channel_multiplier=0).then_inc(ident_ready, 1)

            @block.scalar
            def _(act):
                act.dma_start(gate_w[:, :, :], gate_t.rearrange("(k p) n -> p k n", p=P)).then_inc(weights_loaded, 16)
                act.dma_start(up_w[:, :, :], up_t.rearrange("(k p) n -> p k n", p=P)).then_inc(weights_loaded, 16)
                act.dma_start(down_w[:, :, :], down_t.rearrange("(k p) n -> p k n", p=P)).then_inc(weights_loaded, 16)
                act.dma_start(wqkv[:, :, :], wqkv_t.rearrange("(k p) n -> p k n", p=P)).then_inc(weights_loaded, 16)
                act.dma_start(dscale[:, :], down_s.to_broadcast([P, T])).then_inc(weights_loaded, 16)
                act.dma_start(gs[:, :], gate_s).then_inc(weights_loaded, 16)
                act.dma_start(us[:, :], up_s).then_inc(weights_loaded, 16)
                act.dma_start(route_w[:, :, :], route_t.rearrange("(k p) n -> p k n", p=P)).then_inc(weights_loaded, 16)
                act.dma_start(subj[:, :], subjects).then_inc(weights_loaded, 16)
                act.dma_start(wT_sb[:, :, :], w_t.rearrange("(c p) r -> p c r", p=P)).then_inc(weights_loaded, 16)
                act.wait_ge(sparse_loaded, 16 * 5)
                act.activation(sig[:, :, :], sig[:, :, :], ACT.Sigmoid).then_inc(sig_ready, 1)
                act.wait_ge(eaw_max, 1)
                act.activation(eaw[:, :], eaw[:, :], ACT.Exp, bias=eaw_s[:, 1:2], accum_out=eaw_s[:, 2:3]).then_inc(eaw_exp, 1)
                act.wait_ge(sin_arg, 1)
                act.activation(sin[:, :, :], ang[:, :, :], ACT.Sin).then_inc(sin_done, 1)
                act.wait_ge(sin_arg, 2)
                act.activation(cos[:, :, :], turns[:, :, :], ACT.Sin).then_inc(sin_done, 1)

            @block.tensor
            def _(pe):
                pe.wait_ge(ident_ready, 6)
                pe.wait_ge(eaw_norm, 1)
                pe.transpose(bk(0)[0:A, 0:E], eaw[:, :], ident[0:E, 0:E]).then_inc(eaw_T, 1)
                pe.wait_ge(eaw_Tsb, 1)
                for s in range(SCH):
                    mm = pe.matmul(bk(1)[:, s * E:(s + 1) * E], atoms_sb[:, s, :], eawT[:, :], start=True, stop=True)
                mm.then_inc(delta_ps, 1)
                pe.wait_ge(wt_ready, 1)
                pe.wait_ge(eq_ready, 1)
                for s in range(SCH):
                    mm = pe.matmul(bk(2)[:, s * E:(s + 1) * E], mrow[:, s, :], wt[:, s, :], start=True, stop=True)
                mm.then_inc(tot_ps, 1)

            @block.vector
            def _(dve):
                n = Count()
                dve.wait_ge(kv_loaded, 16)
                dve.wait_ge(iotas, 9)
                dve.tensor_copy(kv_f[:, :], kv_i[:, :]).then_inc(p_dve, 1)
                dve.tensor_scalar(kvq_i[:, :], kv_i[:, :], 4, None, ALU.arith_shift_right).then_inc(p_dve, 1)
                dve.tensor_scalar(kvr_i[:, :], kv_i[:, :], 15, None, ALU.bitwise_and).then_inc(p_dve, 1)
                dve.tensor_copy(jcol[:, :], jcol_i[:, :]).then_inc(p_dve, 1)
                dve.tensor_copy(io21[:, :], io21_i[:, :]).then_inc(p_dve, 1)
                dve.tensor_copy(bbase[:, :], bbase_i[:, :]).then_inc(p_dve, 1)
                dve.tensor_copy(jrow[:, :], jrow_i[:, :]).then_inc(p_dve, 1)
                dve.tensor_copy(dump[:, :], dump_i[:, :]).then_inc(p_dve, 1)
                dve.tensor_copy(tpos[:, :], tpos_i[:, :]).then_inc(p_dve, 1)
                dve.tensor_copy(dist[:, :], dist_i[:, :]).then_inc(p_dve, 1)
                n.n = 10
                dve.wait_ge(p_dve, 10)
                dve.tensor_copy(kvq[:, :], kvq_i[:, :]).then_inc(p_dve, 1)
                dve.tensor_copy(kvr[:, :], kvr_i[:, :]).then_inc(p_dve, 1)
                dve.tensor_scalar(thr[:, :], kv_f[:, :], -1.0, float(WINDOW), ALU.mult, ALU.add).then_inc(p_dve, 1)
                dve.tensor_scalar(band[:, :], dist[:, :], 0.0, None, ALU.is_gt).then_inc(p_dve, 1)
                n.n = 14
                dve.wait_ge(p_dve, 14)
                dve.scalar_tensor_tensor(out=band[:, :], in0=dist[:, :], scalar=float(WINDOW), in1=band[:, :],
                                         op0=ALU.is_le, op1=ALU.mult).then_inc(p_dve, 1)
                dve.wait_ge(p_dve, n.next())
                dve.tensor_scalar(band[:, :], band[:, :], -MASKED, MASKED, ALU.mult, ALU.add).then_inc(p_dve, 1)
                dve.wait_ge(p_dve, n.next())
                dve.wait_ge(sparse_loaded, 16 * 5)
                dve.tensor_reduce(eaw_s[:, 0:1], eaw[:, :], AX, ALU.max).then_inc(p_dve, 1)
                dve.wait_ge(p_dve, n.next())
                dve.tensor_scalar(eaw_s[:, 1:2], eaw_s[:, 0:1], -1.0, None, ALU.mult).then_inc(eaw_max, 1)
                dve.tensor_copy(mcol[:, :], mcol_i[:, :]).then_inc(p_dve, 1)
                dve.wait_ge(p_dve, n.next())
                dve.tensor_copy(mrow[:, :, :], mrow_i[:, :, :]).then_inc(p_dve, 1)
                dve.wait_ge(p_dve, n.next())
                dve.tensor_tensor(mrow[:, :, :], mrow[:, :, :], mcol[:, :].unsqueeze(2).to_broadcast([P, SCH, P]),
                                  ALU.is_equal).then_inc(eq_ready, 1)
                dve.wait_ge(eaw_exp, 1)
                dve.reciprocal(eaw_s[:, 3:4], eaw_s[:, 2:3]).then_inc(p_dve, 1)
                dve.wait_ge(p_dve, n.next())
                dve.tensor_scalar(eaw[:, :], eaw[:, :], eaw_s[:, 3:4], None, ALU.mult).then_inc(eaw_norm, 1)
                dve.wait_ge(eq_ready, 1)
                low = mrow_i[:, :, :].bitcast(F32)
                dve.wait_ge(ident_ready, 6)
                dve.tensor_tensor(low, mrow[:, :, :], lowtri[:, :].unsqueeze(1).to_broadcast([P, SCH, P]), ALU.mult).then_inc(p_dve, 1)
                dve.wait_ge(p_dve, n.next())
                dve.wait_ge(eaw_T, 1)
                dve.tensor_copy(eawT[:, :], bk(0)[0:A, 0:E]).then_inc(eaw_Tsb, 1)
                dve.tensor_reduce(earlier[:, :], low, AX, ALU.add).then_inc(p_dve, 1)
                dve.wait_ge(p_dve, n.next())
                dve.tensor_scalar(mhi_i[:, :], mcol_i[:, :], 9, None, ALU.arith_shift_right).then_inc(p_dve, 1)
                dve.tensor_scalar(mlo_i[:, :], mcol_i[:, :], T - 1, None, ALU.bitwise_and).then_inc(p_dve, 1)
                dve.tensor_scalar(earlier[:, :], earlier[:, :], 1.0, None, ALU.min).then_inc(p_dve, 1)
                n.n += 3
                dve.wait_ge(p_dve, n.n)
                dve.tensor_copy(mhi[:, :], mhi_i[:, :]).then_inc(p_dve, 1)
                dve.tensor_copy(mlo[:, :], mlo_i[:, :]).then_inc(p_dve, 1)
                n.n += 2
                dve.wait_ge(p_dve, n.n)
                dve.scalar_tensor_tensor(out=mlo[:, :], in0=mlo[:, :], scalar=float(T), in1=mhi[:, :], op0=ALU.mult, op1=ALU.add).then_inc(p_dve, 1)
                dve.wait_ge(p_dve, n.next())
                dve.tensor_scalar(mhi[:, :], mlo[:, :], -1.0, dump[:, :], ALU.mult, ALU.add).then_inc(p_dve, 1)
                dve.wait_ge(p_dve, n.next())
                dve.tensor_tensor(mhi[:, :], mhi[:, :], earlier[:, :], ALU.mult).then_inc(p_dve, 1)
                dve.wait_ge(p_dve, n.next())
                dve.tensor_tensor(table_idx[:, :], mhi[:, :], mlo[:, :], ALU.add).then_inc(p_dve, 1)
                dve.wait_ge(p_dve, n.next())
                dve.wait_ge(delta_ps, 1)
                dve.wait_ge(sig_ready, 1)
                dve.tensor_tensor(wt[:, :, :], bk(1)[:, 0:SCH * E].rearrange("p (s e) -> p s e", e=E), sig[:, :, :], ALU.mult).then_inc(wt_ready, 1)
                dve.wait_ge(consts_loaded, 16 * 5)
                dve.tensor_copy(kvt[:, :], kvt_i[:, :]).then_inc(p_dve, 1)
                dve.wait_ge(p_dve, n.next())
                dve.tensor_scalar(kvt[:, :], kvt[:, :], tpos[:, :], None, ALU.add).then_inc(p_dve, 1)
                dve.wait_ge(p_dve, n.next())
                dve.tensor_tensor(ang[:, :, :], kvt[:, :].unsqueeze(2).to_broadcast([P, PAIRS, HALF]),
                                  inv[:, :].unsqueeze(1).to_broadcast([P, PAIRS, HALF]), ALU.mult).then_inc(p_dve, 1)
                dve.wait_ge(p_dve, n.next())
                dve.tensor_scalar(turns[:, :, :], ang[:, :, :], float(1 / TWO_PI), MAGIC, ALU.mult, ALU.add).then_inc(p_dve, 1)
                dve.wait_ge(p_dve, n.next())
                dve.tensor_scalar(turns[:, :, :], turns[:, :, :], MAGIC, None, ALU.subtract).then_inc(p_dve, 1)
                dve.wait_ge(p_dve, n.next())
                for part in (C1, C2, C3):
                    dve.scalar_tensor_tensor(out=ang[:, :, :], in0=turns[:, :, :], scalar=-part, in1=ang[:, :, :],
                                             op0=ALU.mult, op1=ALU.add).then_inc(p_dve, 1)
                    dve.wait_ge(p_dve, n.next())
                dve.tensor_scalar(ang[:, :, :], ang[:, :, :], PI_IN, -PI_IN, ALU.min, ALU.max).then_inc(sin_arg, 1)
                dve.wait_ge(sin_arg, 1)
                dve.scalar_tensor_tensor(out=turns[:, :, :], in0=ang[:, :, :], scalar=-1.0, in1=ang[:, :, :],
                                         op0=ALU.mult, op1=ALU.max).then_inc(p_dve, 1)
                dve.wait_ge(p_dve, n.next())
                dve.tensor_scalar(turns[:, :, :], turns[:, :, :], -1.0, float(np.pi / 2), ALU.mult, ALU.add).then_inc(sin_arg, 1)
                dve.tensor_scalar(nscale[:, 0:H, :], qn[:, 0:1, :].to_broadcast([P, H, HD]), 1.0, None, ALU.add).then_inc(p_dve, 1)
                dve.tensor_scalar(nscale[:, H:NQK, :], qn[:, 1:2, :].to_broadcast([P, G, HD]), 1.0, None, ALU.add).then_inc(p_dve, 1)
                n.n += 2
                dve.tensor_scalar(slot0[:, :], kvq[:, :], float(WINDOW // BLOCK), 0.0, ALU.subtract, ALU.max).then_inc(p_dve, 1)
                dve.tensor_tensor(posk_i[:, :, :], kv_f[:, :].unsqueeze(2).to_broadcast([P, B, NCH]),
                                  jcol[:, :].unsqueeze(1).to_broadcast([P, B, NCH]), ALU.add).then_inc(p_dve, 1)
                n.n += 2
                dve.wait_ge(p_dve, n.n)
                dve.tensor_scalar(posk_i[:, :, :], posk_i[:, :, :], 0.0, None, ALU.max).then_inc(p_dve, 1)
                dve.wait_ge(p_dve, n.next())
                dve.tensor_scalar(slot_i[:, :, :], posk_i[:, :, :], 4, None, ALU.arith_shift_right).then_inc(p_dve, 1)
                dve.tensor_scalar(off_i[:, :, :], posk_i[:, :, :], 15, None, ALU.bitwise_and).then_inc(p_dve, 1)
                n.n += 2
                dve.wait_ge(p_dve, n.n)
                dve.tensor_copy(rel[:, :, :], slot_i[:, :, :]).then_inc(p_dve, 1)
                dve.tensor_copy(off_f[:, :, :], off_i[:, :, :]).then_inc(p_dve, 1)
                n.n += 2
                dve.wait_ge(p_dve, n.n)
                dve.tensor_tensor(rel[:, :, :], rel[:, :, :], slot0[:, :].unsqueeze(2).to_broadcast([P, B, NCH]), ALU.subtract).then_inc(p_dve, 1)
                dve.wait_ge(tables_loaded, 16 * B)
                dve.tensor_copy(tb_f[:, :, :], tb_i[:, :, :]).then_inc(p_dve, 1)
                n.n += 2
                dve.wait_ge(p_dve, n.n)

                def look_up(to, which):
                    dve.tensor_tensor(oh[:, :, :], which.unsqueeze(2).to_broadcast([P, B, SLOTS]),
                                      io21[:, :].unsqueeze(1).to_broadcast([P, B, SLOTS]), ALU.is_equal).then_inc(p_dve, 1)
                    dve.wait_ge(p_dve, n.next())
                    dve.tensor_tensor(oh[:, :, :], oh[:, :, :], tb_f[:, :, :], ALU.mult).then_inc(p_dve, 1)
                    dve.wait_ge(p_dve, n.next())
                    dve.tensor_reduce(to, oh[:, :, :], AX, ALU.add).then_inc(p_dve, 1)
                    dve.wait_ge(p_dve, n.next())

                for c in range(NCH):
                    look_up(kblk[:, :, c], rel[:, :, c])
                dve.scalar_tensor_tensor(out=key_addr[:, :].rearrange("p (b c) -> p b c", c=NCH), in0=kblk[:, :, :], scalar=float(BLOCK),
                                         in1=off_f[:, :, :], op0=ALU.mult, op1=ALU.add).then_inc(p_dve, 1)
                n.n += 1
                for i in range(SEG):
                    dve.scalar_tensor_tensor(out=seg_rel[:, :], in0=kvq[:, :], scalar=float(i), in1=slot0[:, :],
                                             op0=ALU.add, op1=ALU.subtract).then_inc(p_dve, 1)
                    dve.tensor_scalar(seg_t[:, :, i], kvr[:, :], -1.0, float(BLOCK * i), ALU.mult, ALU.add).then_inc(p_dve, 1)
                    dve.tensor_scalar(seg_hi[:, :, i], kvr[:, :], -1.0, float(BLOCK * (i + 1)), ALU.mult, ALU.add).then_inc(p_dve, 1)
                    n.n += 3
                    dve.wait_ge(p_dve, n.n)
                    look_up(seg_blk[:, :, i], seg_rel[:, :])
                dve.tensor_scalar(seg_t[:, :, :], seg_t[:, :, :], 0.0, None, ALU.max).then_inc(p_dve, 1)
                dve.tensor_scalar(seg_hi[:, :, :], seg_hi[:, :, :], float(C), None, ALU.min).then_inc(p_dve, 1)
                n.n += 2
                dve.wait_ge(p_dve, n.n)
                for seg, src in ((seg_lo, seg_t), (seg_hi, seg_hi)):
                    dve.tensor_tensor(seg[:, :, :], src[:, :, :], bbase[:, :].unsqueeze(2).to_broadcast([P, B, SEG]), ALU.add).then_inc(p_dve, 1)
                dve.tensor_scalar(seg_blk[:, :, :], seg_blk[:, :, :], float(BLOCK), None, ALU.mult).then_inc(p_dve, 1)
                n.n += 3
                dve.wait_ge(p_dve, n.n)
                dve.tensor_tensor(seg_blk[:, :, 0], seg_blk[:, :, 0], kvr[:, :], ALU.add).then_inc(p_dve, 1)
                dve.wait_ge(p_dve, n.next())
                dve.tensor_tensor(seg_shift[:, :, :], seg_lo[:, :, :], seg_blk[:, :, :], ALU.subtract).then_inc(p_dve, 1)
                dve.wait_ge(p_dve, n.next())
                dve.wait_ge(tot_ps, 1)
                dve.tensor_copy(tot[:, :, :], bk(2)[:, 0:SCH * E].rearrange("p (s e) -> p s e", e=E)).then_inc(p_dve, 1)
                dve.wait_ge(p_dve, n.next())

        WEIGHTS = 16 * 10
        cw_zero = sem("cw_zero")
        xc_loaded = sem("xc_loaded")
        xr_loaded = sem("xr_loaded")
        cw_loaded = sem("cw_loaded")
        proj_ps = sem("proj_ps")
        h_ready = sem("h_ready")
        gu_ps = sem("gu_ps")
        silu_ready = sem("silu_ready")
        hdn_ready = sem("hdn_ready")
        down_ps = sem("down_ps")
        res_ready = sem("res_ready")
        x1T_ps = sem("x1T_ps")
        x1T_ready = sem("x1T_ready")
        x1_stored = [sem(f"x1_stored{k}") for k in range(2)]
        qkv_ps = sem("qkv_ps")
        qkv_sq = sem("qkv_sq")
        qkv_copied = sem("qkv_copied")
        std_arg = sem("std_arg")
        std_ready = sem("std_ready")
        qk_ready = sem("qk_ready")
        q_stored = [sem(f"q_stored{k}") for k in range(2)]
        kv_stored = [sem(f"kv_stored{k}") for k in range(2)]
        d0 = sem("d0")
        DSTEPS = 112
        wexp_full = sem("wexp_full")
        table_init = sem("table_init")
        TABLE_INIT = 16 * (2 * KT + 1)
        slot_ready = sem("slot_ready")
        entry_added = sem("entry_added")
        slot_taken = sem("slot_taken")

        with nc.Block() as block:
            @block.sync
            def _(sp):
                sp.wait_ge(weights_loaded, WEIGHTS)
                with sp.Fori(0, GROUPS) as g:
                    sp.wait_ge(proj_ps, g * KT + 1)
                    sp.dma_start(xc[:, :, :], x[bass.ds(g * GT, GT), :].rearrange("(k p) t -> p k t", p=P)).then_inc(xc_loaded, 16)
                    for s in range(SPG):
                        r = sp.value_load(subj[0:1, bass.ds(g * SPG + s, 1)], min_val=0, max_val=NSUB - 1)
                        half = s % 2 * C
                        sp.dma_start(cw[half:half + C, s // 2, half:half + C], cond_w[bass.ds(r, 1), :, :].rearrange("a c d -> (a c) d")).then_inc(cw_loaded, 16)
                    sp.wait_ge(res_ready, g * TPG + 1)
                    sp.dma_start(xr[:, :, :], x[bass.ds(g * GT, GT), :].rearrange("(k p) t -> p k t", p=P)).then_inc(xr_loaded, 16)

            @block.tensor
            def _(pe):
                pe.wait_ge(cw_zero, 1)
                for s in (proj_ps, gu_ps, down_ps, qkv_ps):
                    pe.sem_inc(s, 1)
                pe.wait_ge(weights_loaded, WEIGHTS)
                with pe.Fori(0, GROUPS) as g:
                    pe.wait_ge(xc_loaded, g * 16 + 16)
                    pe.wait_ge(cw_loaded, g * (16 * SPG) + 16 * SPG)
                    for k in range(KT):
                        if k < 2:
                            pe.wait_ge(res_ready, g * TPG + 1)
                        else:
                            pe.wait_ge(h_ready, g * KT + k - 1)
                        for j in range(TPG):
                            mm = pe.matmul(bk(4 + k % 2)[:, j * P:(j + 1) * P], xc[:, j, k * P:(k + 1) * P], cw[:, j, :],
                                           start=True, stop=True)
                        mm.then_inc(proj_ps, 1)
                    for i in range(IT):
                        if i < 2:
                            pe.wait_ge(qkv_copied, g * TPG + 1)
                        else:
                            pe.wait_ge(hdn_ready, g * IT + i + 1)
                        if i == 0:
                            pe.wait_ge(h_ready, g * KT + KT)
                        for w, half in ((gate_w, 0), (up_w, 1)):
                            for k in range(KT):
                                mm = pe.matmul(bk(2 * (i % 2) + half), w[:, k, i * P:(i + 1) * P], hT[:, k, :],
                                               start=(k == 0), stop=(k == KT - 1))
                        mm.then_inc(gu_ps, 1)

                    def down(j):
                        if j >= 2:
                            pe.wait_ge(res_ready, g * TPG + j)
                        for i in range(IT):
                            if j == 0:
                                pe.wait_ge(hdn_ready, g * IT + i + 3)
                            mm = pe.matmul(bk(4 + j % 2), hdn[:, i, j * P:(j + 1) * P], down_w[:, i, :],
                                           start=(i == 0), stop=(i == IT - 1))
                        mm.then_inc(down_ps, 1)

                    def turn(j):
                        pe.wait_ge(res_ready, g * TPG + j + 2)
                        pe.wait_ge(x1T_ready, g * TPG + j + 1)
                        for k in range(KT):
                            mm = pe.transpose(bk(6)[:, k * P:(k + 1) * P], x1[:, j % 2, k * P:(k + 1) * P], ident[:, :])
                        mm.then_inc(x1T_ps, 1)

                    def qkv(j):
                        pe.wait_ge(x1T_ready, g * TPG + j + 2)
                        if j >= 2:
                            pe.wait_ge(qkv_copied, g * TPG + j)
                        for half in range(2):
                            for k in range(KT):
                                mm = pe.matmul(bk(2 * (j % 2) + half), x1T[:, k, j * P:(j + 1) * P], wqkv[:, k, half * T:(half + 1) * T],
                                               start=(k == 0), stop=(k == KT - 1))
                        mm.then_inc(qkv_ps, 1)

                    down(0)
                    down(1)
                    turn(0)
                    down(2)
                    turn(1)
                    qkv(0)
                    down(3)
                    turn(2)
                    qkv(1)
                    turn(3)
                    qkv(2)
                    qkv(3)

            @block.scalar
            def _(act):
                act.sem_inc(x1T_ready, 1)
                act.sem_inc(qkv_copied, 1)
                with act.Fori(0, GROUPS) as g:
                    for k in range(KT):
                        act.wait_ge(proj_ps, g * KT + k + 2)
                        if k == 0:
                            act.wait_ge(gu_ps, g * IT + 1)
                        act.activation(hT[:, k, :], bk(4 + k % 2), ACT.Copy).then_inc(h_ready, 1)
                    for i in range(IT):
                        act.wait_ge(gu_ps, g * IT + i + 2)
                        act.wait_ge(hdn_ready, g * IT + i + 1)
                        act.activation(silu[:, i % 2, :], bk(2 * (i % 2)), ACT.Silu, scale=gs[:, i:i + 1]).then_inc(silu_ready, 1)
                    def x1T_copy(j):
                        act.wait_ge(x1T_ps, g * TPG + j + 1)
                        act.wait_ge(qkv_ps, g * TPG + 1)
                        act.activation(x1T[:, :, j * P:(j + 1) * P], bk(6).rearrange("p (k n) -> p k n", n=P), ACT.Copy).then_inc(x1T_ready, 1)
                        act.wait_ge(res_ready, g * TPG + j + 2)
                        act.dma_start(x1_dram[bass.ds(g * GT + j * P, P), :], x1[:, j % 2, :]).then_inc(x1_stored[j % 2], 16)

                    def qkv_copy(j):
                        act.wait_ge(qkv_ps, g * TPG + j + 2)
                        act.wait_ge(qk_ready, g * TPG + j + 1)
                        act.wait_ge(kv_stored[j % 2], g * 32 + 16 * (j // 2) + 16)
                        act.activation(sq[:, :], bank[j % 2][:, :, :].rearrange("p a n -> p (a n)")[:, 0:NQK * HD], ACT.Square).then_inc(qkv_sq, 1)
                        act.activation(raw[:, j % 2, :], bank[j % 2][:, :, :].rearrange("p a n -> p (a n)")[:, 0:NQK * HD], ACT.Copy)
                        act.activation(kv_out[:, j % 2, G * HD:], bk(2 * (j % 2) + 1)[:, G * HD:], ACT.Copy).then_inc(qkv_copied, 1)

                    def roots(j):
                        act.wait_ge(std_arg, g * TPG + j + 1)
                        act.activation(ssum[:, 2, :], ssum[:, 1, :], ACT.Sqrt).then_inc(std_ready, 1)

                    def store(j):
                        act.wait_ge(qk_ready, g * TPG + j + 3)
                        act.dma_start(q_dram[bass.ds(g * GT + j * P, P), :], q_out[:, j % 2, :]).then_inc(q_stored[j % 2], 16)
                        act.dma_start(kv_dram[bass.ds(g * GT + j * P, P), :], kv_out[:, j % 2, :]).then_inc(kv_stored[j % 2], 16)

                    x1T_copy(0)
                    x1T_copy(1)
                    qkv_copy(0)
                    roots(0)
                    x1T_copy(2)
                    store(0)
                    qkv_copy(1)
                    roots(1)
                    x1T_copy(3)
                    store(1)
                    for j in (2, 3):
                        qkv_copy(j)
                        roots(j)
                        store(j)
                for s in x1_stored:
                    act.wait_ge(s, 16 * (GROUPS * TPG // 2) + 16)
                for s in q_stored + kv_stored:
                    act.wait_ge(s, 16 * (GROUPS * TPG // 2) + 16)

            @block.vector
            def _(dve):
                dve.memset(cw[:, :, :], 0.0).then_inc(cw_zero, 1)
                dve.sem_inc(res_ready, 1)
                dve.sem_inc(hdn_ready, 2)
                dve.sem_inc(qk_ready, 2)
                for s in x1_stored + q_stored + kv_stored:
                    dve.sem_inc(s, 16)
                dve.wait_ge(weights_loaded, WEIGHTS)
                with dve.Fori(0, GROUPS) as g:
                    n = Count()

                    def owners(c):
                        full = [P, KCOLS, NSEG]
                        flat = lambda t: t[:, :, :].rearrange("p b i -> p (b i)").unsqueeze(1).to_broadcast(full)
                        cols = bass.ds(g * (SPG * NCH) + c * KCOLS, KCOLS)
                        addr = key_addr[:, cols]
                        dve.tensor_tensor(own_u[:, :, :], addr.unsqueeze(2).to_broadcast(full), flat(seg_shift), ALU.add).then_inc(d0, 1)
                        dve.wait_ge(d0, g * DSTEPS + n.next())
                        dve.tensor_tensor(own_m[:, :, :], own_u[:, :, :], flat(seg_lo), ALU.is_ge).then_inc(d0, 1)
                        dve.wait_ge(d0, g * DSTEPS + n.next())
                        dve.tensor_tensor(own_m[:, :, :], own_m[:, :, :], own_u[:, :, :], ALU.mult).then_inc(d0, 1)
                        dve.wait_ge(d0, g * DSTEPS + n.next())
                        dve.tensor_tensor(own_u[:, :, :], own_u[:, :, :], flat(seg_hi), ALU.is_lt).then_inc(d0, 1)
                        dve.wait_ge(d0, g * DSTEPS + n.next())
                        dve.tensor_tensor(own_u[:, :, :], own_u[:, :, :], own_m[:, :, :], ALU.mult).then_inc(d0, 1)
                        dve.wait_ge(d0, g * DSTEPS + n.next())
                        dve.tensor_reduce(owner[:, 0, :], own_u[:, :, :], AX, ALU.max).then_inc(d0, 1)
                        dve.wait_ge(d0, g * DSTEPS + n.next())
                        dve.tensor_scalar(owner[:, 1, :], owner[:, 0, :], 0.0, SKIP, ALU.is_gt, ALU.mult).then_inc(d0, 1)
                        dve.wait_ge(d0, g * DSTEPS + n.next())
                        dve.tensor_tensor(own_cache[:, cols], owner[:, 1, :], addr, ALU.add).then_inc(d0, 1)
                        dve.wait_ge(d0, g * DSTEPS + n.next())
                        dve.tensor_scalar(owner[:, 1, :], owner[:, 1, :], -1.0, SKIP - 1.0, ALU.mult, ALU.add).then_inc(d0, 1)
                        dve.wait_ge(d0, g * DSTEPS + n.next())
                        dve.tensor_tensor(own_new[:, cols], owner[:, 1, :], owner[:, 0, :], ALU.add).then_inc(d0, 1)
                        dve.wait_ge(d0, g * DSTEPS + n.next())

                    OWN = SPG * NCH // KCOLS
                    for i in range(IT):
                        dve.wait_ge(silu_ready, g * IT + i + 1)
                        if i == 0:
                            dve.wait_ge(down_ps, g * TPG + 1)
                        dve.scalar_tensor_tensor(out=hdn[:, i, :], in0=bk(2 * (i % 2) + 1), scalar=us[:, i:i + 1], in1=silu[:, i % 2, :],
                                                 op0=ALU.mult, op1=ALU.mult).then_inc(hdn_ready, 1)
                        if i < OWN:
                            owners(i)

                    def residual(j):
                        dve.wait_ge(down_ps, g * TPG + j + 2)
                        if j == 0:
                            dve.wait_ge(xr_loaded, g * 16 + 16)
                        dve.wait_ge(x1_stored[j % 2], g * 32 + 16 * (j // 2) + 16)
                        if j >= 2:
                            dve.wait_ge(x1T_ps, g * TPG + j - 1)
                        dve.tensor_tensor(x1[:, j % 2, :], bk(4 + j % 2), dscale[:, :], ALU.mult).then_inc(d0, 1)
                        dve.wait_ge(d0, g * DSTEPS + n.next())
                        dve.tensor_tensor(x1[:, j % 2, :], x1[:, j % 2, :], xr[:, j, :], ALU.add).then_inc(res_ready, 1)

                    def rotate(j):
                        heads = raw[:, j % 2, :].rearrange("p (h d) -> p h d", d=HD)
                        wide = [P, NQK, HALF]
                        tile_cos = cos[:, bass.ds(g * TPG + j, 1), :].to_broadcast(wide)
                        tile_sin = sin[:, bass.ds(g * TPG + j, 1), :].to_broadcast(wide)
                        dve.wait_ge(qkv_sq, g * TPG + j + 1)
                        dve.tensor_reduce(ssum[:, 0, :], sq[:, :].rearrange("p (h d) -> p h d", d=HD), AX, ALU.add).then_inc(d0, 1)
                        dve.wait_ge(d0, g * DSTEPS + n.next())
                        dve.tensor_scalar(ssum[:, 1, :], ssum[:, 0, :], 1.0 / HD, EPS, ALU.mult, ALU.add).then_inc(std_arg, 1)
                        dve.wait_ge(qkv_copied, g * TPG + j + 2)
                        dve.tensor_tensor(heads, heads, nscale[:, :, :], ALU.mult).then_inc(d0, 1)
                        dve.wait_ge(d0, g * DSTEPS + n.next())
                        dve.wait_ge(std_ready, g * TPG + j + 1)
                        dve.reciprocal(ssum[:, 0, :], ssum[:, 2, :]).then_inc(d0, 1)
                        dve.wait_ge(d0, g * DSTEPS + n.next())
                        dve.tensor_tensor(heads, heads, ssum[:, 0, :].unsqueeze(2).to_broadcast([P, NQK, HD]), ALU.mult).then_inc(d0, 1)
                        dve.wait_ge(d0, g * DSTEPS + n.next())
                        x_lo, x_hi = heads[:, :, 0:HALF], heads[:, :, HALF:HD]
                        dve.wait_ge(q_stored[j % 2], g * 32 + 16 * (j // 2) + 16)
                        dve.wait_ge(kv_stored[j % 2], g * 32 + 16 * (j // 2) + 16)
                        for part, (first, second, op) in enumerate(((x_lo, x_hi, ALU.subtract), (x_hi, x_lo, ALU.add))):
                            dve.tensor_tensor(rot_a[:, :, :], first, tile_cos, ALU.mult).then_inc(d0, 1)
                            dve.tensor_tensor(rot_b[:, :, :], second, tile_sin, ALU.mult).then_inc(d0, 1)
                            n.next()
                            dve.wait_ge(d0, g * DSTEPS + n.next())
                            at = slice(part * HALF, (part + 1) * HALF)
                            dve.tensor_tensor(q_out[:, j % 2, :].rearrange("p (h d) -> p h d", d=HD)[:, :, at],
                                              rot_a[:, 0:H, :], rot_b[:, 0:H, :], op).then_inc(d0, 1)
                            last = dve.tensor_tensor(kv_out[:, j % 2, 0:G * HD].rearrange("p (h d) -> p h d", d=HD)[:, :, at],
                                                     rot_a[:, H:NQK, :], rot_b[:, H:NQK, :], op)
                            last.then_inc(d0, 1)
                            n.next()
                            dve.wait_ge(d0, g * DSTEPS + n.next())
                        dve.sem_inc(qk_ready, 1)

                    residual(0)
                    residual(1)
                    residual(2)
                    rotate(0)
                    residual(3)
                    rotate(1)
                    rotate(2)
                    rotate(3)
                    assert n.n == DSTEPS, n.n

            @block.gpsimd
            def _(pool):
                pool.wait_ge(weights_loaded, WEIGHTS)
                for c in range(KT):
                    for h in range(2):
                        if 2 * c + h >= 1:
                            pool.wait_ge(table_init, 16 * (2 * c + h))
                        half = wT_sb[:, c, h * (T // 2):(h + 1) * (T // 2)]
                        pool.tensor_copy(wexp[:, :, :], half.unsqueeze(2).to_broadcast([P, T // 2, E])).then_inc(wexp_full, 1)
                        pool.wait_ge(wexp_full, 2 * c + h + 1)
                        pool.dma_start(table_dram[c * P * T:(c + 1) * P * T, :].rearrange("(p h r) e -> p h (r e)", p=P, h=2)[:, h, :],
                                       wexp[:, :, :].rearrange("p r e -> p (r e)")).then_inc(table_init, 16)
                pool.dma_start(table_dram[TBL:TBL + P, :], zero8[:, :]).then_inc(table_init, 16)
                pool.wait_ge(table_init, TABLE_INIT)
                with pool.Fori(0, SCH) as s:
                    pool.tensor_copy(slot_idx[:, :], table_idx[:, bass.ds(s, 1)]).then_inc(slot_ready, 1)
                    pool.tensor_copy(slot_val[:, :], tot[:, bass.ds(s, 1), :].rearrange("p a e -> p (a e)")).then_inc(slot_ready, 1)
                    pool.wait_ge(slot_ready, s * 2 + 2)
                    pool.sem_inc(slot_taken, 1)
                    pool.indirect_dma_start(table_dram, bass.IndirectOffsetOnAxis(slot_idx[:, 0:1], 0), slot_val[:, :], None,
                                            compute_op=ALU.add).then_inc(entry_added, 16)
                    pool.wait_ge(entry_added, s * 16 + 16)


        wo_loaded = sem("wo_loaded")
        piece_loaded = [sem(f"piece_loaded{r}") for r in range(2)]
        piece_hi = sem("piece_hi")
        experts_ready = sem("experts_ready")
        idx_copied = sem("idx_copied")
        idx_taken = sem("idx_taken")
        kv_gathered = [sem(f"kv_gathered{u}") for u in range(2)]
        q_loaded = [sem(f"q_loaded{u}") for u in range(2)]
        acc_loaded = [sem(f"acc_loaded{u}") for u in range(2)]
        out_stored = [sem(f"out_stored{u}") for u in range(2)]
        kT_ps = sem("kT_ps")
        kT_ready = sem("kT_ready")
        qT_ps = sem("qT_ps")
        qT_ready = sem("qT_ready")
        mask_ready = sem("mask_ready")
        score_ps = sem("score_ps")
        score_taken = sem("score_taken")
        sm_ready = sem("sm_ready")
        nmx_ready = sem("nmx_ready")
        prob_ready = sem("prob_ready")
        pT_ps = sem("pT_ps")
        pT_ready = sem("pT_ready")
        o_ps = sem("o_ps")
        o_ready = sem("o_ready")
        oT_ps = sem("oT_ps")
        oT_ready = sem("oT_ready")
        yT_ps = sem("yT_ps")
        yT_ready = sem("yT_ready")
        lg_ps = sem("lg_ps")
        lg_read = sem("lg_read")
        lg_negmax = sem("lg_negmax")
        lg_exp = sem("lg_exp")
        rw_ready = sem("rw_ready")
        mix_ps = sem("mix_ps")
        mix_done = sem("mix_done")
        mask_step = sem("mask_step")
        rinv_step = sem("rinv_step")
        route_step = sem("route_step")
        ROUTE_STEPS = 11
        GATHERS = 16 * (4 + 2 * NCH)

        def each_pair(eng, pair):
            pair(0, 0, None, (1, 1, 0))
            with eng.Fori(0, PAIRS // 2 - 1) as i:
                pair(i * 2 + 1, 1, i * 2, (i * 2 + 2, 0, i + 1))
                pair(i * 2 + 2, 0, i * 2 + 1, (i * 2 + 3, 1, i + 1))
            pair(PAIRS - 1, 1, PAIRS - 2, None)

        with nc.Block() as block:
            @block.sync
            def _(sp):
                sp.dma_start(wo[:, :, :], wo_t.rearrange("(k p) n -> p k n", p=P)).then_inc(wo_loaded, 16)

                sp.dma_start(q_t[:, 0, :], q_dram[0:P, :]).then_inc(q_loaded[0], 16)
                for k in range(KT):
                    for r in range(PIECES):
                        if k * PIECES + r >= 2:
                            sp.wait_ge(experts_ready, k * PIECES + r - 1)
                        sp.dma_start(stage[:, r % 2, :, :], table_dram[k * P * T:(k + 1) * P * T, :].rearrange(
                            "(p r) e -> p r e", p=P)[:, r * PIECE:(r + 1) * PIECE, :]).then_inc(piece_loaded[r % 2], 16)
                sp.dma_start(acc[:, 0, :], x1_dram[0:P, :]).then_inc(acc_loaded[0], 16)
                sp.dma_start(q_t[:, 1, :], q_dram[P:2 * P, :]).then_inc(q_loaded[1], 16)
                sp.dma_start(acc[:, 1, :], x1_dram[P:2 * P, :]).then_inc(acc_loaded[1], 16)
                with sp.Fori(1, PAIRS // 2) as i:
                    for u in range(2):
                        sp.wait_ge(qT_ps, i * 2 + (u + 1))
                        sp.dma_start(q_t[:, u, :], q_dram[bass.ds(i * (2 * P) + u * P, P), :]).then_inc(q_loaded[u], 16)
                        sp.wait_ge(out_stored[u], i * 16 + 16)
                        sp.dma_start(acc[:, u, :], x1_dram[bass.ds(i * (2 * P) + u * P, P), :]).then_inc(acc_loaded[u], 16)

            @block.gpsimd
            def _(pool):
                with pool.Fori(0, PAIRS // 2) as i:
                    for u in range(2):
                        cols = bass.ds(i * (4 * NCH) + u * (2 * NCH), 2 * NCH)
                        pool.tensor_copy(idx_c[u][:, :], own_cache[:, cols]).then_inc(idx_copied, 1)
                        pool.tensor_copy(idx_n[u][:, :], own_new[:, cols]).then_inc(idx_copied, 1)
                        pool.wait_ge(idx_copied, i * 4 + (2 * u + 2))
                        pool.sem_inc(idx_taken, 1)
                        pool.wait_ge(o_ps, i * 4 + (2 * u + 2))
                        pool.sem_inc(idx_taken, 1)
                        for b in range(2):
                            for c in range(2):
                                pool.indirect_dma_start(kv_t[u][b][:, c, :], None, kv_cache,
                                                        bass.IndirectOffsetOnAxis(idx_c[u][:, b * NCH + c:b * NCH + c + 1], 0),
                                                        bounds_check=POOL_ROWS - 1, oob_is_err=False).then_inc(kv_gathered[u], 16)
                        pool.wait_ge(kv_gathered[u], i * GATHERS + 16 * 4)
                        pool.sem_inc(idx_taken, 1)
                        for b in range(2):
                            for c, rows in enumerate(KCH):
                                pool.indirect_dma_start(kv_t[u][b][0:rows, c, :], None, kv_dram,
                                                        bass.IndirectOffsetOnAxis(idx_n[u][0:rows, b * NCH + c:b * NCH + c + 1], 0),
                                                        bounds_check=TOK - 1, oob_is_err=False).then_inc(kv_gathered[u], 16)
                        pool.wait_ge(kv_gathered[u], i * GATHERS + GATHERS)
                        pool.sem_inc(idx_taken, 1)

            @block.tensor
            def _(pe):
                pe.sem_inc(o_ps, 4)
                pe.sem_inc(qT_ps, 2)

                def mix_expert(m, e):
                    pe.wait_ge(mix_done, m * E + (e + 1))
                    for k in range(KT):
                        for n, (y, w) in enumerate(((yT_hi, experts_hi), (yT_hi, experts_lo), (yT_lo, experts_hi))):
                            mm = pe.matmul(bk(5 + 2 * (e % 2)), y[:, k, :].bitcast(F32R), w[:, k, e, :].bitcast(F32R),
                                           start=(k == 0 and n == 0), stop=(k == KT - 1 and n == 2))
                    mm.then_inc(mix_ps, 1)

                def turn_k(pr, b):
                    p, u, use = pr
                    for gp in range(2):
                        for c, rows in enumerate(KCH):
                            mm = pe.transpose(bk(5 + 2 * gp)[:, c * P:c * P + rows], kv_t[u][b][0:rows, c, gp * P:(gp + 1) * P],
                                              ident[0:rows, 0:rows])
                    mm.then_inc(kT_ps, 1)

                def turn_q(pr):
                    p, u, use = pr
                    pe.wait_ge(q_loaded[u], use * 16 + 16)
                    for k in range(KT):
                        mm = pe.transpose(bk(6)[:, k * P:(k + 1) * P], q_t[:, u, k * P:(k + 1) * P], ident[:, :])
                    mm.then_inc(qT_ps, 1)

                def pair(p, u, mix, nxt):
                    def score(s):
                        b, gp, g = s // 4, s // 2 % 2, s % 2
                        rows = slice(g * HD, (g + 1) * HD)
                        if s == 0:
                            pe.wait_ge(qT_ready, p * 2 + 2)
                            pe.wait_ge(kT_ready, p * 4 + 4)
                        pe.wait_ge(sm_ready, p * 8 + (s + 1))
                        pe.matmul(bk(s % 2)[:, 0:KEYS], qT[rows, gp, b, :, :].rearrange("p h t -> p (h t)"), kT[rows, b, gp, :],
                                  start=True, stop=True).then_inc(score_ps, 1)

                    score(0)
                    for s in range(8):
                        if s < 7:
                            score(s + 1)
                        if s == 0:
                            pe.wait_ge(lg_read, p + 1)
                        pe.wait_ge(prob_ready, p * 8 + (s + 3))
                        for c, rows in enumerate(KCH):
                            mm = pe.transpose(bk(4)[0:rows, c * P:(c + 1) * P], prob[:, s % 2, c * P:c * P + rows], ident[:, :])
                        mm.then_inc(pT_ps, 1)
                        if mix is not None:
                            mix_expert(mix, s)
                        pe.wait_ge(pT_ready, p * 8 + (s + 1))
                        b, g = s // 4, s % 4
                        for c, rows in enumerate(KCH):
                            mm = pe.matmul(bk(2 if b else 6)[:, g * HD:(g + 1) * HD], pT[0:rows, s % 2, c, :],
                                           kv_t[u][b][0:rows, c, (G + g) * HD:(G + g + 1) * HD], start=(c == 0), stop=(c == NCH - 1))
                        if g == 3:
                            mm.then_inc(o_ps, 1)
                    if nxt is not None:
                        pe.wait_ge(kv_gathered[nxt[1]], nxt[2] * GATHERS + GATHERS)
                        if mix is not None:
                            pe.wait_ge(mix_done, mix * E + (E + 2))
                        turn_k(nxt, 0)
                    pe.wait_ge(o_ready, p * 2 + 2)
                    for b in range(2):
                        for gp in range(2):
                            at = (2 * b + gp) * P
                            mm = pe.transpose(bk(3)[:, at:at + P], o_sb[:, b, gp * P:(gp + 1) * P], ident[:, :])
                    mm.then_inc(oT_ps, 1)
                    if nxt is not None:
                        turn_q(nxt)
                    if mix is None:
                        pe.wait_ge(wo_loaded, 16)
                    pe.wait_ge(oT_ready, p + 1)
                    for d in range(KT):
                        for k in range(KT):
                            mm = pe.matmul(bk(2)[:, d * P:(d + 1) * P], wo[:, k, d * P:(d + 1) * P],
                                           oT[:, :, k // 2, k % 2, :], start=(k == 0), stop=(k == KT - 1))
                    mm.then_inc(yT_ps, 1)
                    if nxt is not None:
                        pe.wait_ge(kT_ready, p * 4 + 6)
                        turn_k(nxt, 1)
                    for half, y in enumerate((yT_hi, yT_lo)):
                        pe.wait_ge(yT_ready, p * 2 + (half + 1))
                        for k in range(KT):
                            mm = pe.matmul(bk(4)[:, 0:E], y[:, k, :], route_w[:, k, :],
                                           start=(half == 0 and k == 0), stop=(half == 1 and k == KT - 1))
                    mm.then_inc(lg_ps, 1)
                    if mix is None:
                        pe.wait_ge(experts_ready, KT * PIECES)

                pe.wait_ge(kv_gathered[0], GATHERS)
                turn_k((0, 0, 0), 0)
                turn_q((0, 0, 0))
                pe.wait_ge(kT_ready, 2)
                turn_k((0, 0, 0), 1)
                each_pair(pe, pair)
                for e in range(E):
                    mix_expert(PAIRS - 1, e)

            @block.scalar
            def _(act):
                for s in out_stored:
                    act.sem_inc(s, 16)

                def store(m, u):
                    act.wait_ge(mix_done, m * E + (E + 2))
                    act.dma_start(out[bass.ds(m * P, P), :], acc[:, u, :]).then_inc(out_stored[u], 16)

                def kT_copy(p, b):
                    act.wait_ge(kT_ps, p * 2 + (b + 1))
                    act.activation(kT[:, b, 0, :], bk(5)[:, 0:KEYS], ACT.Copy).then_inc(kT_ready, 1)

                def qT_copy(p):
                    act.wait_ge(qT_ps, p + 3)
                    for gp in range(2):
                        act.activation(qT[:, gp, :, :, :].rearrange("p b h t -> p h b t"),
                                       bk(6)[:, gp * T // 2:(gp + 1) * T // 2].rearrange("p (h b t) -> p h b t", h=2, b=2),
                                       ACT.Copy).then_inc(qT_ready, 1)

                def route_exp(p):
                    act.wait_ge(lg_negmax, p + 1)
                    act.activation(rt[:, 2, :], lg[:, :], ACT.Exp, bias=rt[:, 1, 0:1]).then_inc(lg_exp, 1)

                def pair(p, u, mix, nxt):
                    for s in range(8):
                        act.wait_ge(nmx_ready, p * 8 + (s + 1))
                        act.activation(prob[:, s % 2, :], sm[:, s % 2, :], ACT.Exp, bias=nmx[:, s:s + 1], scale=SCALE,
                                       accum_out=rsum[:, s:s + 1]).then_inc(prob_ready, 1)
                        if s == 0 and mix is not None:
                            route_exp(mix)
                        act.wait_ge(pT_ps, p * 8 + (s + 1))
                        act.activation(pT[:, s % 2, 0:2, :], bk(4)[:, 0:2 * P].rearrange("p (c t) -> p c t", c=2), ACT.Copy)
                        act.activation(pT[0:C, s % 2, 2, :], bk(4)[0:C, 2 * P:3 * P], ACT.Copy).then_inc(pT_ready, 1)
                        if mix is None:
                            for piece in (2 * s, 2 * s + 1):
                                k, r = piece // PIECES, piece % PIECES
                                act.wait_ge(piece_loaded[piece % 2], piece // 2 * 16 + 16)
                                act.activation(experts_hi[:, k, :, r * PIECE:(r + 1) * PIECE].bitcast(F32R),
                                               stage[:, r % 2, :, :].rearrange("p r e -> p e r"), ACT.Copy).then_inc(piece_hi, 1)
                    if nxt is not None:
                        kT_copy(nxt[0], 0)
                    act.wait_ge(oT_ps, p + 1)
                    act.activation(oT[:, :, :, :, :].rearrange("p b g h t -> p (b g h t)"), bk(3), ACT.Copy).then_inc(oT_ready, 1)
                    if nxt is not None:
                        qT_copy(nxt[0])
                    act.wait_ge(yT_ps, p + 1)
                    act.activation(yT_hi[:, :, :].bitcast(F32R), bk(2).rearrange("p (k n) -> p k n", n=P), ACT.Copy).then_inc(yT_ready, 1)
                    if nxt is not None:
                        kT_copy(nxt[0], 1)
                    if mix is not None:
                        store(mix, 1 - u)

                kT_copy(0, 0)
                qT_copy(0)
                kT_copy(0, 1)
                each_pair(act, pair)
                route_exp(PAIRS - 1)
                store(PAIRS - 1, 1)
                for s in out_stored:
                    act.wait_ge(s, 16 * (PAIRS // 2) + 16)

            @block.vector
            def _(dve):
                dve.sem_inc(sm_ready, 2)
                dve.sem_inc(mix_done, 2)
                dve.sem_inc(lg_read, 1)

                def mix_add(m, u, e):
                    dve.wait_ge(mix_ps, m * E + (e + 1))
                    dve.wait_ge(mix_done, m * E + (e + 2))
                    dve.scalar_tensor_tensor(out=acc[:, u, :], in0=bk(5 + 2 * (e % 2)), scalar=rt[:, 6, e:e + 1], in1=acc[:, u, :],
                                             op0=ALU.mult, op1=ALU.add).then_inc(mix_done, 1)

                def kT_copy(p, b):
                    dve.wait_ge(kT_ps, p * 2 + (b + 1))
                    dve.tensor_copy(kT[:, b, 1, :], bk(7)[:, 0:KEYS]).then_inc(kT_ready, 1)

                def make_mask(p, b):
                    first = thr[:, bass.ds(p * 2 + b, 1)].to_broadcast([P, KEYS])
                    dve.tensor_tensor(mask[:, b, :], jrow[:, :], first, ALU.is_lt).then_inc(mask_step, 1)
                    dve.wait_ge(mask_step, p * 4 + (2 * b + 1))
                    dve.scalar_tensor_tensor(out=mask[:, b, :], in0=mask[:, b, :], scalar=MASKED, in1=band[:, :],
                                             op0=ALU.mult, op1=ALU.add).then_inc(mask_step, 1)

                def clip(p):
                    dve.wait_ge(lg_ps, p + 1)
                    dve.tensor_scalar(lg[:, :], bk(4)[:, 0:E], 50.0, -50.0, ALU.min, ALU.max).then_inc(lg_read, 1)

                def route(p):
                    n = Count()

                    def step(ins):
                        ins.then_inc(route_step, 1)
                        dve.wait_ge(route_step, p * ROUTE_STEPS + n.next())

                    dve.wait_ge(lg_read, p + 2)
                    step(dve.tensor_reduce(rt[:, 0, 0:1], lg[:, :], AX, ALU.max))
                    dve.tensor_scalar(rt[:, 1, 0:1], rt[:, 0, 0:1], -1.0, None, ALU.mult).then_inc(lg_negmax, 1)
                    other = lg[:, :].unsqueeze(1).to_broadcast([P, E, E])
                    own = lg[:, :].unsqueeze(2).to_broadcast([P, E, E])
                    step(dve.tensor_tensor(gtr[:, :, :], other, own, ALU.is_gt))
                    step(dve.tensor_tensor(eqr[:, :, :], other, own, ALU.is_equal))
                    step(dve.tensor_tensor(eqr[:, :, :], eqr[:, :, :], before[:, :, :], ALU.mult))
                    step(dve.tensor_tensor(gtr[:, :, :], gtr[:, :, :], eqr[:, :, :], ALU.add))
                    step(dve.tensor_reduce(rt[:, 3, :], gtr[:, :, :], AX, ALU.add))
                    step(dve.tensor_scalar(rt[:, 3, :], rt[:, 3, :], 2.0, None, ALU.is_lt))
                    dve.wait_ge(lg_exp, p + 1)
                    step(dve.tensor_tensor(rt[:, 4, :], rt[:, 3, :], rt[:, 2, :], ALU.mult))
                    step(dve.tensor_reduce(rt[:, 5, 0:1], rt[:, 4, :], AX, ALU.add))
                    step(dve.reciprocal(rt[:, 5, 1:2], rt[:, 5, 0:1]))
                    step(dve.tensor_scalar(rt[:, 6, :], rt[:, 4, :], rt[:, 5, 1:2], None, ALU.mult))
                    assert n.n == ROUTE_STEPS, n.n

                def low_parts(s):
                    for piece in (2 * s, 2 * s + 1):
                        k, r = piece // PIECES, piece % PIECES
                        dve.wait_ge(piece_hi, piece + 1)
                        at = slice(r * PIECE, (r + 1) * PIECE)
                        dve.tensor_tensor(experts_lo[:, k, :, at].bitcast(F32R), stage[:, r % 2, :, :].rearrange("p r e -> p e r"),
                                          experts_hi[:, k, :, at], ALU.subtract).then_inc(experts_ready, 1)

                def pair(p, u, mix, nxt):
                    def finish(s):
                        b = s // 4
                        if mix is not None:
                            if s == 0:
                                dve.wait_ge(acc_loaded[1 - u], (mix - (1 - u)) * 8 + 16)
                            mix_add(mix, 1 - u, s)
                        if s % 4 == 3:
                            dve.wait_ge(o_ps, p * 2 + (b + 5))
                            dve.reciprocal(rinv[:, 4 * b:4 * b + 4], rsum[:, 4 * b:4 * b + 4]).then_inc(rinv_step, 1)
                            dve.wait_ge(rinv_step, p * 2 + (b + 1))
                            dve.tensor_tensor(o_sb[:, b, :].rearrange("p (g d) -> p g d", g=G),
                                              bk(2 if b else 6)[:, 0:G * HD].rearrange("p (g d) -> p g d", g=G),
                                              rinv[:, 4 * b:4 * b + 4].unsqueeze(2).to_broadcast([P, G, HD]), ALU.mult).then_inc(o_ready, 1)

                    dve.wait_ge(mask_step, p * 4 + 4)
                    for s in range(8):
                        dve.wait_ge(score_ps, p * 8 + (s + 1))
                        dve.wait_ge(prob_ready, p * 8 + (s + 1))
                        dve.sem_inc(score_taken, 1)
                        dve.tensor_tensor_reduce(sm[:, s % 2, :], bk(s % 2)[:, 0:KEYS], mask[:, s // 4, :], 1.0, MASKED,
                                                 ALU.add, ALU.max, mx[:, s:s + 1]).then_inc(sm_ready, 1)
                        dve.wait_ge(sm_ready, p * 8 + (s + 3))
                        dve.tensor_scalar(nmx[:, s:s + 1], mx[:, s:s + 1], -SCALE, None, ALU.mult).then_inc(nmx_ready, 1)
                        if s == 0 and mix is not None:
                            route(mix)
                        if s >= 1:
                            finish(s - 1)
                        if s >= 1 and mix is None:
                            low_parts(s - 1)
                        if s == 5 and nxt is not None:
                            make_mask(nxt[0], 0)
                    if nxt is not None:
                        make_mask(nxt[0], 1)
                    finish(7)
                    if mix is None:
                        low_parts(7)
                    if nxt is not None:
                        kT_copy(nxt[0], 0)
                    dve.wait_ge(yT_ready, p * 2 + 1)
                    dve.tensor_tensor(yT_lo[:, :, :].bitcast(F32R), bk(2).rearrange("p (k n) -> p k n", n=P), yT_hi[:, :, :],
                                      ALU.subtract).then_inc(yT_ready, 1)
                    if nxt is not None:
                        kT_copy(nxt[0], 1)
                    clip(p)

                dve.sem_inc(prob_ready, 2)
                make_mask(0, 0)
                make_mask(0, 1)
                kT_copy(0, 0)
                kT_copy(0, 1)
                each_pair(dve, pair)
                route(PAIRS - 1)
                dve.wait_ge(acc_loaded[1], 16 * (PAIRS // 2))
                for e in range(E):
                    mix_add(PAIRS - 1, 1, e)



def _arrays(inputs):
    i = {k: np.asarray(v) for k, v in inputs.items()}
    heads = [(2 * gp + g) * 2 + h2 for gp in range(2) for h2 in range(2) for g in range(2)]
    wq = i["L1_cond_Wq"].reshape(H, HD, T)[heads].reshape(H * HD, T)
    wo = i["L1_cond_Wo"].reshape(T, H, HD)[:, heads].reshape(T, H * HD)
    kc, vc = (i[f"L1_cond_{n}_blocks"].transpose(0, 2, 1, 3).reshape(POOL_ROWS, G * HD) for n in "kv")
    half = np.arange(HALF, dtype=np.float32) / np.float32(HALF)
    return {
        "x": i["x"].reshape(TOK, T),
        "kv_lens": i["itok_B_37_3939"],
        "subjects": i["itok_B_0_7"].reshape(1, B),
        "tables": i["itok_Bx257_0_4111"].reshape(B * NBLK),
        "cond_w": i["L0_cond_weights"],
        "gate_t": i["L0_ffn_gate_w"].T,
        "up_t": i["L0_ffn_up_w"].T,
        "down_t": i["L0_ffn_down_w"].T,
        "gate_s": i["L0_ffn_gate_s"].reshape(IT, P).T,
        "up_s": i["L0_ffn_up_s"].reshape(IT, P).T,
        "down_s": i["L0_ffn_down_s"].reshape(1, T),
        "wqkv_t": np.concatenate([wq, i["L1_cond_Wk"], i["L1_cond_Wv"]]).T,
        "wo_t": wo.T,
        "q_norm": i["L1_cond_q_norm_scale"].reshape(1, HD),
        "k_norm": i["L1_cond_k_norm_scale"].reshape(1, HD),
        "kv_cache": np.concatenate([kc, vc], axis=1),
        "inv_freq": (np.float32(1.0) / np.float32(10000.0) ** half).reshape(1, HALF),
        "route_t": i["L1_ffn_gate_w"].T,
        "w_t": i["L1_ffn_W"].T,
        "atoms": i["L1_ffn_atoms"].reshape(A, P, SCH).transpose(0, 2, 1),
        "expert_atom": i["L1_ffn_expert_atom_weights"],
        "importance": i["L1_ffn_importance"].T.reshape(P, SCH, E),
        "mask_col": i["L1_ffn_mask_idx"].reshape(P, SCH),
        "mask_row": i["L1_ffn_mask_idx"].reshape(P, SCH).T,
    }


def kernel(**inputs):
    import numpy as _np
    import concourse.bacc as _bacc
    from concourse import mybir as _mybir
    from concourse.bass_utils import run_bass_kernel_spmd as _run

    nc = _bacc.Bacc("TRN2", target_bir_lowering=False, num_devices=1)
    arrays, args = {}, {}
    for name, a in _arrays(inputs).items():
        a = _np.ascontiguousarray(a)
        arrays[f"in_{name}"] = a
        args[name] = nc.dram_tensor(f"in_{name}", a.shape, _mybir.dt.from_np(a.dtype), kind="ExternalInput").ap()
    args["out"] = nc.dram_tensor("out_dram", (TOK, T), F32, kind="ExternalOutput").ap()
    bass_adaln_ffn_kernel(nc, **args)
    r = _run(nc, [arrays], core_ids=[0])
    return r.results[0]["out_dram"].reshape(B, C, T)
```

```python
from contextlib import ExitStack

import numpy as np

import concourse.bass as bass
from concourse import mybir

F32 = mybir.dt.float32
F32R = mybir.dt.float32r
I32 = mybir.dt.int32
ALU = mybir.AluOpType
ACT = mybir.ActivationFunctionType
AX = mybir.AxisListType.X

P = 128
B, C, T = 32, 64, 512
TOK = B * C
KT = T // P
NSUB = 8
INTER = 1408
IT = INTER // P
GROUPS = 4
GT = TOK // GROUPS
TPG = GT // P
SPG = B // GROUPS
PAIRS = B // 2
H, G, HD = 8, 4, 64
HALF = HD // 2
NQK = H + G
BLOCK, WINDOW, NBLK = 16, 256, 257
POOL_ROWS = 16 * NBLK * BLOCK
KEYS = WINDOW + C
KCH = (128, 128, 64)
NCH = len(KCH)
SLOTS = 21
SEG = 5
NSEG = B * SEG
SCALE = 256.0 ** -0.5
EPS = 1e-6
E, A, NS = 8, 64, 4096
SCH = NS // P
TBL = T * T
KEY = float(POOL_ROWS + 1)
SKIP = float(1 << 20)
MASKED = -1.0e30
TWO_PI = 2 * np.pi
C1 = 6.28125
C2 = float(np.floor((TWO_PI - C1) * 2**21) / 2**21)
C3 = float(np.float32(TWO_PI - C1 - C2))
MAGIC = 1.5 * 2.0**23
PI_IN = 3.1415925


class Count:

    def __init__(self, start=0):
        self.n = start

    def next(self):
        self.n += 1
        return self.n


def bass_adaln_ffn_kernel(nc, x, kv_lens, subjects, tables, cond_w, gate_t, up_t, down_t, gate_s, up_s, down_s,
                          wqkv_t, wo_t, q_norm, k_norm, kv_cache, inv_freq, route_t, w_t, atoms, expert_atom,
                          importance, mask_col, mask_row, out):
    q_dram = nc.dram_tensor("q_dram", (TOK, T), F32, kind="Internal").ap()
    kv_dram = nc.dram_tensor("kv_dram", (TOK, T), F32, kind="Internal").ap()
    x1_dram = nc.dram_tensor("x1_dram", (TOK, T), F32, kind="Internal").ap()
    table_dram = nc.dram_tensor("table_dram", (TBL + P, E), F32, kind="Internal").ap()

    sbuf_map = [(nc.sbuf_base + 31) // 32 * 32]

    def place(name, shape, dt=F32):
        off = sbuf_map[0]
        sbuf_map[0] = off + (int(np.prod(shape[1:])) * 4 + 31) // 32 * 32
        return nc.alloc_sbuf_tensor_at(name, list(shape), dt, offset=off)

    with ExitStack() as ctx:
        def sem(name):
            return ctx.enter_context(nc.semaphore(name))

        def psum(name, shape):
            return ctx.enter_context(nc.psum_tensor(name, shape, F32))

        ident = place("ident", (P, P))
        own_cache = place("own_cache", (P, B * NCH), I32)
        own_new = place("own_new", (P, B * NCH), I32)
        thr = place("thr", (P, B))
        band = place("band", (P, KEYS))
        jrow = place("jrow", (P, KEYS))
        before = place("before", (P, E, E))
        route_w = place("route_w", (P, KT, E))
        keep_at = sbuf_map[0]
        wqkv = place("wqkv", (P, KT, 2 * T))
        cos = place("cos", (P, PAIRS, HALF))
        sin = place("sin", (P, PAIRS, HALF))
        nscale = place("nscale", (P, NQK, HD))
        dscale = place("dscale", (P, T))
        gs = place("gs", (P, IT))
        us = place("us", (P, IT))
        key_addr = place("key_addr", (P, B * NCH))
        seg_start = place("seg_start", (P, B, SEG))
        seg_len = place("seg_len", (P, B, SEG))
        seg_key = place("seg_key", (P, B, SEG))
        tot = place("tot", (P, SCH, E))
        table_idx = place("table_idx", (P, SCH), I32)
        subj = place("subj", (1, B), I32)
        inexact = place("inexact", (1, 1), I32)
        wT_sb = place("wT_sb", (P, KT, T))
        zero8 = place("zero8", (P, E))
        RCOLS = T // 4
        wexp = place("wexp", (P, RCOLS, E))
        xc = place("xc", (P, TPG, T))
        cw = place("cw", (P, TPG, P))
        weights_at = sbuf_map[0]
        gate_raw = place("gate_raw", (P, KT, INTER))
        up_raw = place("up_raw", (P, KT, INTER))
        down_raw = place("down_raw", (P, IT, T))
        work_at = sbuf_map[0]
        sbuf_map[0] = weights_at
        gate_w = place("gate_w", (P, KT, INTER), F32R)
        up_w = place("up_w", (P, KT, INTER), F32R)
        down_w = place("down_w", (P, IT, T), F32R)
        assert sbuf_map[0] == work_at

        mrow_i = place("mrow_i", (P, SCH, P), I32)
        mrow = place("mrow", (P, SCH, P))
        mcol_i = place("mcol_i", (P, SCH), I32)
        mcol = place("mcol", (P, SCH))
        mhi_i = place("mhi_i", (P, SCH), I32)
        mlo_i = place("mlo_i", (P, SCH), I32)
        mhi = place("mhi", (P, SCH))
        mlo = place("mlo", (P, SCH))
        earlier = place("earlier", (P, SCH))
        lowtri = place("lowtri", (P, P))
        dump_i = place("dump_i", (P, 1), I32)
        dump = place("dump", (P, 1))
        wt = place("wt", (P, SCH, E))
        sig = place("sig", (P, SCH, E))
        eaw = place("eaw", (E, A))
        eaw_s = place("eaw_s", (E, 4))
        eawT = place("eawT", (A, E))
        atoms_sb = place("atoms_sb", (A, SCH, P))
        ang = place("ang", (P, PAIRS, HALF))
        turns = place("turns", (P, PAIRS, HALF))
        kvt_i = place("kvt_i", (P, PAIRS), I32)
        kvt = place("kvt", (P, PAIRS))
        tpos_i = place("tpos_i", (P, 1), I32)
        tpos = place("tpos", (P, 1))
        inv = place("inv", (P, HALF))
        qn = place("qn", (P, 2, HD))
        jrow_i = place("jrow_i", (P, KEYS), I32)
        dist_i = place("dist_i", (P, KEYS), I32)
        dist = place("dist", (P, KEYS))
        bits = place("bits", (P, INTER), I32)
        bits_max = place("bits_max", (P, 1))
        ones = place("ones", (P, 1))
        prologue_end = sbuf_map[0]

        sbuf_map[0] = work_at
        xr = place("xr", (P, TPG, T))
        hT_hi = place("hT_hi", (P, KT, GT))
        hT_lo = place("hT_lo", (P, KT, GT))
        hdn = place("hdn", (P, 2, GT))
        hdn_hi = place("hdn_hi", (P, 3, GT))
        hdn_lo = place("hdn_lo", (P, 3, GT))
        silu = place("silu", (P, 2, GT))
        x1 = place("x1", (P, 2, T))
        x1T = place("x1T", (P, KT, GT))
        rot_a = place("rot_a", (P, NQK, HALF))
        rot_b = place("rot_b", (P, NQK, HALF))
        ssum = place("ssum", (P, 3, NQK))
        KCOLS = 4
        own_v = place("own_v", (P, KCOLS, NSEG))
        own_m = place("own_m", (P, KCOLS, NSEG))
        GCOLS = B * NCH // (GROUPS - 1)
        found = place("found", (P, GCOLS))
        owned = place("owned", (P, GCOLS))
        slot_val = place("slot_val", (P, E))
        slot_idx = place("slot_idx", (P, 1), I32)
        raw_at = sbuf_map[0]
        raw = place("raw", (P, 2, NQK * HD))
        sq = place("sq", (P, NQK * HD))
        q_out = place("q_out", (P, 2, T))
        kv_out = place("kv_out", (P, 2, T))
        layer0_end = sbuf_map[0]

        sbuf_map[0] = max(raw_at, prologue_end)
        oh = place("oh", (P, B, SLOTS))
        tb_f = place("tb_f", (P, B, SLOTS))
        tb_i = place("tb_i", (P, B, SLOTS), I32)
        kv_i = place("kv_i", (P, B), I32)
        kv_f = place("kv_f", (P, B))
        kvq_i = place("kvq_i", (P, B), I32)
        kvr_i = place("kvr_i", (P, B), I32)
        kvq = place("kvq", (P, B))
        kvr = place("kvr", (P, B))
        slot0 = place("slot0", (P, B))
        jcol_i = place("jcol_i", (P, NCH), I32)
        jcol = place("jcol", (P, NCH))
        posk_i = place("posk_i", (P, B, NCH), I32)
        slot_i = place("slot_i", (P, B, NCH), I32)
        off_i = place("off_i", (P, B, NCH), I32)
        rel = place("rel", (P, B, NCH))
        off_f = place("off_f", (P, B, NCH))
        kblk = place("kblk", (P, B, NCH))
        seg_rel = place("seg_rel", (P, B))
        seg_lo = place("seg_lo", (P, B, SEG))
        seg_hi = place("seg_hi", (P, B, SEG))
        seg_t = place("seg_t", (P, B, SEG))
        bbase_i = place("bbase_i", (P, B), I32)
        bbase = place("bbase", (P, B))
        io21_i = place("io21_i", (P, SLOTS), I32)
        io21 = place("io21", (P, SLOTS))
        index_end = sbuf_map[0]

        sbuf_map[0] = keep_at
        experts_hi = place("experts_hi", (P, KT, E, T))
        experts_lo = place("experts_lo", (P, KT, E, T))
        PIECE = T // 4
        PIECES = T // PIECE
        stage = place("stage", (P, 2, PIECE, E))
        wo = place("wo", (P, KT, T))
        kv_t = [[place(f"kv_t{u}{b}", (P, NCH, T)) for b in range(2)] for u in range(2)]
        idx_c = [place(f"idx_c{u}", (P, 2 * NCH), I32) for u in range(2)]
        idx_n = [place(f"idx_n{u}", (P, 2 * NCH), I32) for u in range(2)]
        q_t = place("q_t", (P, 2, T))
        acc = place("acc", (P, 2, T))
        qT = place("qT", (P, 2, 2, 2, C))
        kT = place("kT", (P, 2, 2, KEYS))
        mask = place("mask", (P, 2, KEYS))
        sm = place("sm", (P, 2, KEYS))
        prob = place("prob", (P, 2, KEYS))
        pT = place("pT", (P, 2, NCH, P))
        mx = place("mx", (P, 8))
        nmx = place("nmx", (P, 8))
        rsum = place("rsum", (P, 8))
        rinv = place("rinv", (P, 8))
        o_sb = place("o_sb", (P, 2, G * HD))
        oT = place("oT", (P, 2, 2, 2, C))
        yT_hi = place("yT_hi", (P, KT, P))
        yT_lo = place("yT_lo", (P, KT, P))
        lg = place("lg", (P, E))
        gtr = place("gtr", (P, E, E))
        eqr = place("eqr", (P, E, E))
        rt = place("rt", (P, 8, E))
        layer1_end = sbuf_map[0]
        assert max(index_end, layer0_end, layer1_end) <= nc.sbuf_usable_end, (
            index_end, layer0_end, layer1_end, nc.sbuf_usable_end)

        bank = [psum(f"bank{i}", [P, 2, T]) for i in range(4)]

        def bk(n):
            return bank[n // 2][:, n % 2, :]

        weights_loaded = sem("weights_loaded")
        ffn_loaded = [sem(f"ffn_loaded{k}") for k in range(3)]
        wexp_full = sem("wexp_full")
        table_init = sem("table_init")
        TABLE_INIT = 16 * (T // RCOLS * KT + 1)

        kv_loaded = sem("kv_loaded")
        consts_loaded = sem("consts_loaded")
        tables_loaded = [sem(f"tables_loaded{k}") for k in range(2)]
        iotas = sem("iotas")
        sparse_loaded = sem("sparse_loaded")
        p_dve = sem("p_dve")
        eaw_max = sem("eaw_max")
        eaw_exp = sem("eaw_exp")
        eaw_norm = sem("eaw_norm")
        eaw_T = sem("eaw_T")
        eaw_Tsb = sem("eaw_Tsb")
        delta_ps = sem("delta_ps")
        sig_ready = sem("sig_ready")
        wt_ready = sem("wt_ready")
        eq_ready = sem("eq_ready")
        tot_ps = sem("tot_ps")
        sin_arg = sem("sin_arg")
        sin_done = sem("sin_done")
        ident_ready = sem("ident_ready")
        w_loaded = sem("w_loaded")
        bits_seen = sem("bits_seen")
        bits_summed = sem("bits_summed")
        inexact_ps = sem("inexact_ps")

        cw_zero = sem("cw_zero")
        subj_loaded = sem("subj_loaded")
        xc_loaded = sem("xc_loaded")
        cw_loaded = sem("cw_loaded")

        def load_blocks(eng, first, end, loaded):
            with eng.Fori(first, end) as b:
                q = eng.snap(eng.value_load(kv_i[0:1, bass.ds(b, 1)], min_val=0, max_val=(NBLK - 1) * BLOCK - C - 1) >> 4)
                slot = eng.snap((q >= 16) * (q - 16)).with_bounds(min_val=0, max_val=NBLK - SLOTS)
                eng.dma_start(tb_i[:, bass.ds(b, 1), :],
                              tables[bass.ds(b * NBLK + slot, SLOTS)].rearrange("(a n) -> a n", a=1).to_broadcast([P, SLOTS])).then_inc(loaded, 16)

        def load_x(eng, g):
            eng.dma_start(xc[:, :, :], x[bass.ds(g * GT, GT), :].rearrange("(k p) t -> p k t", p=P)).then_inc(xc_loaded, 16)
            for s in range(SPG):
                r = eng.value_load(subj[0:1, bass.ds(g * SPG + s, 1)], min_val=0, max_val=NSUB - 1)
                half = s % 2 * C
                eng.dma_start(cw[half:half + C, s // 2, half:half + C], cond_w[bass.ds(r, 1), :, :].rearrange("a c d -> (a c) d")).then_inc(cw_loaded, 16)

        with nc.Block() as block:
            @block.sync
            def _(sp):
                sp.dma_start(subj[:, :], subjects).then_inc(subj_loaded, 16)
                sp.dma_start(kv_i[:, :], kv_lens.rearrange("(a n) -> a n", a=1).to_broadcast([P, B])).then_inc(kv_loaded, 16)
                by_half = kv_lens.rearrange("(i h) -> h i", h=2)
                for h in range(2):
                    with nc.allow_non_contiguous_dma(reason="32 lengths"):
                        sp.dma_start(kvt_i[h * C:(h + 1) * C, :], by_half[h:h + 1, :].to_broadcast([C, PAIRS])).then_inc(consts_loaded, 16)
                sp.dma_start(inv[:, :], inv_freq.to_broadcast([P, HALF])).then_inc(consts_loaded, 16)
                sp.dma_start(qn[:, 0, :], q_norm.to_broadcast([P, HD])).then_inc(consts_loaded, 16)
                sp.dma_start(qn[:, 1, :], k_norm.to_broadcast([P, HD])).then_inc(consts_loaded, 16)
                sp.dma_start(mcol_i[:, :], mask_col).then_inc(sparse_loaded, 16)
                sp.dma_start(mrow_i[:, :, :], mask_row.rearrange("(a c) p -> a c p", a=1).to_broadcast([P, SCH, P])).then_inc(sparse_loaded, 16)
                sp.dma_start(eaw[:, :], expert_atom).then_inc(sparse_loaded, 16)
                sp.dma_start(atoms_sb[:, :, :], atoms).then_inc(sparse_loaded, 16)
                sp.dma_start(sig[:, :, :], importance).then_inc(sparse_loaded, 16)
                sp.wait_ge(kv_loaded, 16)
                load_blocks(sp, 0, B // 2, tables_loaded[0])
                sp.wait_ge(cw_zero, 1)
                sp.wait_ge(subj_loaded, 16)
                load_x(sp, 0)

            @block.gpsimd
            def _(pool):
                pool.memset(cw[:, :, :], 0.0).then_inc(cw_zero, 1)
                pool.memset(ident[:, :], 0.0).then_inc(ident_ready, 1)
                pool.memset(lowtri[:, :], 1.0).then_inc(ident_ready, 1)
                pool.memset(zero8[:, :], 0.0)
                pool.memset(ones[:, :], 1.0)
                pool.memset(before[:, :, :], 1.0).then_inc(ident_ready, 1)
                pool.iota(jcol_i[:, :], [[P, NCH]], base=-WINDOW, channel_multiplier=1).then_inc(iotas, 1)
                pool.iota(io21_i[:, :], [[1, SLOTS]], base=0, channel_multiplier=0).then_inc(iotas, 1)
                pool.iota(bbase_i[:, :], [[C, B]], base=1, channel_multiplier=0).then_inc(iotas, 1)
                pool.iota(jrow_i[:, :], [[1, KEYS]], base=0, channel_multiplier=0).then_inc(iotas, 1)
                pool.iota(dump_i[:, :], [[0, 1]], base=TBL, channel_multiplier=1).then_inc(iotas, 1)
                for h in range(2):
                    pool.wait_ge(iotas, 5 + 2 * h)
                    pool.iota(tpos_i[h * C:(h + 1) * C, :], [[0, 1]], base=0, channel_multiplier=1).then_inc(iotas, 1)
                    pool.iota(dist_i[h * C:(h + 1) * C, :], [[1, KEYS]], base=0, channel_multiplier=-1).then_inc(iotas, 1)
                pool.wait_ge(ident_ready, 3)
                pool.wait_ge(iotas, 9)
                pool.affine_select(out=ident[:, :], in_=ident[:, :], compare_op=ALU.not_equal, fill=1.0,
                                   base=0, pattern=[[-1, P]], channel_multiplier=1).then_inc(ident_ready, 1)
                pool.affine_select(out=lowtri[:, :], in_=lowtri[:, :], compare_op=ALU.is_gt, fill=0.0,
                                   base=0, pattern=[[-1, P]], channel_multiplier=1).then_inc(ident_ready, 1)
                pool.affine_select(out=before[:, :, :], in_=before[:, :, :], compare_op=ALU.is_gt, fill=0.0,
                                   base=0, pattern=[[1, E], [-1, E]], channel_multiplier=0).then_inc(ident_ready, 1)
                pool.wait_ge(kv_loaded, 16)
                load_blocks(pool, B // 2, B, tables_loaded[1])

            @block.scalar
            def _(act):
                act.dma_start(wT_sb[:, :, :], w_t.rearrange("(c p) r -> p c r", p=P)).then_inc(w_loaded, 16)
                act.wait_ge(sparse_loaded, 16 * 5)
                for w, (to, src) in enumerate(((gate_raw, gate_t), (up_raw, up_t), (down_raw, down_t))):
                    act.dma_start(to[:, :, :], src.rearrange("(k p) n -> p k n", p=P)).then_inc(ffn_loaded[w], 16)
                act.dma_start(wqkv[:, :, :], wqkv_t.rearrange("(k p) n -> p k n", p=P)).then_inc(weights_loaded, 16)
                act.dma_start(dscale[:, :], down_s.to_broadcast([P, T])).then_inc(weights_loaded, 16)
                act.dma_start(gs[:, :], gate_s).then_inc(weights_loaded, 16)
                act.dma_start(us[:, :], up_s).then_inc(weights_loaded, 16)
                act.dma_start(route_w[:, :, :], route_t.rearrange("(k p) n -> p k n", p=P)).then_inc(weights_loaded, 16)
                act.activation(sig[:, :, :], sig[:, :, :], ACT.Sigmoid).then_inc(sig_ready, 1)
                act.wait_ge(eaw_max, 1)
                act.activation(eaw[:, :], eaw[:, :], ACT.Exp, bias=eaw_s[:, 1:2], accum_out=eaw_s[:, 2:3]).then_inc(eaw_exp, 1)
                act.wait_ge(sin_arg, 1)
                act.activation(sin[:, :, :], ang[:, :, :], ACT.Sin).then_inc(sin_done, 1)
                act.wait_ge(sin_arg, 2)
                act.activation(cos[:, :, :], turns[:, :, :], ACT.Sin).then_inc(sin_done, 1)
                for w, (to, loaded) in enumerate(((gate_w, gate_raw), (up_w, up_raw), (down_w, down_raw))):
                    act.wait_ge(bits_seen, w + 1)
                    act.activation(to[:, :, :], loaded[:, :, :], ACT.Copy)

            @block.tensor
            def _(pe):
                pe.wait_ge(ident_ready, 6)
                pe.wait_ge(eaw_norm, 1)
                pe.transpose(bk(0)[0:A, 0:E], eaw[:, :], ident[0:E, 0:E]).then_inc(eaw_T, 1)
                pe.wait_ge(eaw_Tsb, 1)
                for s in range(SCH):
                    mm = pe.matmul(bk(1)[:, s * E:(s + 1) * E], atoms_sb[:, s, :], eawT[:, :], start=True, stop=True)
                mm.then_inc(delta_ps, 1)
                pe.wait_ge(wt_ready, 1)
                pe.wait_ge(eq_ready, 1)
                for s in range(SCH):
                    mm = pe.matmul(bk(2)[:, s * E:(s + 1) * E], mrow[:, s, :], wt[:, s, :], start=True, stop=True)
                mm.then_inc(tot_ps, 1)
                pe.wait_ge(bits_summed, 1)
                pe.matmul(bk(3)[0:1, 0:1], bits_max[:, :], ones[:, :], start=True, stop=True).then_inc(inexact_ps, 1)

            @block.vector
            def _(dve):
                n = Count()
                dve.wait_ge(kv_loaded, 16)
                dve.wait_ge(iotas, 9)
                dve.tensor_copy(kv_f[:, :], kv_i[:, :]).then_inc(p_dve, 1)
                dve.tensor_scalar(kvq_i[:, :], kv_i[:, :], 4, None, ALU.arith_shift_right).then_inc(p_dve, 1)
                dve.tensor_scalar(kvr_i[:, :], kv_i[:, :], 15, None, ALU.bitwise_and).then_inc(p_dve, 1)
                dve.tensor_copy(jcol[:, :], jcol_i[:, :]).then_inc(p_dve, 1)
                dve.tensor_copy(io21[:, :], io21_i[:, :]).then_inc(p_dve, 1)
                dve.tensor_copy(bbase[:, :], bbase_i[:, :]).then_inc(p_dve, 1)
                dve.tensor_copy(jrow[:, :], jrow_i[:, :]).then_inc(p_dve, 1)
                dve.tensor_copy(dump[:, :], dump_i[:, :]).then_inc(p_dve, 1)
                dve.tensor_copy(tpos[:, :], tpos_i[:, :]).then_inc(p_dve, 1)
                dve.tensor_copy(dist[:, :], dist_i[:, :]).then_inc(p_dve, 1)
                n.n = 10
                dve.wait_ge(p_dve, 10)
                dve.tensor_copy(kvq[:, :], kvq_i[:, :]).then_inc(p_dve, 1)
                dve.tensor_copy(kvr[:, :], kvr_i[:, :]).then_inc(p_dve, 1)
                dve.tensor_scalar(thr[:, :], kv_f[:, :], -1.0, float(WINDOW), ALU.mult, ALU.add).then_inc(p_dve, 1)
                dve.tensor_scalar(band[:, :], dist[:, :], 0.0, None, ALU.is_gt).then_inc(p_dve, 1)
                n.n = 14
                dve.wait_ge(p_dve, 14)
                dve.scalar_tensor_tensor(out=band[:, :], in0=dist[:, :], scalar=float(WINDOW), in1=band[:, :],
                                         op0=ALU.is_le, op1=ALU.mult).then_inc(p_dve, 1)
                dve.wait_ge(p_dve, n.next())
                dve.tensor_scalar(band[:, :], band[:, :], -MASKED, MASKED, ALU.mult, ALU.add).then_inc(p_dve, 1)
                dve.wait_ge(p_dve, n.next())
                dve.wait_ge(sparse_loaded, 16 * 5)
                dve.tensor_reduce(eaw_s[:, 0:1], eaw[:, :], AX, ALU.max).then_inc(p_dve, 1)
                dve.wait_ge(p_dve, n.next())
                dve.tensor_scalar(eaw_s[:, 1:2], eaw_s[:, 0:1], -1.0, None, ALU.mult).then_inc(eaw_max, 1)
                dve.tensor_copy(mcol[:, :], mcol_i[:, :]).then_inc(p_dve, 1)
                dve.wait_ge(p_dve, n.next())
                dve.tensor_copy(mrow[:, :, :], mrow_i[:, :, :]).then_inc(p_dve, 1)
                dve.wait_ge(p_dve, n.next())
                dve.tensor_tensor(mrow[:, :, :], mrow[:, :, :], mcol[:, :].unsqueeze(2).to_broadcast([P, SCH, P]),
                                  ALU.is_equal).then_inc(eq_ready, 1)
                dve.wait_ge(eaw_exp, 1)
                dve.reciprocal(eaw_s[:, 3:4], eaw_s[:, 2:3]).then_inc(p_dve, 1)
                dve.wait_ge(p_dve, n.next())
                dve.tensor_scalar(eaw[:, :], eaw[:, :], eaw_s[:, 3:4], None, ALU.mult).then_inc(eaw_norm, 1)
                dve.wait_ge(eq_ready, 1)
                low = mrow_i[:, :, :].bitcast(F32)
                dve.wait_ge(ident_ready, 6)
                dve.tensor_tensor(low, mrow[:, :, :], lowtri[:, :].unsqueeze(1).to_broadcast([P, SCH, P]), ALU.mult).then_inc(p_dve, 1)
                dve.wait_ge(p_dve, n.next())
                dve.wait_ge(eaw_T, 1)
                dve.tensor_copy(eawT[:, :], bk(0)[0:A, 0:E]).then_inc(eaw_Tsb, 1)
                dve.tensor_reduce(earlier[:, :], low, AX, ALU.add).then_inc(p_dve, 1)
                dve.wait_ge(p_dve, n.next())
                dve.tensor_scalar(mhi_i[:, :], mcol_i[:, :], 9, None, ALU.arith_shift_right).then_inc(p_dve, 1)
                dve.tensor_scalar(mlo_i[:, :], mcol_i[:, :], T - 1, None, ALU.bitwise_and).then_inc(p_dve, 1)
                dve.tensor_scalar(earlier[:, :], earlier[:, :], 1.0, None, ALU.min).then_inc(p_dve, 1)
                n.n += 3
                dve.wait_ge(p_dve, n.n)
                dve.tensor_copy(mhi[:, :], mhi_i[:, :]).then_inc(p_dve, 1)
                dve.tensor_copy(mlo[:, :], mlo_i[:, :]).then_inc(p_dve, 1)
                n.n += 2
                dve.wait_ge(p_dve, n.n)
                dve.scalar_tensor_tensor(out=mlo[:, :], in0=mlo[:, :], scalar=float(T), in1=mhi[:, :], op0=ALU.mult, op1=ALU.add).then_inc(p_dve, 1)
                dve.wait_ge(p_dve, n.next())
                dve.tensor_scalar(mhi[:, :], mlo[:, :], -1.0, dump[:, :], ALU.mult, ALU.add).then_inc(p_dve, 1)
                dve.wait_ge(p_dve, n.next())
                dve.tensor_tensor(mhi[:, :], mhi[:, :], earlier[:, :], ALU.mult).then_inc(p_dve, 1)
                dve.wait_ge(p_dve, n.next())
                dve.tensor_tensor(table_idx[:, :], mhi[:, :], mlo[:, :], ALU.add).then_inc(p_dve, 1)
                dve.wait_ge(p_dve, n.next())
                dve.wait_ge(delta_ps, 1)
                dve.wait_ge(sig_ready, 1)
                dve.tensor_tensor(wt[:, :, :], bk(1)[:, 0:SCH * E].rearrange("p (s e) -> p s e", e=E), sig[:, :, :], ALU.mult).then_inc(wt_ready, 1)
                chunks = [w[:, :, :].rearrange("p k n -> p (k n)").bitcast(I32)[:, c * INTER:(c + 1) * INTER]
                          for w in (gate_raw, up_raw, down_raw) for c in range(KT)]
                for c, chunk in enumerate(chunks):
                    if c % KT == 0:
                        dve.wait_ge(ffn_loaded[c // KT], 16)
                    if c == 0:
                        dve.tensor_copy(bits[:, :], chunk).then_inc(p_dve, 1)
                    else:
                        dve.tensor_tensor(bits[:, :], bits[:, :], chunk, ALU.bitwise_or).then_inc(p_dve, 1)
                    dve.wait_ge(p_dve, n.next())
                    if c % KT == KT - 1:
                        dve.sem_inc(bits_seen, 1)
                dve.tensor_scalar(bits[:, :], bits[:, :], (1 << 12) - 1, None, ALU.bitwise_and).then_inc(p_dve, 1)
                dve.wait_ge(p_dve, n.next())
                dve.tensor_reduce(bits_max[:, :], bits[:, :], AX, ALU.max).then_inc(bits_summed, 1)
                dve.wait_ge(consts_loaded, 16 * 5)
                dve.tensor_copy(kvt[:, :], kvt_i[:, :]).then_inc(p_dve, 1)
                dve.wait_ge(p_dve, n.next())
                dve.tensor_scalar(kvt[:, :], kvt[:, :], tpos[:, :], None, ALU.add).then_inc(p_dve, 1)
                dve.wait_ge(p_dve, n.next())
                dve.tensor_tensor(ang[:, :, :], kvt[:, :].unsqueeze(2).to_broadcast([P, PAIRS, HALF]),
                                  inv[:, :].unsqueeze(1).to_broadcast([P, PAIRS, HALF]), ALU.mult).then_inc(p_dve, 1)
                dve.wait_ge(p_dve, n.next())
                dve.tensor_scalar(turns[:, :, :], ang[:, :, :], float(1 / TWO_PI), MAGIC, ALU.mult, ALU.add).then_inc(p_dve, 1)
                dve.wait_ge(p_dve, n.next())
                dve.tensor_scalar(turns[:, :, :], turns[:, :, :], MAGIC, None, ALU.subtract).then_inc(p_dve, 1)
                dve.wait_ge(p_dve, n.next())
                for part in (C1, C2, C3):
                    dve.scalar_tensor_tensor(out=ang[:, :, :], in0=turns[:, :, :], scalar=-part, in1=ang[:, :, :],
                                             op0=ALU.mult, op1=ALU.add).then_inc(p_dve, 1)
                    dve.wait_ge(p_dve, n.next())
                dve.tensor_scalar(ang[:, :, :], ang[:, :, :], PI_IN, -PI_IN, ALU.min, ALU.max).then_inc(sin_arg, 1)
                dve.wait_ge(sin_arg, 1)
                dve.scalar_tensor_tensor(out=turns[:, :, :], in0=ang[:, :, :], scalar=-1.0, in1=ang[:, :, :],
                                         op0=ALU.mult, op1=ALU.max).then_inc(p_dve, 1)
                dve.wait_ge(p_dve, n.next())
                dve.tensor_scalar(turns[:, :, :], turns[:, :, :], -1.0, float(np.pi / 2), ALU.mult, ALU.add).then_inc(sin_arg, 1)
                dve.tensor_scalar(nscale[:, 0:H, :], qn[:, 0:1, :].to_broadcast([P, H, HD]), 1.0, None, ALU.add).then_inc(p_dve, 1)
                dve.tensor_scalar(nscale[:, H:NQK, :], qn[:, 1:2, :].to_broadcast([P, G, HD]), 1.0, None, ALU.add).then_inc(p_dve, 1)
                n.n += 2
                dve.wait_ge(tot_ps, 1)
                dve.wait_ge(inexact_ps, 1)
                dve.tensor_scalar(inexact[:, :], bk(3)[0:1, 0:1], 1.0, None, ALU.min).then_inc(p_dve, 1)
                n.n += 1
                dve.tensor_copy(tot[:, :, :], bk(2)[:, 0:SCH * E].rearrange("p (s e) -> p s e", e=E)).then_inc(p_dve, 1)
                dve.wait_ge(p_dve, n.next())
                for loaded in tables_loaded:
                    dve.wait_ge(loaded, 16 * B // 2)

        WEIGHTS = 16 * 5
        xr_loaded = sem("xr_loaded")
        proj_ps = sem("proj_ps")
        h_hi = sem("h_hi")
        h_ready = sem("h_ready")
        gu_ps = sem("gu_ps")
        silu_ready = sem("silu_ready")
        hdn_ready = sem("hdn_ready")
        hdn_hi_ready = sem("hdn_hi_ready")
        hdn_split = sem("hdn_split")
        down_ps = sem("down_ps")
        DOWNS = IT - 1 + TPG
        weights_reloaded = sem("weights_reloaded")
        res_ready = sem("res_ready")
        x1T_ps = sem("x1T_ps")
        x1T_ready = sem("x1T_ready")
        x1_stored = [sem(f"x1_stored{k}") for k in range(2)]
        qkv_ps = sem("qkv_ps")
        qkv_sq = sem("qkv_sq")
        qkv_copied = sem("qkv_copied")
        std_arg = sem("std_arg")
        std_ready = sem("std_ready")
        qk_ready = sem("qk_ready")
        q_stored = [sem(f"q_stored{k}") for k in range(2)]
        kv_stored = [sem(f"kv_stored{k}") for k in range(2)]
        d0 = sem("d0")
        own_gate = sem("own_gate")
        OWN = GCOLS // KCOLS
        OWN_STEPS = 5 + 7 * OWN
        DSTEPS = 52 + OWN_STEPS
        index_step = sem("index_step")

        def each_group(eng, group):
            with eng.Fori(0, GROUPS - 1) as g:
                group(g, False)
            group(GROUPS - 1, True)
        slot_ready = sem("slot_ready")
        entry_added = sem("entry_added")
        slot_taken = sem("slot_taken")

        with nc.Block() as block:
            @block.sync
            def _(sp):
                with sp.If(sp.value_load(inexact[0:1, 0:1], min_val=0, max_val=1) == 1):
                    for to, src in ((gate_raw, gate_t), (up_raw, up_t), (down_raw, down_t)):
                        sp.dma_start(to[:, :, :], src.rearrange("(k p) n -> p k n", p=P)).then_inc(weights_reloaded, 16)
                    sp.wait_ge(weights_reloaded, 16 * 3)
                sp.wait_ge(weights_loaded, WEIGHTS)

                def load_xr(g):
                    sp.dma_start(xr[:, :, :], x[bass.ds(g * GT, GT), :].rearrange("(k p) t -> p k t", p=P)).then_inc(xr_loaded, 16)

                def group(g, last):
                    def store_x1(j):
                        sp.wait_ge(res_ready, g * TPG + j + 1)
                        sp.dma_start(x1_dram[bass.ds(g * GT + j * P, P), :], x1[:, j % 2, :]).then_inc(x1_stored[j % 2], 16)

                    def store_qkv(j):
                        sp.wait_ge(qk_ready, g * TPG + j + 3)
                        sp.dma_start(q_dram[bass.ds(g * GT + j * P, P), :], q_out[:, j % 2, :]).then_inc(q_stored[j % 2], 16)
                        sp.dma_start(kv_dram[bass.ds(g * GT + j * P, P), :], kv_out[:, j % 2, :]).then_inc(kv_stored[j % 2], 16)

                    if not last:
                        sp.wait_ge(proj_ps, g * KT + KT)
                        load_x(sp, g + 1)
                    store_x1(0)
                    store_x1(1)
                    store_x1(2)
                    store_qkv(0)
                    store_x1(3)
                    if not last:
                        load_xr(g + 1)
                    for j in range(1, TPG):
                        store_qkv(j)

                load_xr(0)
                each_group(sp, group)
                for s in x1_stored + q_stored + kv_stored:
                    sp.wait_ge(s, 16 * (GROUPS * TPG // 2) + 16)

            @block.tensor
            def _(pe):
                pe.wait_ge(weights_loaded, WEIGHTS)

                def project(g):
                    pe.wait_ge(xc_loaded, g * 16 + 16)
                    pe.wait_ge(cw_loaded, g * (16 * SPG) + 16 * SPG)
                    for k in range(KT):
                        for j in range(TPG):
                            mm = pe.matmul(bk(k)[:, j * P:(j + 1) * P], xc[:, j, k * P:(k + 1) * P], cw[:, j, :],
                                           start=True, stop=True)
                        mm.then_inc(proj_ps, 1)

                def all_groups(form):
                    gate, up, down_rows = (gate_w, up_w, down_w) if form == F32R else (gate_raw, up_raw, down_raw)

                    def group(g, last):
                        def gate_up(i):
                            if i < 2:
                                pe.wait_ge(qkv_copied, g * TPG + i + 1)
                            else:
                                pe.wait_ge(hdn_ready, g * IT + i - 1)
                            if i == 0:
                                pe.wait_ge(h_ready, g * KT + KT)
                            for w, half in ((gate, 0), (up, 1)):
                                for k in range(KT):
                                    for n, part in enumerate((hT_hi, hT_lo)):
                                        mm = pe.matmul(bk(2 * (i % 2) + half), w[:, k, i * P:(i + 1) * P],
                                                       part[:, k, :].bitcast(form), start=(k == 0 and n == 0), stop=(k == KT - 1 and n == 1))
                            mm.then_inc(gu_ps, 1)

                        def down(i):
                            pe.wait_ge(hdn_split, g * IT + i + 1)
                            if i == 0:
                                pe.wait_ge(x1T_ready, g * TPG + 1)
                            for j in range(TPG):
                                for n, part in enumerate((hdn_hi, hdn_lo)):
                                    mm = pe.matmul(bk(4 + j), part[:, i % 3, j * P:(j + 1) * P].bitcast(form),
                                                   down_rows[:, i, :], start=(i == 0 and n == 0), stop=(i == IT - 1 and n == 1))
                                if i == IT - 1 or j == TPG - 1:
                                    mm.then_inc(down_ps, 1)

                        def turn(j):
                            pe.wait_ge(res_ready, g * TPG + j + 1)
                            for k in range(KT):
                                mm = pe.transpose(bk(4 + j)[:, k * P:(k + 1) * P], x1[:, j % 2, k * P:(k + 1) * P], ident[:, :])
                            mm.then_inc(x1T_ps, 1)

                        def qkv(j):
                            pe.wait_ge(x1T_ready, g * TPG + j + 2)
                            if j >= 2:
                                pe.wait_ge(qkv_copied, g * TPG + j + 1)
                            elif not last:
                                pe.wait_ge(h_ready, (g + 1) * KT + 2 * j + 2)
                            for half in range(2):
                                for k in range(KT):
                                    mm = pe.matmul(bk(2 * (j % 2) + half), x1T[:, k, j * P:(j + 1) * P], wqkv[:, k, half * T:(half + 1) * T],
                                                   start=(k == 0), stop=(k == KT - 1))
                            mm.then_inc(qkv_ps, 1)

                        for i in range(IT):
                            gate_up(i)
                            if i >= 2:
                                down(i - 2)
                        down(IT - 2)
                        down(IT - 1)
                        if not last:
                            project(g + 1)
                        turn(0)
                        turn(1)
                        qkv(0)
                        turn(2)
                        qkv(1)
                        turn(3)
                        qkv(2)
                        qkv(3)

                    each_group(pe, group)

                project(0)
                general = pe.value_load(inexact[0:1, 0:1], min_val=0, max_val=1)
                with pe.If(general == 0):
                    all_groups(F32R)
                with pe.Else():
                    pe.wait_ge(weights_reloaded, 16 * 3)
                    all_groups(F32)

            @block.scalar
            def _(act):
                act.sem_inc(x1T_ready, 1)
                act.sem_inc(qkv_copied, 2)

                def high_h(g, k):
                    act.wait_ge(proj_ps, g * KT + k + 1)
                    act.activation(hT_hi[:, k, :].bitcast(F32R), bk(k), ACT.Copy).then_inc(h_hi, 1)

                def group(g, last):
                    def high_hdn(i):
                        act.wait_ge(hdn_ready, g * IT + i + 1)
                        if i >= 3:
                            act.wait_ge(down_ps, g * DOWNS + i - 2)
                        act.activation(hdn_hi[:, i % 3, :].bitcast(F32R), hdn[:, i % 2, :], ACT.Copy).then_inc(hdn_hi_ready, 1)

                    for i in range(IT):
                        act.wait_ge(gu_ps, g * IT + i + 1)
                        act.activation(silu[:, i % 2, :], bk(2 * (i % 2)), ACT.Silu, scale=gs[:, i:i + 1]).then_inc(silu_ready, 1)
                        if i >= 1:
                            high_hdn(i - 1)
                    high_hdn(IT - 1)

                    def x1T_copy(j):
                        act.wait_ge(x1T_ps, g * TPG + j + 1)
                        act.activation(x1T[:, :, j * P:(j + 1) * P], bk(4 + j).rearrange("p (k n) -> p k n", n=P), ACT.Copy).then_inc(x1T_ready, 1)

                    def qkv_copy(j):
                        act.wait_ge(qkv_ps, g * TPG + j + 1)
                        act.wait_ge(qk_ready, g * TPG + j + 1)
                        act.wait_ge(kv_stored[j % 2], g * 32 + 16 * (j // 2) + 16)
                        act.activation(sq[:, :], bank[j % 2][:, :, :].rearrange("p a n -> p (a n)")[:, 0:NQK * HD], ACT.Square).then_inc(qkv_sq, 1)
                        act.activation(raw[:, j % 2, :], bank[j % 2][:, :, :].rearrange("p a n -> p (a n)")[:, 0:NQK * HD], ACT.Copy)
                        act.activation(kv_out[:, j % 2, G * HD:], bk(2 * (j % 2) + 1)[:, G * HD:], ACT.Copy).then_inc(qkv_copied, 1)

                    def roots(j):
                        act.wait_ge(std_arg, g * TPG + j + 1)
                        act.activation(ssum[:, 2, :], ssum[:, 1, :], ACT.Sqrt).then_inc(std_ready, 1)

                    if not last:
                        high_h(g + 1, 0)
                        high_h(g + 1, 1)
                    x1T_copy(0)
                    if not last:
                        high_h(g + 1, 2)
                        high_h(g + 1, 3)
                    x1T_copy(1)
                    qkv_copy(0)
                    x1T_copy(2)
                    roots(0)
                    qkv_copy(1)
                    x1T_copy(3)
                    roots(1)
                    for j in (2, 3):
                        qkv_copy(j)
                        roots(j)

                for k in range(KT):
                    high_h(0, k)
                each_group(act, group)

            @block.vector
            def _(dve):
                dve.sem_inc(qk_ready, 2)
                for s in x1_stored + q_stored + kv_stored:
                    dve.sem_inc(s, 16)
                dve.wait_ge(weights_loaded, WEIGHTS)

                m = Count()

                def istep(*ins):
                    for one in ins:
                        one.then_inc(index_step, 1)
                        m.next()
                    dve.wait_ge(index_step, m.n)

                def look_up(to, which):
                    istep(dve.tensor_tensor(oh[:, :, :], which.unsqueeze(2).to_broadcast([P, B, SLOTS]),
                                            io21[:, :].unsqueeze(1).to_broadcast([P, B, SLOTS]), ALU.is_equal))
                    istep(dve.tensor_tensor(oh[:, :, :], oh[:, :, :], tb_f[:, :, :], ALU.mult))
                    istep(dve.tensor_reduce(to, oh[:, :, :], AX, ALU.add))

                def slot_places():
                    istep(dve.tensor_scalar(slot0[:, :], kvq[:, :], float(WINDOW // BLOCK), 0.0, ALU.subtract, ALU.max),
                          dve.tensor_tensor(posk_i[:, :, :], kv_f[:, :].unsqueeze(2).to_broadcast([P, B, NCH]),
                                            jcol[:, :].unsqueeze(1).to_broadcast([P, B, NCH]), ALU.add))
                    istep(dve.tensor_scalar(posk_i[:, :, :], posk_i[:, :, :], 0.0, None, ALU.max))
                    istep(dve.tensor_scalar(slot_i[:, :, :], posk_i[:, :, :], 4, None, ALU.arith_shift_right),
                          dve.tensor_scalar(off_i[:, :, :], posk_i[:, :, :], 15, None, ALU.bitwise_and))
                    istep(dve.tensor_copy(rel[:, :, :], slot_i[:, :, :]),
                          dve.tensor_copy(off_f[:, :, :], off_i[:, :, :]),
                          dve.tensor_copy(tb_f[:, :, :], tb_i[:, :, :]))
                    istep(dve.tensor_tensor(rel[:, :, :], rel[:, :, :], slot0[:, :].unsqueeze(2).to_broadcast([P, B, NCH]), ALU.subtract))

                def slot_rows():
                    istep(dve.scalar_tensor_tensor(out=key_addr[:, :].rearrange("p (b c) -> p b c", c=NCH), in0=kblk[:, :, :],
                                                   scalar=float(BLOCK), in1=off_f[:, :, :], op0=ALU.mult, op1=ALU.add))

                def segment(i):
                    istep(dve.scalar_tensor_tensor(out=seg_rel[:, :], in0=kvq[:, :], scalar=float(i), in1=slot0[:, :],
                                                   op0=ALU.add, op1=ALU.subtract),
                          dve.tensor_scalar(seg_t[:, :, i], kvr[:, :], -1.0, float(BLOCK * i), ALU.mult, ALU.add),
                          dve.tensor_scalar(seg_hi[:, :, i], kvr[:, :], -1.0, float(BLOCK * (i + 1)), ALU.mult, ALU.add))
                    look_up(seg_start[:, :, i], seg_rel[:, :])

                def segment_rows():
                    istep(dve.tensor_scalar(seg_t[:, :, :], seg_t[:, :, :], 0.0, None, ALU.max),
                          dve.tensor_scalar(seg_hi[:, :, :], seg_hi[:, :, :], float(C), None, ALU.min),
                          dve.tensor_scalar(seg_start[:, :, :], seg_start[:, :, :], float(BLOCK), None, ALU.mult))
                    number = bbase[:, :].unsqueeze(2).to_broadcast([P, B, SEG])
                    istep(dve.tensor_tensor(seg_lo[:, :, :], seg_t[:, :, :], number, ALU.add),
                          dve.tensor_tensor(seg_len[:, :, :], seg_hi[:, :, :], seg_t[:, :, :], ALU.subtract),
                          dve.tensor_tensor(seg_start[:, :, 0], seg_start[:, :, 0], kvr[:, :], ALU.add))
                    istep(dve.scalar_tensor_tensor(out=seg_key[:, :, :], in0=seg_lo[:, :, :], scalar=KEY, in1=seg_start[:, :, :],
                                                   op0=ALU.add, op1=ALU.subtract))

                def index_work(i):
                    if i == 1:
                        slot_places()
                    elif 2 <= i < 2 + NCH:
                        look_up(kblk[:, :, i - 2], rel[:, :, i - 2])
                    elif i >= 2 + NCH and i - 2 - NCH < SEG:
                        if i == 2 + NCH:
                            slot_rows()
                        segment(i - 2 - NCH)
                    elif i == IT - 1:
                        segment_rows()

                def low_h(g, k):
                    dve.wait_ge(h_hi, g * KT + k + 1)
                    dve.tensor_tensor(hT_lo[:, k, :].bitcast(F32R), bk(k), hT_hi[:, k, :], ALU.subtract).then_inc(h_ready, 1)

                def group(g, last, first=False):
                    n = Count()

                    def owners(c):
                        full = [P, KCOLS, NSEG]
                        flat = lambda t: t[:, :, :].rearrange("p b i -> p (b i)")
                        wide = lambda t: flat(t).unsqueeze(1).to_broadcast(full)
                        addr = key_addr[:, bass.ds((g - 1) * GCOLS + c * KCOLS, KCOLS)]
                        if c >= 1:
                            dve.wait_ge(d0, g * DSTEPS + n.n)
                        dve.tensor_tensor(own_v[:, :, :], addr.unsqueeze(2).to_broadcast(full), wide(seg_start), ALU.subtract).then_inc(d0, 1)
                        dve.wait_ge(d0, g * DSTEPS + n.next())
                        dve.tensor_tensor(own_m[:, :, :], own_v[:, :, :], wide(seg_len), ALU.is_lt).then_inc(d0, 1)
                        dve.wait_ge(d0, g * DSTEPS + n.next())
                        dve.scalar_tensor_tensor(out=own_m[:, :, :], in0=own_v[:, :, :], scalar=0.0, in1=own_m[:, :, :],
                                                 op0=ALU.is_ge, op1=ALU.mult).then_inc(d0, 1)
                        dve.wait_ge(d0, g * DSTEPS + n.next())
                        dve.sem_inc(own_gate, 1)
                        for k in range(KCOLS):
                            at = c * KCOLS + k
                            dve.tensor_tensor_reduce(own_v[:, k, :], own_m[:, k, :], flat(seg_key), 1.0, 0.0, ALU.mult, ALU.max,
                                                     found[:, at:at + 1]).then_inc(d0, 1)
                            n.next()

                    def own_rows():
                        cols = bass.ds((g - 1) * GCOLS, GCOLS)
                        addr = key_addr[:, cols]
                        dve.wait_ge(d0, g * DSTEPS + n.n)
                        dve.tensor_scalar(owned[:, :], found[:, :], 0.0, SKIP, ALU.is_gt, ALU.mult).then_inc(d0, 1)
                        dve.wait_ge(d0, g * DSTEPS + n.next())
                        dve.tensor_tensor(own_cache[:, cols], owned[:, :], addr, ALU.add).then_inc(d0, 1)
                        dve.tensor_scalar(found[:, :], found[:, :], SKIP - KEY - 1.0, None, ALU.add).then_inc(d0, 1)
                        n.next()
                        dve.wait_ge(d0, g * DSTEPS + n.next())
                        dve.tensor_tensor(found[:, :], found[:, :], owned[:, :], ALU.subtract).then_inc(d0, 1)
                        dve.wait_ge(d0, g * DSTEPS + n.next())
                        dve.tensor_tensor(own_new[:, cols], found[:, :], addr, ALU.add).then_inc(d0, 1)
                        dve.wait_ge(d0, g * DSTEPS + n.next())

                    def low_hdn(i):
                        dve.wait_ge(hdn_hi_ready, g * IT + i + 1)
                        dve.tensor_tensor(hdn_lo[:, i % 3, :].bitcast(F32R), hdn[:, i % 2, :], hdn_hi[:, i % 3, :],
                                          ALU.subtract).then_inc(hdn_split, 1)

                    for i in range(IT):
                        dve.wait_ge(silu_ready, g * IT + i + 1)
                        if i >= 2:
                            dve.wait_ge(hdn_split, g * IT + i - 1)
                        dve.scalar_tensor_tensor(out=hdn[:, i % 2, :], in0=bk(2 * (i % 2) + 1), scalar=us[:, i:i + 1], in1=silu[:, i % 2, :],
                                                 op0=ALU.mult, op1=ALU.mult).then_inc(hdn_ready, 1)
                        if i >= 1:
                            low_hdn(i - 1)
                        if first:
                            index_work(i)
                        elif 1 <= i <= OWN:
                            owners(i - 1)
                        elif i == OWN + 1:
                            own_rows()
                    low_hdn(IT - 1)

                    def residual(j):
                        dve.wait_ge(down_ps, g * DOWNS + IT + j)
                        if j == 0:
                            dve.wait_ge(xr_loaded, g * 16 + 16)
                        dve.wait_ge(x1_stored[j % 2], g * 32 + 16 * (j // 2) + 16)
                        if j >= 2:
                            dve.wait_ge(x1T_ps, g * TPG + j - 1)
                        dve.tensor_tensor(x1[:, j % 2, :], bk(4 + j), dscale[:, :], ALU.mult).then_inc(d0, 1)
                        dve.wait_ge(d0, g * DSTEPS + n.next())
                        dve.tensor_tensor(x1[:, j % 2, :], x1[:, j % 2, :], xr[:, j, :], ALU.add).then_inc(res_ready, 1)

                    def rotate(j):
                        heads = raw[:, j % 2, :].rearrange("p (h d) -> p h d", d=HD)
                        wide = [P, NQK, HALF]
                        tile_cos = cos[:, bass.ds(g * TPG + j, 1), :].to_broadcast(wide)
                        tile_sin = sin[:, bass.ds(g * TPG + j, 1), :].to_broadcast(wide)
                        dve.wait_ge(qkv_sq, g * TPG + j + 1)
                        dve.tensor_reduce(ssum[:, 0, :], sq[:, :].rearrange("p (h d) -> p h d", d=HD), AX, ALU.add).then_inc(d0, 1)
                        dve.wait_ge(d0, g * DSTEPS + n.next())
                        dve.tensor_scalar(ssum[:, 1, :], ssum[:, 0, :], 1.0 / HD, EPS, ALU.mult, ALU.add).then_inc(std_arg, 1)
                        dve.wait_ge(qkv_copied, g * TPG + j + 3)
                        dve.tensor_tensor(heads, heads, nscale[:, :, :], ALU.mult).then_inc(d0, 1)
                        dve.wait_ge(d0, g * DSTEPS + n.next())
                        dve.wait_ge(std_ready, g * TPG + j + 1)
                        dve.reciprocal(ssum[:, 0, :], ssum[:, 2, :]).then_inc(d0, 1)
                        dve.wait_ge(d0, g * DSTEPS + n.next())
                        dve.tensor_tensor(heads, heads, ssum[:, 0, :].unsqueeze(2).to_broadcast([P, NQK, HD]), ALU.mult).then_inc(d0, 1)
                        dve.wait_ge(d0, g * DSTEPS + n.next())
                        x_lo, x_hi = heads[:, :, 0:HALF], heads[:, :, HALF:HD]
                        dve.wait_ge(q_stored[j % 2], g * 32 + 16 * (j // 2) + 16)
                        dve.wait_ge(kv_stored[j % 2], g * 32 + 16 * (j // 2) + 16)
                        for part, (first, second, op) in enumerate(((x_lo, x_hi, ALU.subtract), (x_hi, x_lo, ALU.add))):
                            dve.tensor_tensor(rot_a[:, :, :], first, tile_cos, ALU.mult).then_inc(d0, 1)
                            dve.tensor_tensor(rot_b[:, :, :], second, tile_sin, ALU.mult).then_inc(d0, 1)
                            n.next()
                            dve.wait_ge(d0, g * DSTEPS + n.next())
                            at = slice(part * HALF, (part + 1) * HALF)
                            dve.tensor_tensor(q_out[:, j % 2, :].rearrange("p (h d) -> p h d", d=HD)[:, :, at],
                                              rot_a[:, 0:H, :], rot_b[:, 0:H, :], op).then_inc(d0, 1)
                            last = dve.tensor_tensor(kv_out[:, j % 2, 0:G * HD].rearrange("p (h d) -> p h d", d=HD)[:, :, at],
                                                     rot_a[:, H:NQK, :], rot_b[:, H:NQK, :], op)
                            last.then_inc(d0, 1)
                            n.next()
                            dve.wait_ge(d0, g * DSTEPS + n.next())
                        dve.sem_inc(qk_ready, 1)

                    residual(0)
                    residual(1)
                    if not last:
                        for k in range(KT):
                            low_h(g + 1, k)
                    residual(2)
                    rotate(0)
                    residual(3)
                    rotate(1)
                    rotate(2)
                    rotate(3)
                    assert n.n == DSTEPS - (OWN_STEPS if first else 0), n.n
                    if first:
                        dve.sem_inc(d0, OWN_STEPS)

                for k in range(KT):
                    low_h(0, k)
                group(0, False, first=True)
                with dve.Fori(1, GROUPS - 1) as g:
                    group(g, False)
                group(GROUPS - 1, True)

            @block.gpsimd
            def _(pool):
                Q = T // RCOLS
                for c in range(KT):
                    for h in range(Q):
                        if Q * c + h >= 1:
                            pool.wait_ge(table_init, 16 * (Q * c + h))
                        part = wT_sb[:, c, h * RCOLS:(h + 1) * RCOLS]
                        pool.tensor_copy(wexp[:, :, :], part.unsqueeze(2).to_broadcast([P, RCOLS, E])).then_inc(wexp_full, 1)
                        pool.wait_ge(wexp_full, Q * c + h + 1)
                        pool.dma_start(table_dram[c * P * T:(c + 1) * P * T, :].rearrange("(p h r) e -> p h (r e)", p=P, h=Q)[:, h, :],
                                       wexp[:, :, :].rearrange("p r e -> p (r e)")).then_inc(table_init, 16)
                pool.dma_start(table_dram[TBL:TBL + P, :], zero8[:, :]).then_inc(table_init, 16)
                pool.wait_ge(table_init, TABLE_INIT)
                with pool.Fori(0, SCH) as s:
                    pool.tensor_copy(slot_idx[:, :], table_idx[:, bass.ds(s, 1)]).then_inc(slot_ready, 1)
                    pool.tensor_copy(slot_val[:, :], tot[:, bass.ds(s, 1), :].rearrange("p a e -> p (a e)")).then_inc(slot_ready, 1)
                    pool.wait_ge(slot_ready, s * 2 + 2)
                    pool.sem_inc(slot_taken, 1)
                    pool.indirect_dma_start(table_dram, bass.IndirectOffsetOnAxis(slot_idx[:, 0:1], 0), slot_val[:, :], None,
                                            compute_op=ALU.add).then_inc(entry_added, 16)
                    pool.wait_ge(entry_added, s * 16 + 16)


        wo_loaded = sem("wo_loaded")
        piece_loaded = [sem(f"piece_loaded{r}") for r in range(2)]
        piece_hi = sem("piece_hi")
        experts_ready = sem("experts_ready")
        idx_copied = sem("idx_copied")
        idx_taken = sem("idx_taken")
        kv_gathered = [sem(f"kv_gathered{u}") for u in range(2)]
        q_loaded = [sem(f"q_loaded{u}") for u in range(2)]
        acc_loaded = [sem(f"acc_loaded{u}") for u in range(2)]
        out_stored = [sem(f"out_stored{u}") for u in range(2)]
        kT_ps = sem("kT_ps")
        kT_ready = sem("kT_ready")
        qT_ps = sem("qT_ps")
        qT_ready = sem("qT_ready")
        mask_ready = sem("mask_ready")
        score_ps = sem("score_ps")
        score_taken = sem("score_taken")
        sm_ready = sem("sm_ready")
        nmx_ready = sem("nmx_ready")
        prob_ready = sem("prob_ready")
        pT_ps = sem("pT_ps")
        pT_ready = sem("pT_ready")
        o_ps = sem("o_ps")
        o_ready = sem("o_ready")
        oT_ps = sem("oT_ps")
        oT_ready = sem("oT_ready")
        yT_ps = sem("yT_ps")
        yT_ready = sem("yT_ready")
        lg_ps = sem("lg_ps")
        lg_read = sem("lg_read")
        lg_negmax = sem("lg_negmax")
        lg_exp = sem("lg_exp")
        rw_ready = sem("rw_ready")
        mix_ps = sem("mix_ps")
        mix_done = sem("mix_done")
        mask_step = sem("mask_step")
        rinv_step = sem("rinv_step")
        route_step = sem("route_step")
        ROUTE_STEPS = 11
        GATHERS = 16 * (4 + 2 * NCH)

        def each_pair(eng, pair):
            pair(0, 0, None, (1, 1, 0))
            with eng.Fori(0, PAIRS // 2 - 1) as i:
                pair(i * 2 + 1, 1, i * 2, (i * 2 + 2, 0, i + 1))
                pair(i * 2 + 2, 0, i * 2 + 1, (i * 2 + 3, 1, i + 1))
            pair(PAIRS - 1, 1, PAIRS - 2, None)

        with nc.Block() as block:
            @block.sync
            def _(sp):
                sp.dma_start(wo[:, :, :], wo_t.rearrange("(k p) n -> p k n", p=P)).then_inc(wo_loaded, 16)

                sp.dma_start(q_t[:, 0, :], q_dram[0:P, :]).then_inc(q_loaded[0], 16)
                for k in range(KT):
                    for r in range(PIECES):
                        if k * PIECES + r >= 2:
                            sp.wait_ge(experts_ready, k * PIECES + r - 1)
                        sp.dma_start(stage[:, r % 2, :, :], table_dram[k * P * T:(k + 1) * P * T, :].rearrange(
                            "(p r) e -> p r e", p=P)[:, r * PIECE:(r + 1) * PIECE, :]).then_inc(piece_loaded[r % 2], 16)
                sp.dma_start(acc[:, 0, :], x1_dram[0:P, :]).then_inc(acc_loaded[0], 16)
                sp.dma_start(q_t[:, 1, :], q_dram[P:2 * P, :]).then_inc(q_loaded[1], 16)
                sp.dma_start(acc[:, 1, :], x1_dram[P:2 * P, :]).then_inc(acc_loaded[1], 16)
                with sp.Fori(1, PAIRS // 2) as i:
                    for u in range(2):
                        sp.wait_ge(qT_ps, i * 2 + (u + 1))
                        sp.dma_start(q_t[:, u, :], q_dram[bass.ds(i * (2 * P) + u * P, P), :]).then_inc(q_loaded[u], 16)
                        sp.wait_ge(out_stored[u], i * 16 + 16)
                        sp.dma_start(acc[:, u, :], x1_dram[bass.ds(i * (2 * P) + u * P, P), :]).then_inc(acc_loaded[u], 16)

            @block.gpsimd
            def _(pool):
                with pool.Fori(0, PAIRS // 2) as i:
                    for u in range(2):
                        cols = bass.ds(i * (4 * NCH) + u * (2 * NCH), 2 * NCH)
                        pool.tensor_copy(idx_c[u][:, :], own_cache[:, cols]).then_inc(idx_copied, 1)
                        pool.tensor_copy(idx_n[u][:, :], own_new[:, cols]).then_inc(idx_copied, 1)
                        pool.wait_ge(idx_copied, i * 4 + (2 * u + 2))
                        pool.sem_inc(idx_taken, 1)
                        pool.wait_ge(o_ps, i * 4 + (2 * u + 2))
                        pool.sem_inc(idx_taken, 1)
                        for b in range(2):
                            for c in range(2):
                                pool.indirect_dma_start(kv_t[u][b][:, c, :], None, kv_cache,
                                                        bass.IndirectOffsetOnAxis(idx_c[u][:, b * NCH + c:b * NCH + c + 1], 0),
                                                        bounds_check=POOL_ROWS - 1, oob_is_err=False).then_inc(kv_gathered[u], 16)
                        pool.wait_ge(kv_gathered[u], i * GATHERS + 16 * 4)
                        pool.sem_inc(idx_taken, 1)
                        for b in range(2):
                            for c, rows in enumerate(KCH):
                                pool.indirect_dma_start(kv_t[u][b][0:rows, c, :], None, kv_dram,
                                                        bass.IndirectOffsetOnAxis(idx_n[u][0:rows, b * NCH + c:b * NCH + c + 1], 0),
                                                        bounds_check=TOK - 1, oob_is_err=False).then_inc(kv_gathered[u], 16)
                        pool.wait_ge(kv_gathered[u], i * GATHERS + GATHERS)
                        pool.sem_inc(idx_taken, 1)

            @block.tensor
            def _(pe):
                pe.sem_inc(o_ps, 4)
                pe.sem_inc(qT_ps, 2)

                def mix_expert(m, e):
                    pe.wait_ge(mix_done, m * E + (e + 1))
                    for k in range(KT):
                        for n, (y, w) in enumerate(((yT_hi, experts_hi), (yT_hi, experts_lo), (yT_lo, experts_hi))):
                            mm = pe.matmul(bk(5 + 2 * (e % 2)), y[:, k, :].bitcast(F32R), w[:, k, e, :].bitcast(F32R),
                                           start=(k == 0 and n == 0), stop=(k == KT - 1 and n == 2))
                    mm.then_inc(mix_ps, 1)

                def turn_k(pr, b):
                    p, u, use = pr
                    for gp in range(2):
                        for c, rows in enumerate(KCH):
                            mm = pe.transpose(bk(5 + 2 * gp)[:, c * P:c * P + rows], kv_t[u][b][0:rows, c, gp * P:(gp + 1) * P],
                                              ident[0:rows, 0:rows])
                    mm.then_inc(kT_ps, 1)

                def turn_q(pr):
                    p, u, use = pr
                    pe.wait_ge(q_loaded[u], use * 16 + 16)
                    for k in range(KT):
                        mm = pe.transpose(bk(6)[:, k * P:(k + 1) * P], q_t[:, u, k * P:(k + 1) * P], ident[:, :])
                    mm.then_inc(qT_ps, 1)

                def pair(p, u, mix, nxt):
                    def score(s):
                        b, gp, g = s // 4, s // 2 % 2, s % 2
                        rows = slice(g * HD, (g + 1) * HD)
                        if s == 0:
                            pe.wait_ge(qT_ready, p * 2 + 2)
                            pe.wait_ge(kT_ready, p * 4 + 4)
                        pe.wait_ge(sm_ready, p * 8 + (s + 1))
                        pe.matmul(bk(s % 2)[:, 0:KEYS], qT[rows, gp, b, :, :].rearrange("p h t -> p (h t)"), kT[rows, b, gp, :],
                                  start=True, stop=True).then_inc(score_ps, 1)

                    score(0)
                    for s in range(8):
                        if s < 7:
                            score(s + 1)
                        if s == 0:
                            pe.wait_ge(lg_read, p + 1)
                        pe.wait_ge(prob_ready, p * 8 + (s + 3))
                        for c, rows in enumerate(KCH):
                            mm = pe.transpose(bk(4)[0:rows, c * P:(c + 1) * P], prob[:, s % 2, c * P:c * P + rows], ident[:, :])
                        mm.then_inc(pT_ps, 1)
                        if mix is not None:
                            mix_expert(mix, s)
                        pe.wait_ge(pT_ready, p * 8 + (s + 1))
                        b, g = s // 4, s % 4
                        for c, rows in enumerate(KCH):
                            mm = pe.matmul(bk(2 if b else 6)[:, g * HD:(g + 1) * HD], pT[0:rows, s % 2, c, :],
                                           kv_t[u][b][0:rows, c, (G + g) * HD:(G + g + 1) * HD], start=(c == 0), stop=(c == NCH - 1))
                        if g == 3:
                            mm.then_inc(o_ps, 1)
                    if nxt is not None:
                        pe.wait_ge(kv_gathered[nxt[1]], nxt[2] * GATHERS + GATHERS)
                        if mix is not None:
                            pe.wait_ge(mix_done, mix * E + (E + 2))
                        turn_k(nxt, 0)
                    pe.wait_ge(o_ready, p * 2 + 2)
                    for b in range(2):
                        for gp in range(2):
                            at = (2 * b + gp) * P
                            mm = pe.transpose(bk(3)[:, at:at + P], o_sb[:, b, gp * P:(gp + 1) * P], ident[:, :])
                    mm.then_inc(oT_ps, 1)
                    if nxt is not None:
                        turn_q(nxt)
                    if mix is None:
                        pe.wait_ge(wo_loaded, 16)
                    pe.wait_ge(oT_ready, p + 1)
                    for d in range(KT):
                        for k in range(KT):
                            mm = pe.matmul(bk(2)[:, d * P:(d + 1) * P], wo[:, k, d * P:(d + 1) * P],
                                           oT[:, :, k // 2, k % 2, :], start=(k == 0), stop=(k == KT - 1))
                    mm.then_inc(yT_ps, 1)
                    if nxt is not None:
                        pe.wait_ge(kT_ready, p * 4 + 6)
                        turn_k(nxt, 1)
                    for half, y in enumerate((yT_hi, yT_lo)):
                        pe.wait_ge(yT_ready, p * 2 + (half + 1))
                        for k in range(KT):
                            mm = pe.matmul(bk(4)[:, 0:E], y[:, k, :], route_w[:, k, :],
                                           start=(half == 0 and k == 0), stop=(half == 1 and k == KT - 1))
                    mm.then_inc(lg_ps, 1)
                    if mix is None:
                        pe.wait_ge(experts_ready, KT * PIECES)

                pe.wait_ge(kv_gathered[0], GATHERS)
                turn_k((0, 0, 0), 0)
                turn_q((0, 0, 0))
                pe.wait_ge(kT_ready, 2)
                turn_k((0, 0, 0), 1)
                each_pair(pe, pair)
                for e in range(E):
                    mix_expert(PAIRS - 1, e)

            @block.scalar
            def _(act):
                for s in out_stored:
                    act.sem_inc(s, 16)

                def store(m, u):
                    act.wait_ge(mix_done, m * E + (E + 2))
                    act.dma_start(out[bass.ds(m * P, P), :], acc[:, u, :]).then_inc(out_stored[u], 16)

                def kT_copy(p, b):
                    act.wait_ge(kT_ps, p * 2 + (b + 1))
                    act.activation(kT[:, b, 0, :], bk(5)[:, 0:KEYS], ACT.Copy).then_inc(kT_ready, 1)

                def qT_copy(p):
                    act.wait_ge(qT_ps, p + 3)
                    for gp in range(2):
                        act.activation(qT[:, gp, :, :, :].rearrange("p b h t -> p h b t"),
                                       bk(6)[:, gp * T // 2:(gp + 1) * T // 2].rearrange("p (h b t) -> p h b t", h=2, b=2),
                                       ACT.Copy).then_inc(qT_ready, 1)

                def route_exp(p):
                    act.wait_ge(lg_negmax, p + 1)
                    act.activation(rt[:, 2, :], lg[:, :], ACT.Exp, bias=rt[:, 1, 0:1]).then_inc(lg_exp, 1)

                def pair(p, u, mix, nxt):
                    for s in range(8):
                        act.wait_ge(nmx_ready, p * 8 + (s + 1))
                        act.activation(prob[:, s % 2, :], sm[:, s % 2, :], ACT.Exp, bias=nmx[:, s:s + 1], scale=SCALE,
                                       accum_out=rsum[:, s:s + 1]).then_inc(prob_ready, 1)
                        if s == 0 and mix is not None:
                            route_exp(mix)
                        act.wait_ge(pT_ps, p * 8 + (s + 1))
                        act.activation(pT[:, s % 2, 0:2, :], bk(4)[:, 0:2 * P].rearrange("p (c t) -> p c t", c=2), ACT.Copy)
                        act.activation(pT[0:C, s % 2, 2, :], bk(4)[0:C, 2 * P:3 * P], ACT.Copy).then_inc(pT_ready, 1)
                        if mix is None:
                            for piece in (2 * s, 2 * s + 1):
                                k, r = piece // PIECES, piece % PIECES
                                act.wait_ge(piece_loaded[piece % 2], piece // 2 * 16 + 16)
                                act.activation(experts_hi[:, k, :, r * PIECE:(r + 1) * PIECE].bitcast(F32R),
                                               stage[:, r % 2, :, :].rearrange("p r e -> p e r"), ACT.Copy).then_inc(piece_hi, 1)
                    if nxt is not None:
                        kT_copy(nxt[0], 0)
                    act.wait_ge(oT_ps, p + 1)
                    act.activation(oT[:, :, :, :, :].rearrange("p b g h t -> p (b g h t)"), bk(3), ACT.Copy).then_inc(oT_ready, 1)
                    if nxt is not None:
                        qT_copy(nxt[0])
                    act.wait_ge(yT_ps, p + 1)
                    act.activation(yT_hi[:, :, :].bitcast(F32R), bk(2).rearrange("p (k n) -> p k n", n=P), ACT.Copy).then_inc(yT_ready, 1)
                    if nxt is not None:
                        kT_copy(nxt[0], 1)
                    if mix is not None:
                        store(mix, 1 - u)

                kT_copy(0, 0)
                qT_copy(0)
                kT_copy(0, 1)
                each_pair(act, pair)
                route_exp(PAIRS - 1)
                store(PAIRS - 1, 1)
                for s in out_stored:
                    act.wait_ge(s, 16 * (PAIRS // 2) + 16)

            @block.vector
            def _(dve):
                dve.sem_inc(sm_ready, 2)
                dve.sem_inc(mix_done, 2)
                dve.sem_inc(lg_read, 1)

                def mix_add(m, u, e):
                    dve.wait_ge(mix_ps, m * E + (e + 1))
                    dve.wait_ge(mix_done, m * E + (e + 2))
                    dve.scalar_tensor_tensor(out=acc[:, u, :], in0=bk(5 + 2 * (e % 2)), scalar=rt[:, 6, e:e + 1], in1=acc[:, u, :],
                                             op0=ALU.mult, op1=ALU.add).then_inc(mix_done, 1)

                def kT_copy(p, b):
                    dve.wait_ge(kT_ps, p * 2 + (b + 1))
                    dve.tensor_copy(kT[:, b, 1, :], bk(7)[:, 0:KEYS]).then_inc(kT_ready, 1)

                def make_mask(p, b):
                    first = thr[:, bass.ds(p * 2 + b, 1)].to_broadcast([P, KEYS])
                    dve.tensor_tensor(mask[:, b, :], jrow[:, :], first, ALU.is_lt).then_inc(mask_step, 1)
                    dve.wait_ge(mask_step, p * 4 + (2 * b + 1))
                    dve.scalar_tensor_tensor(out=mask[:, b, :], in0=mask[:, b, :], scalar=MASKED, in1=band[:, :],
                                             op0=ALU.mult, op1=ALU.add).then_inc(mask_step, 1)

                def clip(p):
                    dve.wait_ge(lg_ps, p + 1)
                    dve.tensor_scalar(lg[:, :], bk(4)[:, 0:E], 50.0, -50.0, ALU.min, ALU.max).then_inc(lg_read, 1)

                def route(p):
                    n = Count()

                    def step(ins):
                        ins.then_inc(route_step, 1)
                        dve.wait_ge(route_step, p * ROUTE_STEPS + n.next())

                    dve.wait_ge(lg_read, p + 2)
                    step(dve.tensor_reduce(rt[:, 0, 0:1], lg[:, :], AX, ALU.max))
                    dve.tensor_scalar(rt[:, 1, 0:1], rt[:, 0, 0:1], -1.0, None, ALU.mult).then_inc(lg_negmax, 1)
                    other = lg[:, :].unsqueeze(1).to_broadcast([P, E, E])
                    own = lg[:, :].unsqueeze(2).to_broadcast([P, E, E])
                    step(dve.tensor_tensor(gtr[:, :, :], other, own, ALU.is_gt))
                    step(dve.tensor_tensor(eqr[:, :, :], other, own, ALU.is_equal))
                    step(dve.tensor_tensor(eqr[:, :, :], eqr[:, :, :], before[:, :, :], ALU.mult))
                    step(dve.tensor_tensor(gtr[:, :, :], gtr[:, :, :], eqr[:, :, :], ALU.add))
                    step(dve.tensor_reduce(rt[:, 3, :], gtr[:, :, :], AX, ALU.add))
                    step(dve.tensor_scalar(rt[:, 3, :], rt[:, 3, :], 2.0, None, ALU.is_lt))
                    dve.wait_ge(lg_exp, p + 1)
                    step(dve.tensor_tensor(rt[:, 4, :], rt[:, 3, :], rt[:, 2, :], ALU.mult))
                    step(dve.tensor_reduce(rt[:, 5, 0:1], rt[:, 4, :], AX, ALU.add))
                    step(dve.reciprocal(rt[:, 5, 1:2], rt[:, 5, 0:1]))
                    step(dve.tensor_scalar(rt[:, 6, :], rt[:, 4, :], rt[:, 5, 1:2], None, ALU.mult))
                    assert n.n == ROUTE_STEPS, n.n

                def low_parts(s):
                    for piece in (2 * s, 2 * s + 1):
                        k, r = piece // PIECES, piece % PIECES
                        dve.wait_ge(piece_hi, piece + 1)
                        at = slice(r * PIECE, (r + 1) * PIECE)
                        dve.tensor_tensor(experts_lo[:, k, :, at].bitcast(F32R), stage[:, r % 2, :, :].rearrange("p r e -> p e r"),
                                          experts_hi[:, k, :, at], ALU.subtract).then_inc(experts_ready, 1)

                def pair(p, u, mix, nxt):
                    def finish(s):
                        b = s // 4
                        if mix is not None:
                            if s == 0:
                                dve.wait_ge(acc_loaded[1 - u], (mix - (1 - u)) * 8 + 16)
                            mix_add(mix, 1 - u, s)
                        if s % 4 == 3:
                            dve.wait_ge(o_ps, p * 2 + (b + 5))
                            dve.reciprocal(rinv[:, 4 * b:4 * b + 4], rsum[:, 4 * b:4 * b + 4]).then_inc(rinv_step, 1)
                            dve.wait_ge(rinv_step, p * 2 + (b + 1))
                            dve.tensor_tensor(o_sb[:, b, :].rearrange("p (g d) -> p g d", g=G),
                                              bk(2 if b else 6)[:, 0:G * HD].rearrange("p (g d) -> p g d", g=G),
                                              rinv[:, 4 * b:4 * b + 4].unsqueeze(2).to_broadcast([P, G, HD]), ALU.mult).then_inc(o_ready, 1)

                    dve.wait_ge(mask_step, p * 4 + 4)
                    for s in range(8):
                        dve.wait_ge(score_ps, p * 8 + (s + 1))
                        dve.wait_ge(prob_ready, p * 8 + (s + 1))
                        dve.sem_inc(score_taken, 1)
                        dve.tensor_tensor_reduce(sm[:, s % 2, :], bk(s % 2)[:, 0:KEYS], mask[:, s // 4, :], 1.0, MASKED,
                                                 ALU.add, ALU.max, mx[:, s:s + 1]).then_inc(sm_ready, 1)
                        dve.wait_ge(sm_ready, p * 8 + (s + 3))
                        dve.tensor_scalar(nmx[:, s:s + 1], mx[:, s:s + 1], -SCALE, None, ALU.mult).then_inc(nmx_ready, 1)
                        if s == 0 and mix is not None:
                            route(mix)
                        if s >= 1:
                            finish(s - 1)
                        if s >= 1 and mix is None:
                            low_parts(s - 1)
                        if s == 5 and nxt is not None:
                            make_mask(nxt[0], 0)
                    if nxt is not None:
                        make_mask(nxt[0], 1)
                    finish(7)
                    if mix is None:
                        low_parts(7)
                    if nxt is not None:
                        kT_copy(nxt[0], 0)
                    dve.wait_ge(yT_ready, p * 2 + 1)
                    dve.tensor_tensor(yT_lo[:, :, :].bitcast(F32R), bk(2).rearrange("p (k n) -> p k n", n=P), yT_hi[:, :, :],
                                      ALU.subtract).then_inc(yT_ready, 1)
                    if nxt is not None:
                        kT_copy(nxt[0], 1)
                    clip(p)

                dve.sem_inc(prob_ready, 2)
                make_mask(0, 0)
                make_mask(0, 1)
                kT_copy(0, 0)
                kT_copy(0, 1)
                each_pair(dve, pair)
                route(PAIRS - 1)
                dve.wait_ge(acc_loaded[1], 16 * (PAIRS // 2))
                for e in range(E):
                    mix_add(PAIRS - 1, 1, e)



def _arrays(inputs):
    i = {k: np.asarray(v) for k, v in inputs.items()}
    heads = [(2 * gp + g) * 2 + h2 for gp in range(2) for h2 in range(2) for g in range(2)]
    wq = i["L1_cond_Wq"].reshape(H, HD, T)[heads].reshape(H * HD, T)
    wo = i["L1_cond_Wo"].reshape(T, H, HD)[:, heads].reshape(T, H * HD)
    kc, vc = (i[f"L1_cond_{n}_blocks"].transpose(0, 2, 1, 3).reshape(POOL_ROWS, G * HD) for n in "kv")
    half = np.arange(HALF, dtype=np.float32) / np.float32(HALF)
    return {
        "x": i["x"].reshape(TOK, T),
        "kv_lens": i["itok_B_37_3939"],
        "subjects": i["itok_B_0_7"].reshape(1, B),
        "tables": i["itok_Bx257_0_4111"].reshape(B * NBLK),
        "cond_w": i["L0_cond_weights"],
        "gate_t": i["L0_ffn_gate_w"].T,
        "up_t": i["L0_ffn_up_w"].T,
        "down_t": i["L0_ffn_down_w"].T,
        "gate_s": i["L0_ffn_gate_s"].reshape(IT, P).T,
        "up_s": i["L0_ffn_up_s"].reshape(IT, P).T,
        "down_s": i["L0_ffn_down_s"].reshape(1, T),
        "wqkv_t": np.concatenate([wq, i["L1_cond_Wk"], i["L1_cond_Wv"]]).T,
        "wo_t": wo.T,
        "q_norm": i["L1_cond_q_norm_scale"].reshape(1, HD),
        "k_norm": i["L1_cond_k_norm_scale"].reshape(1, HD),
        "kv_cache": np.concatenate([kc, vc], axis=1),
        "inv_freq": (np.float32(1.0) / np.float32(10000.0) ** half).reshape(1, HALF),
        "route_t": i["L1_ffn_gate_w"].T,
        "w_t": i["L1_ffn_W"].T,
        "atoms": i["L1_ffn_atoms"].reshape(A, P, SCH).transpose(0, 2, 1),
        "expert_atom": i["L1_ffn_expert_atom_weights"],
        "importance": i["L1_ffn_importance"].T.reshape(P, SCH, E),
        "mask_col": i["L1_ffn_mask_idx"].reshape(P, SCH),
        "mask_row": i["L1_ffn_mask_idx"].reshape(P, SCH).T,
    }


def kernel(**inputs):
    import numpy as _np
    import concourse.bacc as _bacc
    from concourse import mybir as _mybir
    from concourse.bass_utils import run_bass_kernel_spmd as _run

    nc = _bacc.Bacc("TRN2", target_bir_lowering=False, num_devices=1)
    arrays, args = {}, {}
    for name, a in _arrays(inputs).items():
        a = _np.ascontiguousarray(a)
        arrays[f"in_{name}"] = a
        args[name] = nc.dram_tensor(f"in_{name}", a.shape, _mybir.dt.from_np(a.dtype), kind="ExternalInput").ap()
    args["out"] = nc.dram_tensor("out_dram", (TOK, T), F32, kind="ExternalOutput").ap()
    bass_adaln_ffn_kernel(nc, **args)
    r = _run(nc, [arrays], core_ids=[0])
    return r.results[0]["out_dram"].reshape(B, C, T)
```

```python
from contextlib import ExitStack

import numpy as np

import concourse.bass as bass
from concourse import mybir

F32 = mybir.dt.float32
F32R = mybir.dt.float32r
I32 = mybir.dt.int32
ALU = mybir.AluOpType
ACT = mybir.ActivationFunctionType
AX = mybir.AxisListType.X

P = 128
B, C, T = 32, 64, 512
TOK = B * C
KT = T // P
NSUB = 8
INTER = 1408
IT = INTER // P
GROUPS = 4
GT = TOK // GROUPS
TPG = GT // P
SPG = B // GROUPS
PAIRS = B // 2
H, G, HD = 8, 4, 64
HALF = HD // 2
NQK = H + G
BLOCK, WINDOW, NBLK = 16, 256, 257
POOL_ROWS = 16 * NBLK * BLOCK
KEYS = WINDOW + C
KCH = (128, 128, 64)
NCH = len(KCH)
SLOTS = 21
SEG = 5
NSEG = B * SEG
SCALE = 256.0 ** -0.5
EPS = 1e-6
E, A, NS = 8, 64, 4096
SCH = NS // P
TBL = T * T
KEY = float(POOL_ROWS + 1)
SKIP = float(1 << 20)
MASKED = -1.0e30
TWO_PI = 2 * np.pi
C1 = 6.28125
C2 = float(np.floor((TWO_PI - C1) * 2**21) / 2**21)
C3 = float(np.float32(TWO_PI - C1 - C2))
MAGIC = 1.5 * 2.0**23
PI_IN = 3.1415925


class Count:

    def __init__(self, start=0):
        self.n = start

    def next(self):
        self.n += 1
        return self.n


def bass_adaln_ffn_kernel(nc, x, kv_lens, subjects, tables, cond_w, gate_t, up_t, down_t, gate_s, up_s, down_s,
                          wqkv_t, wo_t, q_norm, k_norm, kv_cache, inv_freq, route_t, w_t, atoms, expert_atom,
                          importance, mask_col, mask_row, out):
    q_dram = nc.dram_tensor("q_dram", (TOK, T), F32, kind="Internal").ap()
    kv_dram = nc.dram_tensor("kv_dram", (TOK, T), F32, kind="Internal").ap()
    x1_dram = nc.dram_tensor("x1_dram", (TOK, T), F32, kind="Internal").ap()
    table_dram = nc.dram_tensor("table_dram", (TBL + P, E), F32, kind="Internal").ap()

    sbuf_map = [(nc.sbuf_base + 31) // 32 * 32]

    def place(name, shape, dt=F32):
        off = sbuf_map[0]
        sbuf_map[0] = off + (int(np.prod(shape[1:])) * 4 + 31) // 32 * 32
        return nc.alloc_sbuf_tensor_at(name, list(shape), dt, offset=off)

    with ExitStack() as ctx:
        def sem(name):
            return ctx.enter_context(nc.semaphore(name))

        def psum(name, shape):
            return ctx.enter_context(nc.psum_tensor(name, shape, F32))

        ident = place("ident", (P, P))
        own_cache = place("own_cache", (P, B * NCH), I32)
        own_new = place("own_new", (P, B * NCH), I32)
        thr = place("thr", (P, B))
        band = place("band", (P, KEYS))
        jrow = place("jrow", (P, KEYS))
        before = place("before", (P, E, E))
        route_w = place("route_w", (P, KT, E))
        idx_c = [place(f"idx_c{u}", (P, 2 * NCH), I32) for u in range(2)]
        idx_n = [place(f"idx_n{u}", (P, 2 * NCH), I32) for u in range(2)]
        keep_at = sbuf_map[0]
        wqkv = place("wqkv", (P, KT, 2 * T))
        cos = place("cos", (P, PAIRS, HALF))
        sin = place("sin", (P, PAIRS, HALF))
        nscale = place("nscale", (P, NQK, HD))
        dscale = place("dscale", (P, T))
        gs = place("gs", (P, IT))
        us = place("us", (P, IT))
        key_addr = place("key_addr", (P, B * NCH))
        seg_start = place("seg_start", (P, B, SEG))
        seg_len = place("seg_len", (P, B, SEG))
        seg_key = place("seg_key", (P, B, SEG))
        tot = place("tot", (P, SCH, E))
        table_idx = place("table_idx", (P, SCH), I32)
        subj = place("subj", (1, B), I32)
        inexact = place("inexact", (1, 1), I32)
        wT_at = sbuf_map[0]
        wT_sb = place("wT_sb", (P, KT, T))
        zero8 = place("zero8", (P, E))
        RCOLS = T // 4
        wexp = place("wexp", (P, RCOLS, E))
        xc_at = sbuf_map[0]
        xc = place("xc", (P, TPG, T))
        cw = place("cw", (P, TPG, P))
        weights_at = sbuf_map[0]
        gate_raw = place("gate_raw", (P, KT, INTER))
        up_raw = place("up_raw", (P, KT, INTER))
        down_raw = place("down_raw", (P, IT, T))
        work_at = sbuf_map[0]
        sbuf_map[0] = weights_at
        gate_w = place("gate_w", (P, KT, INTER), F32R)
        up_w = place("up_w", (P, KT, INTER), F32R)
        down_w = place("down_w", (P, IT, T), F32R)
        assert sbuf_map[0] == work_at

        mrow_i = place("mrow_i", (P, SCH, P), I32)
        low = mrow_i[:, :, :].bitcast(F32)
        mrow = place("mrow", (P, SCH, P))
        mcol_i = place("mcol_i", (P, SCH), I32)
        mcol = place("mcol", (P, SCH))
        mhi_i = place("mhi_i", (P, SCH), I32)
        mlo_i = place("mlo_i", (P, SCH), I32)
        mhi = place("mhi", (P, SCH))
        mlo = place("mlo", (P, SCH))
        earlier = place("earlier", (P, SCH))
        lowtri = place("lowtri", (P, P))
        dump_i = place("dump_i", (P, 1), I32)
        dump = place("dump", (P, 1))
        wt = place("wt", (P, SCH, E))
        sig = place("sig", (P, SCH, E))
        eaw = place("eaw", (E, A))
        eaw_s = place("eaw_s", (E, 4))
        eawT = place("eawT", (A, E))
        atoms_sb = place("atoms_sb", (A, SCH, P))
        ang = place("ang", (P, PAIRS, HALF))
        turns = place("turns", (P, PAIRS, HALF))
        kvt_i = place("kvt_i", (P, PAIRS), I32)
        kvt = place("kvt", (P, PAIRS))
        tpos_i = place("tpos_i", (P, 1), I32)
        tpos = place("tpos", (P, 1))
        inv = place("inv", (P, HALF))
        qn = place("qn", (P, 2, HD))
        jrow_i = place("jrow_i", (P, KEYS), I32)
        dist_i = place("dist_i", (P, KEYS), I32)
        dist = place("dist", (P, KEYS))
        bits = place("bits", (P, INTER), I32)
        bits_max = place("bits_max", (P, 1))
        ones = place("ones", (P, 1))
        prologue_end = sbuf_map[0]

        sbuf_map[0] = work_at
        xr = place("xr", (P, TPG, T))
        hT_at = sbuf_map[0]
        hT_hi = place("hT_hi", (P, KT, GT))
        hT_lo = place("hT_lo", (P, KT, GT))
        hdn = place("hdn", (P, 2, GT))
        hdn_hi = place("hdn_hi", (P, 3, GT))
        hdn_lo = place("hdn_lo", (P, 3, GT))
        silu = place("silu", (P, 2, GT))
        x1 = place("x1", (P, TPG, T))
        x1T = place("x1T", (P, KT, GT))
        rot_a = place("rot_a", (P, NQK, HALF))
        rot_b = place("rot_b", (P, NQK, HALF))
        ssum = place("ssum", (P, 3, NQK))
        KCOLS = 4
        own_v = place("own_v", (P, KCOLS, NSEG))
        own_m = place("own_m", (P, KCOLS, NSEG))
        GCOLS = B * NCH // (GROUPS - 1)
        found = place("found", (P, GCOLS))
        owned = place("owned", (P, GCOLS))
        slot_val = place("slot_val", (P, E))
        slot_idx = place("slot_idx", (P, 1), I32)
        raw_at = sbuf_map[0]
        raw = place("raw", (P, 2, NQK * HD))
        sq = place("sq", (P, NQK * HD))
        q_out = place("q_out", (P, 2, T))
        kv_out = place("kv_out", (P, 2, T))
        layer0_end = sbuf_map[0]

        sbuf_map[0] = max(raw_at, prologue_end)
        oh = place("oh", (P, B, SLOTS))
        tb_f = place("tb_f", (P, B, SLOTS))
        tb_i = place("tb_i", (P, B, SLOTS), I32)
        kv_i = place("kv_i", (P, B), I32)
        kv_f = place("kv_f", (P, B))
        kvq_i = place("kvq_i", (P, B), I32)
        kvr_i = place("kvr_i", (P, B), I32)
        kvq = place("kvq", (P, B))
        kvr = place("kvr", (P, B))
        slot0 = place("slot0", (P, B))
        jcol_i = place("jcol_i", (P, NCH), I32)
        jcol = place("jcol", (P, NCH))
        posk_i = place("posk_i", (P, B, NCH), I32)
        slot_i = place("slot_i", (P, B, NCH), I32)
        off_i = place("off_i", (P, B, NCH), I32)
        rel = place("rel", (P, B, NCH))
        off_f = place("off_f", (P, B, NCH))
        kblk = place("kblk", (P, B, NCH))
        seg_rel = place("seg_rel", (P, B))
        seg_lo = place("seg_lo", (P, B, SEG))
        seg_hi = place("seg_hi", (P, B, SEG))
        seg_t = place("seg_t", (P, B, SEG))
        bbase_i = place("bbase_i", (P, B), I32)
        bbase = place("bbase", (P, B))
        io21_i = place("io21_i", (P, SLOTS), I32)
        io21 = place("io21", (P, SLOTS))
        index_end = sbuf_map[0]

        sbuf_map[0] = weights_at
        EARLY = KT // 2
        experts_hi, experts_lo = ([None] * KT for _ in range(2))
        for k in range(EARLY):
            experts_hi[k] = place(f"experts_hi{k}", (P, E, T), F32R)
            experts_lo[k] = place(f"experts_lo{k}", (P, E, T), F32R)
        assert sbuf_map[0] <= work_at
        after_experts = sbuf_map[0]
        EPIECE = T // 4
        EPIECES = T // EPIECE
        sbuf_map[0] = hT_at
        early_stage = place("early_stage", (P, 4, EPIECE, E))
        assert sbuf_map[0] <= hT_at + 2 * KT * GT * 4
        sbuf_map[0] = wT_at
        kv_t = [[place(f"kv_t0{b}", (P, NCH, T)) for b in range(2)]]
        assert sbuf_map[0] <= xc_at
        sbuf_map[0] = keep_at
        experts_hi[KT - 2] = place(f"experts_hi{KT - 2}", (P, E, T), F32R)
        wo = place("wo", (P, KT, T))
        mask = place("mask", (P, 2, KEYS))
        o_sb = place("o_sb", (P, 2, G * HD))
        assert sbuf_map[0] <= wT_at
        sbuf_map[0] = xc_at
        kT_hi = place("kT_hi", (P, 2, 2, KEYS), F32R)
        q_t = place("q_t", (P, 2, T))
        lg = place("lg", (P, E))
        gtr = place("gtr", (P, E, E))
        eqr = place("eqr", (P, E, E))
        rt = place("rt", (P, 8, E))
        mx = place("mx", (P, 8))
        nmx = place("nmx", (P, 8))
        rsum = place("rsum", (P, 8))
        exp_table = place("exp_table", (P, 1))
        rinv = place("rinv", (P, 8))
        assert sbuf_map[0] <= weights_at
        sbuf_map[0] = after_experts
        experts_lo[KT - 2] = place(f"experts_lo{KT - 2}", (P, E, T), F32R)
        experts_hi[KT - 1] = place(f"experts_hi{KT - 1}", (P, E, T), F32R)
        experts_lo[KT - 1] = place(f"experts_lo{KT - 1}", (P, E, T), F32R)
        PIECE = T // 8
        PIECES = T // PIECE
        STAGES = 4
        stage_at = sbuf_map[0]
        stage = place("stage", (P, STAGES, PIECE, E))
        sbuf_map[0] = stage_at + STAGES // 2 * PIECE * E * 4
        acc = place("acc", (P, 2, T))
        assert sbuf_map[0] == stage_at + STAGES * PIECE * E * 4
        kv_t.append([place(f"kv_t1{b}", (P, NCH, T)) for b in range(2)])
        qT_hi = place("qT_hi", (P, 2, 2, 2, C), F32R)
        qT_lo = place("qT_lo", (P, 2, 2, 2, C), F32R)
        kT_lo = place("kT_lo", (P, 2, 2, KEYS), F32R)
        route_hi = place("route_hi", (P, KT, E), F32R)
        route_lo = place("route_lo", (P, KT, E), F32R)
        prob = place("prob", (P, 2, KEYS))
        pT = place("pT", (P, 2, NCH, P))
        oT = place("oT", (P, 2, 2, 2, C))
        yT_hi = place("yT_hi", (P, KT, P), F32R)
        yT_lo = place("yT_lo", (P, KT, P), F32R)
        layer1_end = sbuf_map[0]
        assert max(index_end, layer0_end, layer1_end) <= nc.sbuf_usable_end, (
            index_end, layer0_end, layer1_end, nc.sbuf_usable_end)

        bank = [psum(f"bank{i}", [P, 2, T]) for i in range(4)]

        def bk(n):
            return bank[n // 2][:, n % 2, :]

        weights_loaded = sem("weights_loaded")
        ffn_loaded = [sem(f"ffn_loaded{k}") for k in range(3)]
        wexp_full = sem("wexp_full")
        table_init = sem("table_init")
        TABLE_INIT = 16 * (T // RCOLS * KT + 1)

        kv_loaded = sem("kv_loaded")
        consts_loaded = sem("consts_loaded")
        tables_loaded = [sem(f"tables_loaded{k}") for k in range(2)]
        iotas = sem("iotas")
        sparse_loaded = sem("sparse_loaded")
        p_dve = sem("p_dve")
        eaw_max = sem("eaw_max")
        eaw_exp = sem("eaw_exp")
        eaw_norm = sem("eaw_norm")
        eaw_T = sem("eaw_T")
        eaw_Tsb = sem("eaw_Tsb")
        delta_ps = sem("delta_ps")
        sig_ready = sem("sig_ready")
        wt_ready = sem("wt_ready")
        eq_ready = sem("eq_ready")
        low_ready = sem("low_ready")
        tot_ps = sem("tot_ps")
        sin_arg = sem("sin_arg")
        sin_done = sem("sin_done")
        ident_ready = sem("ident_ready")
        w_loaded = sem("w_loaded")
        bits_seen = sem("bits_seen")
        bits_summed = sem("bits_summed")
        inexact_ps = sem("inexact_ps")

        cw_zero = sem("cw_zero")
        subj_loaded = sem("subj_loaded")
        xc_loaded = sem("xc_loaded")
        cw_loaded = sem("cw_loaded")

        def load_blocks(eng, first, end, loaded):
            with eng.Fori(first, end) as b:
                q = eng.snap(eng.value_load(kv_i[0:1, bass.ds(b, 1)], min_val=0, max_val=(NBLK - 1) * BLOCK - C - 1) >> 4)
                slot = eng.snap((q >= 16) * (q - 16)).with_bounds(min_val=0, max_val=NBLK - SLOTS)
                eng.dma_start(tb_i[:, bass.ds(b, 1), :],
                              tables[bass.ds(b * NBLK + slot, SLOTS)].rearrange("(a n) -> a n", a=1).to_broadcast([P, SLOTS])).then_inc(loaded, 16)

        def load_x(eng, g):
            eng.dma_start(xc[:, :, :], x[bass.ds(g * GT, GT), :].rearrange("(k p) t -> p k t", p=P)).then_inc(xc_loaded, 16)
            for s in range(SPG):
                r = eng.value_load(subj[0:1, bass.ds(g * SPG + s, 1)], min_val=0, max_val=NSUB - 1)
                half = s % 2 * C
                eng.dma_start(cw[half:half + C, s // 2, half:half + C], cond_w[bass.ds(r, 1), :, :].rearrange("a c d -> (a c) d")).then_inc(cw_loaded, 16)

        with nc.Block() as block:
            @block.sync
            def _(sp):
                sp.dma_start(subj[:, :], subjects).then_inc(subj_loaded, 16)
                sp.dma_start(kv_i[:, :], kv_lens.rearrange("(a n) -> a n", a=1).to_broadcast([P, B])).then_inc(kv_loaded, 16)
                by_half = kv_lens.rearrange("(i h) -> h i", h=2)
                for h in range(2):
                    with nc.allow_non_contiguous_dma(reason="32 lengths"):
                        sp.dma_start(kvt_i[h * C:(h + 1) * C, :], by_half[h:h + 1, :].to_broadcast([C, PAIRS])).then_inc(consts_loaded, 16)
                sp.dma_start(inv[:, :], inv_freq.to_broadcast([P, HALF])).then_inc(consts_loaded, 16)
                sp.dma_start(qn[:, 0, :], q_norm.to_broadcast([P, HD])).then_inc(consts_loaded, 16)
                sp.dma_start(qn[:, 1, :], k_norm.to_broadcast([P, HD])).then_inc(consts_loaded, 16)
                sp.dma_start(mcol_i[:, :], mask_col).then_inc(sparse_loaded, 16)
                sp.dma_start(mrow_i[:, :, :], mask_row.rearrange("(a c) p -> a c p", a=1).to_broadcast([P, SCH, P])).then_inc(sparse_loaded, 16)
                sp.dma_start(eaw[:, :], expert_atom).then_inc(sparse_loaded, 16)
                sp.dma_start(atoms_sb[:, :, :], atoms).then_inc(sparse_loaded, 16)
                sp.dma_start(sig[:, :, :], importance).then_inc(sparse_loaded, 16)
                sp.wait_ge(kv_loaded, 16)
                load_blocks(sp, 0, B // 2, tables_loaded[0])
                sp.wait_ge(cw_zero, 1)
                sp.wait_ge(subj_loaded, 16)
                load_x(sp, 0)

            @block.gpsimd
            def _(pool):
                pool.memset(cw[:, :, :], 0.0).then_inc(cw_zero, 1)
                pool.memset(ident[:, :], 0.0).then_inc(ident_ready, 1)
                pool.memset(lowtri[:, :], 1.0).then_inc(ident_ready, 1)
                pool.memset(zero8[:, :], 0.0)
                pool.memset(ones[:, :], 1.0)
                pool.memset(before[:, :, :], 1.0).then_inc(ident_ready, 1)
                pool.iota(jcol_i[:, :], [[P, NCH]], base=-WINDOW, channel_multiplier=1).then_inc(iotas, 1)
                pool.iota(io21_i[:, :], [[1, SLOTS]], base=0, channel_multiplier=0).then_inc(iotas, 1)
                pool.iota(bbase_i[:, :], [[C, B]], base=1, channel_multiplier=0).then_inc(iotas, 1)
                pool.iota(jrow_i[:, :], [[1, KEYS]], base=0, channel_multiplier=0).then_inc(iotas, 1)
                pool.iota(dump_i[:, :], [[0, 1]], base=TBL, channel_multiplier=1).then_inc(iotas, 1)
                for h in range(2):
                    pool.wait_ge(iotas, 5 + 2 * h)
                    pool.iota(tpos_i[h * C:(h + 1) * C, :], [[0, 1]], base=0, channel_multiplier=1).then_inc(iotas, 1)
                    pool.iota(dist_i[h * C:(h + 1) * C, :], [[1, KEYS]], base=0, channel_multiplier=-1).then_inc(iotas, 1)
                pool.wait_ge(ident_ready, 3)
                pool.wait_ge(iotas, 9)
                pool.affine_select(out=ident[:, :], in_=ident[:, :], compare_op=ALU.not_equal, fill=1.0,
                                   base=0, pattern=[[-1, P]], channel_multiplier=1).then_inc(ident_ready, 1)
                pool.affine_select(out=lowtri[:, :], in_=lowtri[:, :], compare_op=ALU.is_gt, fill=0.0,
                                   base=0, pattern=[[-1, P]], channel_multiplier=1).then_inc(ident_ready, 1)
                pool.affine_select(out=before[:, :, :], in_=before[:, :, :], compare_op=ALU.is_gt, fill=0.0,
                                   base=0, pattern=[[1, E], [-1, E]], channel_multiplier=0).then_inc(ident_ready, 1)
                pool.wait_ge(kv_loaded, 16)
                load_blocks(pool, B // 2, B, tables_loaded[1])
                pool.wait_ge(eq_ready, 1)
                pool.wait_ge(ident_ready, 6)
                pool.tensor_tensor(low, mrow[:, :, :], lowtri[:, :].unsqueeze(1).to_broadcast([P, SCH, P]), ALU.mult).then_inc(low_ready, 1)

            @block.scalar
            def _(act):
                act.dma_start(wT_sb[:, :, :], w_t.rearrange("(c p) r -> p c r", p=P)).then_inc(w_loaded, 16)
                act.wait_ge(sparse_loaded, 16 * 5)
                for w, (to, src) in enumerate(((gate_raw, gate_t), (up_raw, up_t), (down_raw, down_t))):
                    act.dma_start(to[:, :, :], src.rearrange("(k p) n -> p k n", p=P)).then_inc(ffn_loaded[w], 16)
                act.dma_start(wqkv[:, :, :], wqkv_t.rearrange("(k p) n -> p k n", p=P)).then_inc(weights_loaded, 16)
                act.dma_start(dscale[:, :], down_s.to_broadcast([P, T])).then_inc(weights_loaded, 16)
                act.dma_start(gs[:, :], gate_s).then_inc(weights_loaded, 16)
                act.dma_start(us[:, :], up_s).then_inc(weights_loaded, 16)
                act.dma_start(route_w[:, :, :], route_t.rearrange("(k p) n -> p k n", p=P)).then_inc(weights_loaded, 16)
                act.activation(sig[:, :, :], sig[:, :, :], ACT.Sigmoid).then_inc(sig_ready, 1)
                act.wait_ge(eaw_max, 1)
                act.activation(eaw[:, :], eaw[:, :], ACT.Exp, bias=eaw_s[:, 1:2], accum_out=eaw_s[:, 2:3]).then_inc(eaw_exp, 1)
                for w, (to, loaded) in enumerate(((gate_w, gate_raw), (up_w, up_raw), (down_w, down_raw))):
                    act.wait_ge(bits_seen, w + 1)
                    act.activation(to[:, :, :], loaded[:, :, :], ACT.Copy)
                act.wait_ge(sin_arg, 1)
                act.activation(sin[:, :, :], ang[:, :, :], ACT.Sin).then_inc(sin_done, 1)
                act.wait_ge(sin_arg, 2)
                act.activation(cos[:, :, :], turns[:, :, :], ACT.Sin).then_inc(sin_done, 1)

            @block.tensor
            def _(pe):
                pe.wait_ge(ident_ready, 6)
                pe.wait_ge(eaw_norm, 1)
                pe.transpose(bk(0)[0:A, 0:E], eaw[:, :], ident[0:E, 0:E]).then_inc(eaw_T, 1)
                pe.wait_ge(eaw_Tsb, 1)
                for s in range(SCH):
                    mm = pe.matmul(bk(1)[:, s * E:(s + 1) * E], atoms_sb[:, s, :], eawT[:, :], start=True, stop=True)
                mm.then_inc(delta_ps, 1)
                pe.wait_ge(wt_ready, 1)
                pe.wait_ge(eq_ready, 1)
                for s in range(SCH):
                    mm = pe.matmul(bk(2)[:, s * E:(s + 1) * E], mrow[:, s, :], wt[:, s, :], start=True, stop=True)
                mm.then_inc(tot_ps, 1)
                pe.wait_ge(bits_summed, 1)
                pe.matmul(bk(3)[0:1, 0:1], bits_max[:, :], ones[:, :], start=True, stop=True).then_inc(inexact_ps, 1)

            @block.vector
            def _(dve):
                n = Count()
                dve.wait_ge(kv_loaded, 16)
                dve.wait_ge(iotas, 9)
                dve.tensor_copy(kv_f[:, :], kv_i[:, :]).then_inc(p_dve, 1)
                dve.tensor_scalar(kvq_i[:, :], kv_i[:, :], 4, None, ALU.arith_shift_right).then_inc(p_dve, 1)
                dve.tensor_scalar(kvr_i[:, :], kv_i[:, :], 15, None, ALU.bitwise_and).then_inc(p_dve, 1)
                dve.tensor_copy(jcol[:, :], jcol_i[:, :]).then_inc(p_dve, 1)
                dve.tensor_copy(io21[:, :], io21_i[:, :]).then_inc(p_dve, 1)
                dve.tensor_copy(bbase[:, :], bbase_i[:, :]).then_inc(p_dve, 1)
                dve.tensor_copy(jrow[:, :], jrow_i[:, :]).then_inc(p_dve, 1)
                dve.tensor_copy(dump[:, :], dump_i[:, :]).then_inc(p_dve, 1)
                dve.tensor_copy(tpos[:, :], tpos_i[:, :]).then_inc(p_dve, 1)
                dve.tensor_copy(dist[:, :], dist_i[:, :]).then_inc(p_dve, 1)
                n.n = 10
                dve.wait_ge(p_dve, 10)
                dve.tensor_copy(kvq[:, :], kvq_i[:, :]).then_inc(p_dve, 1)
                dve.tensor_copy(kvr[:, :], kvr_i[:, :]).then_inc(p_dve, 1)
                dve.tensor_scalar(thr[:, :], kv_f[:, :], -1.0, float(WINDOW), ALU.mult, ALU.add).then_inc(p_dve, 1)
                dve.tensor_scalar(band[:, :], dist[:, :], 0.0, None, ALU.is_gt).then_inc(p_dve, 1)
                n.n = 14
                dve.wait_ge(p_dve, 14)
                dve.scalar_tensor_tensor(out=band[:, :], in0=dist[:, :], scalar=float(WINDOW), in1=band[:, :],
                                         op0=ALU.is_le, op1=ALU.mult).then_inc(p_dve, 1)
                dve.wait_ge(p_dve, n.next())
                dve.tensor_scalar(band[:, :], band[:, :], -MASKED, MASKED, ALU.mult, ALU.add).then_inc(p_dve, 1)
                dve.wait_ge(p_dve, n.next())
                dve.wait_ge(sparse_loaded, 16 * 5)
                dve.tensor_reduce(eaw_s[:, 0:1], eaw[:, :], AX, ALU.max).then_inc(p_dve, 1)
                dve.wait_ge(p_dve, n.next())
                dve.tensor_scalar(eaw_s[:, 1:2], eaw_s[:, 0:1], -1.0, None, ALU.mult).then_inc(eaw_max, 1)
                dve.tensor_copy(mcol[:, :], mcol_i[:, :]).then_inc(p_dve, 1)
                dve.wait_ge(p_dve, n.next())
                dve.tensor_copy(mrow[:, :, :], mrow_i[:, :, :]).then_inc(p_dve, 1)
                dve.wait_ge(p_dve, n.next())
                dve.tensor_tensor(mrow[:, :, :], mrow[:, :, :], mcol[:, :].unsqueeze(2).to_broadcast([P, SCH, P]),
                                  ALU.is_equal).then_inc(eq_ready, 1)
                dve.wait_ge(eaw_exp, 1)
                dve.reciprocal(eaw_s[:, 3:4], eaw_s[:, 2:3]).then_inc(p_dve, 1)
                dve.wait_ge(p_dve, n.next())
                dve.tensor_scalar(eaw[:, :], eaw[:, :], eaw_s[:, 3:4], None, ALU.mult).then_inc(eaw_norm, 1)
                dve.wait_ge(eaw_T, 1)
                dve.tensor_copy(eawT[:, :], bk(0)[0:A, 0:E]).then_inc(eaw_Tsb, 1)
                chunks = [w[:, :, :].rearrange("p k n -> p (k n)").bitcast(I32)[:, c * INTER:(c + 1) * INTER]
                          for w in (gate_raw, up_raw, down_raw) for c in range(KT)]
                for c, chunk in enumerate(chunks):
                    if c == 2 * KT:
                        dve.wait_ge(delta_ps, 1)
                        dve.wait_ge(sig_ready, 1)
                        dve.tensor_tensor(wt[:, :, :], bk(1)[:, 0:SCH * E].rearrange("p (s e) -> p s e", e=E), sig[:, :, :], ALU.mult).then_inc(wt_ready, 1)
                    if c % KT == 0:
                        dve.wait_ge(ffn_loaded[c // KT], 16)
                    if c == 0:
                        dve.tensor_copy(bits[:, :], chunk).then_inc(p_dve, 1)
                    else:
                        dve.tensor_tensor(bits[:, :], bits[:, :], chunk, ALU.bitwise_or).then_inc(p_dve, 1)
                    dve.wait_ge(p_dve, n.next())
                    if c % KT == KT - 1:
                        dve.sem_inc(bits_seen, 1)
                dve.tensor_scalar(bits[:, :], bits[:, :], (1 << 12) - 1, None, ALU.bitwise_and).then_inc(p_dve, 1)
                dve.wait_ge(p_dve, n.next())
                dve.tensor_reduce(bits_max[:, :], bits[:, :], AX, ALU.max).then_inc(bits_summed, 1)
                dve.wait_ge(low_ready, 1)
                dve.tensor_reduce(earlier[:, :], low, AX, ALU.add).then_inc(p_dve, 1)
                dve.wait_ge(p_dve, n.next())
                dve.tensor_scalar(mhi_i[:, :], mcol_i[:, :], 9, None, ALU.arith_shift_right).then_inc(p_dve, 1)
                dve.tensor_scalar(mlo_i[:, :], mcol_i[:, :], T - 1, None, ALU.bitwise_and).then_inc(p_dve, 1)
                dve.tensor_scalar(earlier[:, :], earlier[:, :], 1.0, None, ALU.min).then_inc(p_dve, 1)
                n.n += 3
                dve.wait_ge(p_dve, n.n)
                dve.tensor_copy(mhi[:, :], mhi_i[:, :]).then_inc(p_dve, 1)
                dve.tensor_copy(mlo[:, :], mlo_i[:, :]).then_inc(p_dve, 1)
                n.n += 2
                dve.wait_ge(p_dve, n.n)
                dve.scalar_tensor_tensor(out=mlo[:, :], in0=mlo[:, :], scalar=float(T), in1=mhi[:, :], op0=ALU.mult, op1=ALU.add).then_inc(p_dve, 1)
                dve.wait_ge(p_dve, n.next())
                dve.tensor_scalar(mhi[:, :], mlo[:, :], -1.0, dump[:, :], ALU.mult, ALU.add).then_inc(p_dve, 1)
                dve.wait_ge(p_dve, n.next())
                dve.tensor_tensor(mhi[:, :], mhi[:, :], earlier[:, :], ALU.mult).then_inc(p_dve, 1)
                dve.wait_ge(p_dve, n.next())
                dve.tensor_tensor(table_idx[:, :], mhi[:, :], mlo[:, :], ALU.add).then_inc(p_dve, 1)
                dve.wait_ge(p_dve, n.next())
                dve.wait_ge(consts_loaded, 16 * 5)
                dve.tensor_copy(kvt[:, :], kvt_i[:, :]).then_inc(p_dve, 1)
                dve.wait_ge(p_dve, n.next())
                dve.tensor_scalar(kvt[:, :], kvt[:, :], tpos[:, :], None, ALU.add).then_inc(p_dve, 1)
                dve.wait_ge(p_dve, n.next())
                dve.tensor_tensor(ang[:, :, :], kvt[:, :].unsqueeze(2).to_broadcast([P, PAIRS, HALF]),
                                  inv[:, :].unsqueeze(1).to_broadcast([P, PAIRS, HALF]), ALU.mult).then_inc(p_dve, 1)
                dve.wait_ge(p_dve, n.next())
                dve.tensor_scalar(turns[:, :, :], ang[:, :, :], float(1 / TWO_PI), MAGIC, ALU.mult, ALU.add).then_inc(p_dve, 1)
                dve.wait_ge(p_dve, n.next())
                dve.tensor_scalar(turns[:, :, :], turns[:, :, :], MAGIC, None, ALU.subtract).then_inc(p_dve, 1)
                dve.wait_ge(p_dve, n.next())
                for part in (C1, C2, C3):
                    dve.scalar_tensor_tensor(out=ang[:, :, :], in0=turns[:, :, :], scalar=-part, in1=ang[:, :, :],
                                             op0=ALU.mult, op1=ALU.add).then_inc(p_dve, 1)
                    dve.wait_ge(p_dve, n.next())
                dve.tensor_scalar(ang[:, :, :], ang[:, :, :], PI_IN, -PI_IN, ALU.min, ALU.max).then_inc(sin_arg, 1)
                dve.wait_ge(sin_arg, 1)
                dve.scalar_tensor_tensor(out=turns[:, :, :], in0=ang[:, :, :], scalar=-1.0, in1=ang[:, :, :],
                                         op0=ALU.mult, op1=ALU.max).then_inc(p_dve, 1)
                dve.wait_ge(p_dve, n.next())
                dve.tensor_scalar(turns[:, :, :], turns[:, :, :], -1.0, float(np.pi / 2), ALU.mult, ALU.add).then_inc(sin_arg, 1)
                dve.tensor_scalar(nscale[:, 0:H, :], qn[:, 0:1, :].to_broadcast([P, H, HD]), 1.0, None, ALU.add).then_inc(p_dve, 1)
                dve.tensor_scalar(nscale[:, H:NQK, :], qn[:, 1:2, :].to_broadcast([P, G, HD]), 1.0, None, ALU.add).then_inc(p_dve, 1)
                n.n += 2
                dve.wait_ge(tot_ps, 1)
                dve.wait_ge(inexact_ps, 1)
                dve.tensor_scalar(inexact[:, :], bk(3)[0:1, 0:1], 1.0, None, ALU.min).then_inc(p_dve, 1)
                n.n += 1
                dve.tensor_copy(tot[:, :, :], bk(2)[:, 0:SCH * E].rearrange("p (s e) -> p s e", e=E)).then_inc(p_dve, 1)
                dve.wait_ge(p_dve, n.next())
                for loaded in tables_loaded:
                    dve.wait_ge(loaded, 16 * B // 2)

        WEIGHTS = 16 * 5
        xr_loaded = sem("xr_loaded")
        proj_ps = sem("proj_ps")
        h_hi = sem("h_hi")
        h_ready = sem("h_ready")
        gu_ps = sem("gu_ps")
        silu_ready = sem("silu_ready")
        hdn_ready = sem("hdn_ready")
        hdn_hi_ready = sem("hdn_hi_ready")
        hdn_split = sem("hdn_split")
        down_ps = sem("down_ps")
        DOWNS = IT - 1 + TPG
        weights_reloaded = sem("weights_reloaded")
        res_ready = sem("res_ready")
        x1T_ps = sem("x1T_ps")
        x1T_ready = sem("x1T_ready")
        x1_stored = [sem(f"x1_stored{j}") for j in range(TPG)]
        qkv_ps = sem("qkv_ps")
        qkv_sq = sem("qkv_sq")
        qkv_copied = sem("qkv_copied")
        std_arg = sem("std_arg")
        std_ready = sem("std_ready")
        qk_ready = sem("qk_ready")
        q_stored = [sem(f"q_stored{k}") for k in range(2)]
        kv_stored = [sem(f"kv_stored{k}") for k in range(2)]
        d0 = sem("d0")
        own_gate = sem("own_gate")
        OWN = GCOLS // KCOLS
        OWN_STEPS = 5 + 7 * OWN
        DSTEPS = 52 + OWN_STEPS
        index_step = sem("index_step")

        def each_group(eng, group):
            with eng.Fori(0, GROUPS - 1) as g:
                group(g, False)
            group(GROUPS - 1, True)
        slot_ready = sem("slot_ready")
        entry_added = sem("entry_added")
        slot_taken = sem("slot_taken")
        idx_copied = sem("idx_copied")
        idx_taken = sem("idx_taken")
        kv_gathered = [sem(f"kv_gathered{u}") for u in range(2)]
        early_loaded = [sem(f"early_loaded{k}") for k in range(4)]
        early_hi = sem("early_hi")
        early_ready = sem("early_ready")

        def copy_idx(pool, u, p):
            cols = bass.ds(p * (2 * NCH), 2 * NCH)
            pool.tensor_copy(idx_c[u][:, :], own_cache[:, cols]).then_inc(idx_copied, 1)
            pool.tensor_copy(idx_n[u][:, :], own_new[:, cols]).then_inc(idx_copied, 1)

        def gather_cache(pool, u):
            for b in range(2):
                for c in range(2):
                    pool.indirect_dma_start(kv_t[u][b][:, c, :], None, kv_cache,
                                            bass.IndirectOffsetOnAxis(idx_c[u][:, b * NCH + c:b * NCH + c + 1], 0),
                                            bounds_check=POOL_ROWS - 1, oob_is_err=False).then_inc(kv_gathered[u], 16)

        def gather_new(pool, u):
            for b in range(2):
                for c, rows in enumerate(KCH):
                    pool.indirect_dma_start(kv_t[u][b][0:rows, c, :], None, kv_dram,
                                            bass.IndirectOffsetOnAxis(idx_n[u][0:rows, b * NCH + c:b * NCH + c + 1], 0),
                                            bounds_check=TOK - 1, oob_is_err=False).then_inc(kv_gathered[u], 16)

        with nc.Block() as block:
            @block.sync
            def _(sp):
                with sp.If(sp.value_load(inexact[0:1, 0:1], min_val=0, max_val=1) == 1):
                    for to, src in ((gate_raw, gate_t), (up_raw, up_t), (down_raw, down_t)):
                        sp.dma_start(to[:, :, :], src.rearrange("(k p) n -> p k n", p=P)).then_inc(weights_reloaded, 16)
                    sp.wait_ge(weights_reloaded, 16 * 3)
                sp.wait_ge(weights_loaded, WEIGHTS)

                def load_piece(piece):
                    k, r = piece // EPIECES, piece % EPIECES
                    sp.dma_start(early_stage[:, piece % 4, :, :], table_dram[k * P * T:(k + 1) * P * T, :].rearrange(
                        "(p r) e -> p r e", p=P)[:, r * EPIECE:(r + 1) * EPIECE, :]).then_inc(early_loaded[piece % 4], 16)

                def load_xr(g):
                    sp.dma_start(xr[:, :, :], x[bass.ds(g * GT, GT), :].rearrange("(k p) t -> p k t", p=P)).then_inc(xr_loaded, 16)

                def group(g, last):
                    def store_x1(j):
                        sp.wait_ge(res_ready, g * TPG + j + 1)
                        sp.dma_start(x1_dram[bass.ds(g * GT + j * P, P), :], x1[:, j, :]).then_inc(x1_stored[j], 16)

                    def store_qkv(j):
                        sp.wait_ge(qk_ready, g * TPG + j + 3)
                        sp.dma_start(q_dram[bass.ds(g * GT + j * P, P), :], q_out[:, j % 2, :]).then_inc(q_stored[j % 2], 16)
                        sp.dma_start(kv_dram[bass.ds(g * GT + j * P, P), :], kv_out[:, j % 2, :]).then_inc(kv_stored[j % 2], 16)

                    if not last:
                        sp.wait_ge(proj_ps, g * KT + KT)
                        load_x(sp, g + 1)
                    if last:
                        sp.wait_ge(entry_added, 16 * SCH)
                        sp.wait_ge(down_ps, GROUPS * DOWNS)
                        for piece in range(4):
                            load_piece(piece)
                    for j in range(TPG):
                        store_x1(j)
                    if not last:
                        load_xr(g + 1)
                    if last:
                        for piece in range(4, EARLY * EPIECES):
                            sp.wait_ge(early_ready, piece - 3)
                            load_piece(piece)
                    for j in range(TPG):
                        store_qkv(j)

                load_xr(0)
                each_group(sp, group)
                for s in x1_stored:
                    sp.wait_ge(s, 16 * GROUPS + 16)
                for s in q_stored + kv_stored:
                    sp.wait_ge(s, 16 * (GROUPS * TPG // 2) + 16)

            @block.tensor
            def _(pe):
                pe.wait_ge(weights_loaded, WEIGHTS)

                def project(g):
                    pe.wait_ge(xc_loaded, g * 16 + 16)
                    pe.wait_ge(cw_loaded, g * (16 * SPG) + 16 * SPG)
                    for k in range(KT):
                        for j in range(TPG):
                            mm = pe.matmul(bk(k)[:, j * P:(j + 1) * P], xc[:, j, k * P:(k + 1) * P], cw[:, j, :],
                                           start=True, stop=True)
                        mm.then_inc(proj_ps, 1)

                def all_groups(form):
                    gate, up, down_rows = (gate_w, up_w, down_w) if form == F32R else (gate_raw, up_raw, down_raw)

                    def group(g, last):
                        def gate_up(i):
                            if i < 2:
                                pe.wait_ge(qkv_copied, g * TPG + i + 1)
                            else:
                                pe.wait_ge(hdn_ready, g * IT + i - 1)
                            if i == 0:
                                pe.wait_ge(h_ready, g * KT + KT)
                            for w, half in ((gate, 0), (up, 1)):
                                for k in range(KT):
                                    for n, part in enumerate((hT_hi, hT_lo)):
                                        mm = pe.matmul(bk(2 * (i % 2) + half), w[:, k, i * P:(i + 1) * P],
                                                       part[:, k, :].bitcast(form), start=(k == 0 and n == 0), stop=(k == KT - 1 and n == 1))
                            mm.then_inc(gu_ps, 1)

                        def down(i):
                            pe.wait_ge(hdn_split, g * IT + i + 1)
                            if i == 0:
                                pe.wait_ge(x1T_ready, g * TPG + 1)
                            for j in range(TPG):
                                for n, part in enumerate((hdn_hi, hdn_lo)):
                                    mm = pe.matmul(bk(4 + j), part[:, i % 3, j * P:(j + 1) * P].bitcast(form),
                                                   down_rows[:, i, :], start=(i == 0 and n == 0), stop=(i == IT - 1 and n == 1))
                                if i == IT - 1 or j == TPG - 1:
                                    mm.then_inc(down_ps, 1)

                        def turn(j):
                            pe.wait_ge(res_ready, g * TPG + j + 1)
                            for k in range(KT):
                                mm = pe.transpose(bk(4 + j)[:, k * P:(k + 1) * P], x1[:, j, k * P:(k + 1) * P], ident[:, :])
                            mm.then_inc(x1T_ps, 1)

                        def qkv(j):
                            pe.wait_ge(x1T_ready, g * TPG + j + 2)
                            if j >= 2:
                                pe.wait_ge(qkv_copied, g * TPG + j + 1)
                            elif not last:
                                pe.wait_ge(h_ready, (g + 1) * KT + 2 * j + 2)
                            for half in range(2):
                                for k in range(KT):
                                    mm = pe.matmul(bk(2 * (j % 2) + half), x1T[:, k, j * P:(j + 1) * P], wqkv[:, k, half * T:(half + 1) * T],
                                                   start=(k == 0), stop=(k == KT - 1))
                            mm.then_inc(qkv_ps, 1)

                        for i in range(IT):
                            gate_up(i)
                            if i >= 2:
                                down(i - 2)
                        down(IT - 2)
                        down(IT - 1)
                        if not last:
                            project(g + 1)
                        turn(0)
                        turn(1)
                        qkv(0)
                        turn(2)
                        qkv(1)
                        turn(3)
                        qkv(2)
                        qkv(3)

                    each_group(pe, group)

                project(0)
                general = pe.value_load(inexact[0:1, 0:1], min_val=0, max_val=1)
                with pe.If(general == 0):
                    all_groups(F32R)
                with pe.Else():
                    pe.wait_ge(weights_reloaded, 16 * 3)
                    all_groups(F32)

            @block.scalar
            def _(act):
                act.sem_inc(x1T_ready, 1)
                act.sem_inc(qkv_copied, 2)

                def high_h(g, k):
                    act.wait_ge(proj_ps, g * KT + k + 1)
                    act.activation(hT_hi[:, k, :].bitcast(F32R), bk(k), ACT.Copy).then_inc(h_hi, 1)

                def group(g, last):
                    def high_hdn(i):
                        act.wait_ge(hdn_ready, g * IT + i + 1)
                        if i >= 3:
                            act.wait_ge(down_ps, g * DOWNS + i - 2)
                        act.activation(hdn_hi[:, i % 3, :].bitcast(F32R), hdn[:, i % 2, :], ACT.Copy).then_inc(hdn_hi_ready, 1)

                    for i in range(IT):
                        act.wait_ge(gu_ps, g * IT + i + 1)
                        act.activation(silu[:, i % 2, :], bk(2 * (i % 2)), ACT.Silu, scale=gs[:, i:i + 1]).then_inc(silu_ready, 1)
                        if i >= 1:
                            high_hdn(i - 1)
                    high_hdn(IT - 1)

                    def x1T_copy(j):
                        act.wait_ge(x1T_ps, g * TPG + j + 1)
                        act.activation(x1T[:, :, j * P:(j + 1) * P], bk(4 + j).rearrange("p (k n) -> p k n", n=P), ACT.Copy).then_inc(x1T_ready, 1)

                    def qkv_copy(j):
                        act.wait_ge(qkv_ps, g * TPG + j + 1)
                        act.wait_ge(qk_ready, g * TPG + j + 1)
                        act.wait_ge(kv_stored[j % 2], g * 32 + 16 * (j // 2) + 16)
                        act.activation(sq[:, :], bank[j % 2][:, :, :].rearrange("p a n -> p (a n)")[:, 0:NQK * HD], ACT.Square).then_inc(qkv_sq, 1)
                        act.activation(raw[:, j % 2, :], bank[j % 2][:, :, :].rearrange("p a n -> p (a n)")[:, 0:NQK * HD], ACT.Copy)
                        act.activation(kv_out[:, j % 2, G * HD:], bk(2 * (j % 2) + 1)[:, G * HD:], ACT.Copy).then_inc(qkv_copied, 1)

                    def roots(j):
                        act.wait_ge(std_arg, g * TPG + j + 1)
                        act.activation(ssum[:, 2, :], ssum[:, 1, :], ACT.Sqrt).then_inc(std_ready, 1)

                    def early_parts(n):
                        if last:
                            for piece in (2 * n, 2 * n + 1):
                                k, r = piece // EPIECES, piece % EPIECES
                                act.wait_ge(down_ps, GROUPS * DOWNS)
                                act.wait_ge(early_loaded[piece % 4], piece // 4 * 16 + 16)
                                act.activation(experts_hi[k][:, :, r * EPIECE:(r + 1) * EPIECE],
                                               early_stage[:, piece % 4, :, :].rearrange("p r e -> p e r"), ACT.Copy).then_inc(early_hi, 1)

                    if not last:
                        high_h(g + 1, 0)
                        high_h(g + 1, 1)
                    x1T_copy(0)
                    if not last:
                        high_h(g + 1, 2)
                        high_h(g + 1, 3)
                    x1T_copy(1)
                    early_parts(0)
                    qkv_copy(0)
                    x1T_copy(2)
                    roots(0)
                    early_parts(1)
                    qkv_copy(1)
                    x1T_copy(3)
                    roots(1)
                    early_parts(2)
                    qkv_copy(2)
                    roots(2)
                    early_parts(3)
                    qkv_copy(3)
                    roots(3)

                for k in range(KT):
                    high_h(0, k)
                each_group(act, group)

            @block.vector
            def _(dve):
                dve.sem_inc(qk_ready, 2)
                for s in x1_stored + q_stored + kv_stored:
                    dve.sem_inc(s, 16)
                dve.wait_ge(weights_loaded, WEIGHTS)

                m = Count()

                def istep(*ins):
                    for one in ins:
                        one.then_inc(index_step, 1)
                        m.next()
                    dve.wait_ge(index_step, m.n)

                def look_up(to, which):
                    istep(dve.tensor_tensor(oh[:, :, :], which.unsqueeze(2).to_broadcast([P, B, SLOTS]),
                                            io21[:, :].unsqueeze(1).to_broadcast([P, B, SLOTS]), ALU.is_equal))
                    istep(dve.tensor_tensor(oh[:, :, :], oh[:, :, :], tb_f[:, :, :], ALU.mult))
                    istep(dve.tensor_reduce(to, oh[:, :, :], AX, ALU.add))

                def slot_places():
                    istep(dve.tensor_scalar(slot0[:, :], kvq[:, :], float(WINDOW // BLOCK), 0.0, ALU.subtract, ALU.max),
                          dve.tensor_tensor(posk_i[:, :, :], kv_f[:, :].unsqueeze(2).to_broadcast([P, B, NCH]),
                                            jcol[:, :].unsqueeze(1).to_broadcast([P, B, NCH]), ALU.add))
                    istep(dve.tensor_scalar(posk_i[:, :, :], posk_i[:, :, :], 0.0, None, ALU.max))
                    istep(dve.tensor_scalar(slot_i[:, :, :], posk_i[:, :, :], 4, None, ALU.arith_shift_right),
                          dve.tensor_scalar(off_i[:, :, :], posk_i[:, :, :], 15, None, ALU.bitwise_and))
                    istep(dve.tensor_copy(rel[:, :, :], slot_i[:, :, :]),
                          dve.tensor_copy(off_f[:, :, :], off_i[:, :, :]),
                          dve.tensor_copy(tb_f[:, :, :], tb_i[:, :, :]))
                    istep(dve.tensor_tensor(rel[:, :, :], rel[:, :, :], slot0[:, :].unsqueeze(2).to_broadcast([P, B, NCH]), ALU.subtract))

                def slot_rows():
                    istep(dve.scalar_tensor_tensor(out=key_addr[:, :].rearrange("p (b c) -> p b c", c=NCH), in0=kblk[:, :, :],
                                                   scalar=float(BLOCK), in1=off_f[:, :, :], op0=ALU.mult, op1=ALU.add))

                def segment(i):
                    istep(dve.scalar_tensor_tensor(out=seg_rel[:, :], in0=kvq[:, :], scalar=float(i), in1=slot0[:, :],
                                                   op0=ALU.add, op1=ALU.subtract),
                          dve.tensor_scalar(seg_t[:, :, i], kvr[:, :], -1.0, float(BLOCK * i), ALU.mult, ALU.add),
                          dve.tensor_scalar(seg_hi[:, :, i], kvr[:, :], -1.0, float(BLOCK * (i + 1)), ALU.mult, ALU.add))
                    look_up(seg_start[:, :, i], seg_rel[:, :])

                def segment_rows():
                    istep(dve.tensor_scalar(seg_t[:, :, :], seg_t[:, :, :], 0.0, None, ALU.max),
                          dve.tensor_scalar(seg_hi[:, :, :], seg_hi[:, :, :], float(C), None, ALU.min),
                          dve.tensor_scalar(seg_start[:, :, :], seg_start[:, :, :], float(BLOCK), None, ALU.mult))
                    number = bbase[:, :].unsqueeze(2).to_broadcast([P, B, SEG])
                    istep(dve.tensor_tensor(seg_lo[:, :, :], seg_t[:, :, :], number, ALU.add),
                          dve.tensor_tensor(seg_len[:, :, :], seg_hi[:, :, :], seg_t[:, :, :], ALU.subtract),
                          dve.tensor_tensor(seg_start[:, :, 0], seg_start[:, :, 0], kvr[:, :], ALU.add))
                    istep(dve.scalar_tensor_tensor(out=seg_key[:, :, :], in0=seg_lo[:, :, :], scalar=KEY, in1=seg_start[:, :, :],
                                                   op0=ALU.add, op1=ALU.subtract))

                def index_work(i):
                    if i == 1:
                        slot_places()
                    elif 2 <= i < 2 + NCH:
                        look_up(kblk[:, :, i - 2], rel[:, :, i - 2])
                    elif i >= 2 + NCH and i - 2 - NCH < SEG:
                        if i == 2 + NCH:
                            slot_rows()
                        segment(i - 2 - NCH)
                    elif i == IT - 1:
                        segment_rows()

                def low_h(g, k):
                    dve.wait_ge(h_hi, g * KT + k + 1)
                    dve.tensor_tensor(hT_lo[:, k, :].bitcast(F32R), bk(k), hT_hi[:, k, :], ALU.subtract).then_inc(h_ready, 1)

                def gated(g, i):
                    dve.wait_ge(silu_ready, g * IT + i + 1)
                    if i >= 2:
                        dve.wait_ge(hdn_split, g * IT + i - 1)
                    dve.scalar_tensor_tensor(out=hdn[:, i % 2, :], in0=bk(2 * (i % 2) + 1), scalar=us[:, i:i + 1], in1=silu[:, i % 2, :],
                                             op0=ALU.mult, op1=ALU.mult).then_inc(hdn_ready, 1)

                def group(g, last, first=False):
                    n = Count()

                    def owners(c):
                        full = [P, KCOLS, NSEG]
                        flat = lambda t: t[:, :, :].rearrange("p b i -> p (b i)")
                        wide = lambda t: flat(t).unsqueeze(1).to_broadcast(full)
                        addr = key_addr[:, bass.ds((g - 1) * GCOLS + c * KCOLS, KCOLS)]
                        if c >= 1:
                            dve.wait_ge(d0, g * DSTEPS + n.n)
                        dve.tensor_tensor(own_v[:, :, :], addr.unsqueeze(2).to_broadcast(full), wide(seg_start), ALU.subtract).then_inc(d0, 1)
                        dve.wait_ge(d0, g * DSTEPS + n.next())
                        dve.tensor_tensor(own_m[:, :, :], own_v[:, :, :], wide(seg_len), ALU.is_lt).then_inc(d0, 1)
                        dve.wait_ge(d0, g * DSTEPS + n.next())
                        dve.scalar_tensor_tensor(out=own_m[:, :, :], in0=own_v[:, :, :], scalar=0.0, in1=own_m[:, :, :],
                                                 op0=ALU.is_ge, op1=ALU.mult).then_inc(d0, 1)
                        dve.wait_ge(d0, g * DSTEPS + n.next())
                        dve.sem_inc(own_gate, 1)
                        for k in range(KCOLS):
                            at = c * KCOLS + k
                            dve.tensor_tensor_reduce(own_v[:, k, :], own_m[:, k, :], flat(seg_key), 1.0, 0.0, ALU.mult, ALU.max,
                                                     found[:, at:at + 1]).then_inc(d0, 1)
                            n.next()

                    def own_rows():
                        cols = bass.ds((g - 1) * GCOLS, GCOLS)
                        addr = key_addr[:, cols]
                        dve.wait_ge(d0, g * DSTEPS + n.n)
                        dve.tensor_scalar(owned[:, :], found[:, :], 0.0, SKIP, ALU.is_gt, ALU.mult).then_inc(d0, 1)
                        dve.wait_ge(d0, g * DSTEPS + n.next())
                        dve.tensor_tensor(own_cache[:, cols], owned[:, :], addr, ALU.add).then_inc(d0, 1)
                        dve.tensor_scalar(found[:, :], found[:, :], SKIP - KEY - 1.0, None, ALU.add).then_inc(d0, 1)
                        n.next()
                        dve.wait_ge(d0, g * DSTEPS + n.next())
                        dve.tensor_tensor(found[:, :], found[:, :], owned[:, :], ALU.subtract).then_inc(d0, 1)
                        dve.wait_ge(d0, g * DSTEPS + n.next())
                        dve.tensor_tensor(own_new[:, cols], found[:, :], addr, ALU.add).then_inc(d0, 1)
                        dve.wait_ge(d0, g * DSTEPS + n.next())

                    def low_hdn(i):
                        dve.wait_ge(hdn_hi_ready, g * IT + i + 1)
                        dve.tensor_tensor(hdn_lo[:, i % 3, :].bitcast(F32R), hdn[:, i % 2, :], hdn_hi[:, i % 3, :],
                                          ALU.subtract).then_inc(hdn_split, 1)

                    for i in range(IT):
                        if i >= 1 or first:
                            gated(g, i)
                        if i >= 1:
                            low_hdn(i - 1)
                        if first:
                            index_work(i)
                        elif 1 <= i <= OWN:
                            owners(i - 1)
                        elif i == OWN + 1:
                            own_rows()
                    low_hdn(IT - 1)

                    def residual(j):
                        dve.wait_ge(down_ps, g * DOWNS + IT + j)
                        if j == 0:
                            dve.wait_ge(xr_loaded, g * 16 + 16)
                        dve.wait_ge(x1_stored[j], g * 16 + 16)
                        dve.tensor_tensor(x1[:, j, :], bk(4 + j), dscale[:, :], ALU.mult).then_inc(d0, 1)
                        dve.wait_ge(d0, g * DSTEPS + n.next())
                        dve.tensor_tensor(x1[:, j, :], x1[:, j, :], xr[:, j, :], ALU.add).then_inc(res_ready, 1)

                    def rotate(j):
                        heads = raw[:, j % 2, :].rearrange("p (h d) -> p h d", d=HD)
                        wide = [P, NQK, HALF]
                        tile_cos = cos[:, bass.ds(g * TPG + j, 1), :].to_broadcast(wide)
                        tile_sin = sin[:, bass.ds(g * TPG + j, 1), :].to_broadcast(wide)
                        dve.wait_ge(qkv_sq, g * TPG + j + 1)
                        dve.tensor_reduce(ssum[:, 0, :], sq[:, :].rearrange("p (h d) -> p h d", d=HD), AX, ALU.add).then_inc(d0, 1)
                        dve.wait_ge(d0, g * DSTEPS + n.next())
                        dve.tensor_scalar(ssum[:, 1, :], ssum[:, 0, :], 1.0 / HD, EPS, ALU.mult, ALU.add).then_inc(std_arg, 1)
                        dve.wait_ge(qkv_copied, g * TPG + j + 3)
                        dve.tensor_tensor(heads, heads, nscale[:, :, :], ALU.mult).then_inc(d0, 1)
                        dve.wait_ge(d0, g * DSTEPS + n.next())
                        dve.wait_ge(std_ready, g * TPG + j + 1)
                        dve.reciprocal(ssum[:, 0, :], ssum[:, 2, :]).then_inc(d0, 1)
                        dve.wait_ge(d0, g * DSTEPS + n.next())
                        dve.tensor_tensor(heads, heads, ssum[:, 0, :].unsqueeze(2).to_broadcast([P, NQK, HD]), ALU.mult).then_inc(d0, 1)
                        dve.wait_ge(d0, g * DSTEPS + n.next())
                        x_lo, x_hi = heads[:, :, 0:HALF], heads[:, :, HALF:HD]
                        dve.wait_ge(q_stored[j % 2], g * 32 + 16 * (j // 2) + 16)
                        dve.wait_ge(kv_stored[j % 2], g * 32 + 16 * (j // 2) + 16)
                        for part, (straight, crossed, op) in enumerate(((x_lo, x_hi, ALU.subtract), (x_hi, x_lo, ALU.add))):
                            dve.tensor_tensor(rot_a[:, :, :], straight, tile_cos, ALU.mult).then_inc(d0, 1)
                            dve.tensor_tensor(rot_b[:, :, :], crossed, tile_sin, ALU.mult).then_inc(d0, 1)
                            n.next()
                            dve.wait_ge(d0, g * DSTEPS + n.next())
                            at = slice(part * HALF, (part + 1) * HALF)
                            dve.tensor_tensor(q_out[:, j % 2, :].rearrange("p (h d) -> p h d", d=HD)[:, :, at],
                                              rot_a[:, 0:H, :], rot_b[:, 0:H, :], op).then_inc(d0, 1)
                            dve.tensor_tensor(kv_out[:, j % 2, 0:G * HD].rearrange("p (h d) -> p h d", d=HD)[:, :, at],
                                              rot_a[:, H:NQK, :], rot_b[:, H:NQK, :], op).then_inc(d0, 1)
                            n.next()
                            dve.wait_ge(d0, g * DSTEPS + n.next())
                            if part == 0 and j == TPG - 1 and not last:
                                gated(g + 1, 0)
                        dve.sem_inc(qk_ready, 1)

                    residual(0)
                    residual(1)
                    if not last:
                        low_h(g + 1, 0)
                        low_h(g + 1, 1)
                    residual(2)
                    if not last:
                        low_h(g + 1, 2)
                        low_h(g + 1, 3)
                    residual(3)
                    rotate(0)
                    rotate(1)
                    rotate(2)
                    rotate(3)
                    assert n.n == DSTEPS - (OWN_STEPS if first else 0), n.n
                    if first:
                        dve.sem_inc(d0, OWN_STEPS)

                for k in range(KT):
                    low_h(0, k)
                group(0, False, first=True)
                with dve.Fori(1, GROUPS - 1) as g:
                    group(g, False)
                group(GROUPS - 1, True)

            @block.gpsimd
            def _(pool):
                Q = T // RCOLS
                for c in range(KT):
                    for h in range(Q):
                        if Q * c + h >= 1:
                            pool.wait_ge(table_init, 16 * (Q * c + h))
                        part = wT_sb[:, c, h * RCOLS:(h + 1) * RCOLS]
                        pool.tensor_copy(wexp[:, :, :], part.unsqueeze(2).to_broadcast([P, RCOLS, E])).then_inc(wexp_full, 1)
                        pool.wait_ge(wexp_full, Q * c + h + 1)
                        pool.dma_start(table_dram[c * P * T:(c + 1) * P * T, :].rearrange("(p h r) e -> p h (r e)", p=P, h=Q)[:, h, :],
                                       wexp[:, :, :].rearrange("p r e -> p (r e)")).then_inc(table_init, 16)
                pool.dma_start(table_dram[TBL:TBL + P, :], zero8[:, :]).then_inc(table_init, 16)
                pool.wait_ge(table_init, TABLE_INIT)
                with pool.Fori(0, SCH) as s:
                    pool.tensor_copy(slot_idx[:, :], table_idx[:, bass.ds(s, 1)]).then_inc(slot_ready, 1)
                    pool.tensor_copy(slot_val[:, :], tot[:, bass.ds(s, 1), :].rearrange("p a e -> p (a e)")).then_inc(slot_ready, 1)
                    pool.wait_ge(slot_ready, s * 2 + 2)
                    pool.sem_inc(slot_taken, 1)
                    pool.indirect_dma_start(table_dram, bass.IndirectOffsetOnAxis(slot_idx[:, 0:1], 0), slot_val[:, :], None,
                                            compute_op=ALU.add).then_inc(entry_added, 16)
                    pool.wait_ge(entry_added, s * 16 + 16)
                pool.wait_ge(d0, DSTEPS * 2)
                pool.sem_inc(slot_taken, 1)
                copy_idx(pool, 0, 0)
                pool.wait_ge(idx_copied, 2)
                pool.sem_inc(slot_taken, 1)
                gather_cache(pool, 0)
                pool.wait_ge(kv_gathered[0], 16 * 4)
                pool.sem_inc(slot_taken, 1)
                for piece in range(EARLY * EPIECES):
                    k, r = piece // EPIECES, piece % EPIECES
                    at = slice(r * EPIECE, (r + 1) * EPIECE)
                    pool.wait_ge(early_hi, piece + 1)
                    pool.tensor_tensor(experts_lo[k][:, :, at], early_stage[:, piece % 4, :, :].rearrange("p r e -> p e r"),
                                       experts_hi[k][:, :, at].bitcast(F32), ALU.subtract).then_inc(early_ready, 1)


        wo_loaded = sem("wo_loaded")
        piece_loaded = [sem(f"piece_loaded{r}") for r in range(STAGES)]
        piece_hi = sem("piece_hi")
        experts_ready = sem("experts_ready")
        q_loaded = [sem(f"q_loaded{u}") for u in range(2)]
        acc_loaded = [sem(f"acc_loaded{u}") for u in range(2)]
        out_stored = [sem(f"out_stored{u}") for u in range(2)]
        kT_ps = sem("kT_ps")
        kT_hi_ready = sem("kT_hi_ready")
        kT_ready = sem("kT_ready")
        qT_ps = sem("qT_ps")
        qT_hi_ready = sem("qT_hi_ready")
        qT_ready = sem("qT_ready")
        route_split = sem("route_split")
        mask_ready = sem("mask_ready")
        score_ps = sem("score_ps")
        score_taken = sem("score_taken")
        sm_ready = sem("sm_ready")
        nmx_ready = sem("nmx_ready")
        prob_ready = sem("prob_ready")
        pT_ps = sem("pT_ps")
        pT_ready = sem("pT_ready")
        o_ps = sem("o_ps")
        o_ready = sem("o_ready")
        oT_ps = sem("oT_ps")
        oT_ready = sem("oT_ready")
        yT_ps = sem("yT_ps")
        yT_ready = sem("yT_ready")
        lg_ps = sem("lg_ps")
        lg_read = sem("lg_read")
        lg_negmax = sem("lg_negmax")
        lg_exp = sem("lg_exp")
        rw_ready = sem("rw_ready")
        mix_ps = sem("mix_ps")
        mix_done = sem("mix_done")
        mask_step = sem("mask_step")
        rinv_step = sem("rinv_step")
        route_step = sem("route_step")
        ROUTE_STEPS = 11
        GATHERS = 16 * (4 + 2 * NCH)

        KBANKS = ((0, 1), (5, 7))

        def each_pair(eng, pair):
            pair(0, 0, None, (1, 1, 0))
            with eng.Fori(0, PAIRS // 2 - 1) as i:
                pair(i * 2 + 1, 1, i * 2, (i * 2 + 2, 0, i + 1))
                pair(i * 2 + 2, 0, i * 2 + 1, (i * 2 + 3, 1, i + 1))
            pair(PAIRS - 1, 1, PAIRS - 2, None)

        with nc.Block() as block:
            @block.sync
            def _(sp):
                sp.dma_start(wo[:, :, :], wo_t.rearrange("(k p) n -> p k n", p=P)).then_inc(wo_loaded, 16)

                sp.dma_start(q_t[:, 0, :], q_dram[0:P, :]).then_inc(q_loaded[0], 16)
                sp.dma_start(q_t[:, 1, :], q_dram[P:2 * P, :]).then_inc(q_loaded[1], 16)
                for k in range(KT - EARLY):
                    for r in range(PIECES):
                        piece = k * PIECES + r
                        if piece >= STAGES:
                            sp.wait_ge(experts_ready, piece - STAGES + 1)
                        sp.dma_start(stage[:, piece % STAGES, :, :], table_dram[(EARLY + k) * P * T:(EARLY + k + 1) * P * T, :].rearrange(
                            "(p r) e -> p r e", p=P)[:, r * PIECE:(r + 1) * PIECE, :]).then_inc(piece_loaded[piece % STAGES], 16)
                sp.wait_ge(experts_ready, (KT - EARLY) * PIECES)
                sp.dma_start(acc[:, 0, :], x1_dram[0:P, :]).then_inc(acc_loaded[0], 16)
                sp.dma_start(acc[:, 1, :], x1_dram[P:2 * P, :]).then_inc(acc_loaded[1], 16)
                with sp.Fori(1, PAIRS // 2) as i:
                    for u in range(2):
                        sp.wait_ge(qT_ps, i * 2 + (u + 1))
                        sp.dma_start(q_t[:, u, :], q_dram[bass.ds(i * (2 * P) + u * P, P), :]).then_inc(q_loaded[u], 16)
                        sp.wait_ge(out_stored[u], i * 16 + 16)
                        sp.dma_start(acc[:, u, :], x1_dram[bass.ds(i * (2 * P) + u * P, P), :]).then_inc(acc_loaded[u], 16)

            @block.gpsimd
            def _(pool):
                gather_new(pool, 0)
                pool.wait_ge(kv_gathered[0], GATHERS)
                pool.sem_inc(idx_taken, 1)

                def pair(p, u, use):
                    copy_idx(pool, u, p)
                    pool.wait_ge(idx_copied, p * 2 + 2)
                    pool.sem_inc(idx_taken, 1)
                    pool.wait_ge(o_ps, p * 2 + 2)
                    pool.sem_inc(idx_taken, 1)
                    gather_cache(pool, u)
                    pool.wait_ge(kv_gathered[u], use * GATHERS + 16 * 4)
                    pool.sem_inc(idx_taken, 1)
                    gather_new(pool, u)
                    pool.wait_ge(kv_gathered[u], use * GATHERS + GATHERS)
                    pool.sem_inc(idx_taken, 1)

                pair(1, 1, 0)
                with pool.Fori(1, PAIRS // 2) as i:
                    for u in range(2):
                        pair(i * 2 + u, u, i)

            @block.tensor
            def _(pe):
                pe.sem_inc(o_ps, 4)
                pe.sem_inc(qT_ps, 2)
                pe.sem_inc(pT_ps, 2)

                def mix_expert(m, e, tiles=range(KT)):
                    if 0 in tiles:
                        pe.wait_ge(mix_done, m * E + (e + 1))
                    for k in tiles:
                        for n, (y, w) in enumerate(((yT_hi, experts_hi), (yT_hi, experts_lo), (yT_lo, experts_hi))):
                            mm = pe.matmul(bk(5 + 2 * (e % 2)), y[:, k, :], w[k][:, e, :],
                                           start=(k == 0 and n == 0), stop=(k == KT - 1 and n == 2))
                    if KT - 1 in tiles:
                        mm.then_inc(mix_ps, 1)

                def logits(m):
                    for n, (y, r) in enumerate(((yT_hi, route_hi), (yT_hi, route_lo), (yT_lo, route_hi))):
                        if n != 1:
                            pe.wait_ge(yT_ready, m * 2 + (1 if n == 0 else 2))
                        for k in range(KT):
                            mm = pe.matmul(bk(3)[:, 0:E], y[:, k, :], r[:, k, :],
                                           start=(n == 0 and k == 0), stop=(n == 2 and k == KT - 1))
                    mm.then_inc(lg_ps, 1)

                def turn_k(pr, b):
                    p, u, use = pr
                    for gp in range(2):
                        for c, rows in enumerate(KCH):
                            mm = pe.transpose(bk(KBANKS[b][gp])[:, c * P:c * P + rows], kv_t[u][b][0:rows, c, gp * P:(gp + 1) * P],
                                              ident[0:rows, 0:rows])
                    mm.then_inc(kT_ps, 1)

                def turn_q(pr):
                    p, u, use = pr
                    pe.wait_ge(q_loaded[u], use * 16 + 16)
                    for k in range(KT):
                        mm = pe.transpose(bk(6)[:, k * P:(k + 1) * P], q_t[:, u, k * P:(k + 1) * P], ident[:, :])
                    mm.then_inc(qT_ps, 1)

                def pair(p, u, mix, nxt):
                    def score(s):
                        b, gp, g = s // 4, s // 2 % 2, s % 2
                        rows = slice(g * HD, (g + 1) * HD)
                        if s == 0:
                            pe.wait_ge(qT_ready, p * 2 + 2)
                            pe.wait_ge(kT_ready, p * 4 + 2)
                        if s == 4:
                            pe.wait_ge(kT_ready, p * 4 + 4)
                        pe.wait_ge(sm_ready, p * 8 + (s + 1))
                        for n, (q, k) in enumerate(((qT_hi, kT_hi), (qT_hi, kT_lo), (qT_lo, kT_hi))):
                            mm = pe.matmul(bk(s % 2)[:, 0:KEYS], q[rows, gp, b, :, :].rearrange("p h t -> p (h t)"), k[rows, b, gp, :],
                                           start=(n == 0), stop=(n == 2))
                        mm.then_inc(score_ps, 1)

                    score(0)
                    for s in range(8):
                        if s < 7 and mix is not None:
                            score(s + 1)
                        if s == 0 and mix is not None:
                            logits(mix)
                            pe.wait_ge(kT_ready, p * 4 + 4)
                            mix_expert(mix, 0, range(KT // 2))
                        pe.wait_ge(prob_ready, p * 8 + (s + 1))
                        for c, rows in enumerate(KCH):
                            mm = pe.transpose(bk(4)[0:rows, c * P:(c + 1) * P], prob[:, s % 2, c * P:c * P + rows], ident[:, :])
                        mm.then_inc(pT_ps, 1)
                        if s < 7 and mix is None:
                            score(s + 1)
                        if mix is not None:
                            mix_expert(mix, s, range(KT // 2, KT) if s == 0 else range(KT))
                        pe.wait_ge(pT_ready, p * 8 + (s + 1))
                        b, g = s // 4, s % 4
                        for c, rows in enumerate(KCH):
                            mm = pe.matmul(bk(2 if b else 6)[:, g * HD:(g + 1) * HD], pT[0:rows, s % 2, c, :],
                                           kv_t[u][b][0:rows, c, (G + g) * HD:(G + g + 1) * HD], start=(c == 0), stop=(c == NCH - 1))
                        if g == 3:
                            mm.then_inc(o_ps, 1)
                    def turn_o(b):
                        pe.wait_ge(o_ready, p * 2 + (b + 1))
                        for gp in range(2):
                            mm = pe.transpose(bk(3 + b)[:, gp * P:(gp + 1) * P], o_sb[:, b, gp * P:(gp + 1) * P], ident[:, :])
                        mm.then_inc(oT_ps, 1)

                    if mix is not None:
                        pe.wait_ge(lg_read, mix + 1)
                    turn_o(0)
                    if nxt is not None:
                        pe.wait_ge(kv_gathered[nxt[1]], nxt[2] * GATHERS + GATHERS)
                        pe.wait_ge(sm_ready, p * 8 + 10)
                        turn_k(nxt, 0)
                    turn_o(1)
                    if nxt is not None:
                        turn_q(nxt)
                    if mix is None:
                        pe.wait_ge(wo_loaded, 16)
                    pe.wait_ge(oT_ready, p * 2 + 2)
                    for d in range(KT):
                        for k in range(KT):
                            mm = pe.matmul(bk(2)[:, d * P:(d + 1) * P], wo[:, k, d * P:(d + 1) * P],
                                           oT[:, :, k // 2, k % 2, :], start=(k == 0), stop=(k == KT - 1))
                    mm.then_inc(yT_ps, 1)
                    if nxt is not None:
                        if mix is not None:
                            pe.wait_ge(mix_done, mix * E + (E + 2))
                        turn_k(nxt, 1)
                    if mix is None:
                        pe.wait_ge(experts_ready, (KT - EARLY) * PIECES)

                turn_q((0, 0, 0))
                pe.wait_ge(kv_gathered[0], GATHERS)
                turn_k((0, 0, 0), 0)
                turn_k((0, 0, 0), 1)
                pe.wait_ge(route_split, 2)
                each_pair(pe, pair)
                logits(PAIRS - 1)
                for e in range(E):
                    mix_expert(PAIRS - 1, e)

            @block.scalar
            def _(act):
                for s in out_stored:
                    act.sem_inc(s, 16)

                def store(m, u):
                    act.wait_ge(mix_done, m * E + (E + 2))
                    act.dma_start(out[bass.ds(m * P, P), :], acc[:, u, :]).then_inc(out_stored[u], 16)

                def kT_copy(p, b):
                    act.wait_ge(kT_ps, p * 2 + (b + 1))
                    for gp in range(2):
                        act.activation(kT_hi[:, b, gp, :], bk(KBANKS[b][gp])[:, 0:KEYS], ACT.Copy).then_inc(kT_hi_ready, 1)

                def qT_copy(p):
                    act.wait_ge(qT_ps, p + 3)
                    for gp in range(2):
                        act.activation(qT_hi[:, gp, :, :, :].rearrange("p b h t -> p h b t"),
                                       bk(6)[:, gp * T // 2:(gp + 1) * T // 2].rearrange("p (h b t) -> p h b t", h=2, b=2),
                                       ACT.Copy).then_inc(qT_hi_ready, 1)

                def high_part(piece):
                    k, r = piece // PIECES, piece % PIECES
                    act.wait_ge(piece_loaded[piece % STAGES], piece // STAGES * 16 + 16)
                    act.activation(experts_hi[EARLY + k][:, :, r * PIECE:(r + 1) * PIECE],
                                   stage[:, piece % STAGES, :, :].rearrange("p r e -> p e r"), ACT.Copy).then_inc(piece_hi, 1)

                def route_exp(p):
                    act.wait_ge(lg_negmax, p + 1)
                    act.activation(rt[:, 2, :], lg[:, :], ACT.Exp, bias=rt[:, 1, 0:1]).then_inc(lg_exp, 1)

                def pair(p, u, mix, nxt):
                    def exponential(s):
                        act.wait_ge(nmx_ready, p * 8 + (s + 1))
                        act.activation(prob[:, s % 2, :], prob[:, s % 2, :], ACT.Exp, bias=nmx[:, s:s + 1], scale=SCALE,
                                       accum_out=rsum[:, s:s + 1]).then_inc(prob_ready, 1)

                    for s in range(8):
                        if s != 1 or mix is None:
                            exponential(s)
                        if s == 0 and mix is not None:
                            exponential(1)
                            route_exp(mix)
                        if mix is None:
                            high_part(2 * s)
                        act.wait_ge(pT_ps, p * 8 + (s + 3))
                        act.activation(pT[:, s % 2, 0:2, :], bk(4)[:, 0:2 * P].rearrange("p (c t) -> p c t", c=2), ACT.Copy)
                        act.activation(pT[0:C, s % 2, 2, :], bk(4)[0:C, 2 * P:3 * P], ACT.Copy).then_inc(pT_ready, 1)
                        if mix is None:
                            high_part(2 * s + 1)
                    for b in range(2):
                        act.wait_ge(oT_ps, p * 2 + (b + 1))
                        act.activation(oT[:, b, :, :, :].rearrange("p g h t -> p (g h t)"), bk(3 + b)[:, 0:2 * P],
                                       ACT.Copy).then_inc(oT_ready, 1)
                    if nxt is not None:
                        kT_copy(nxt[0], 0)
                        qT_copy(nxt[0])
                    act.wait_ge(yT_ps, p + 1)
                    act.activation(yT_hi[:, :, :], bk(2).rearrange("p (k n) -> p k n", n=P), ACT.Copy).then_inc(yT_ready, 1)
                    if nxt is not None:
                        kT_copy(nxt[0], 1)
                    if mix is not None:
                        store(mix, 1 - u)

                act.activation(exp_table[:, :], ident[:, 0:1], ACT.Exp)
                qT_copy(0)
                kT_copy(0, 0)
                kT_copy(0, 1)
                each_pair(act, pair)
                route_exp(PAIRS - 1)
                store(PAIRS - 1, 1)
                for s in out_stored:
                    act.wait_ge(s, 16 * (PAIRS // 2) + 16)

            @block.vector
            def _(dve):
                dve.sem_inc(sm_ready, 2)
                dve.sem_inc(mix_done, 2)

                def mix_add(m, u, e):
                    dve.wait_ge(mix_ps, m * E + (e + 1))
                    dve.wait_ge(mix_done, m * E + (e + 2))
                    dve.scalar_tensor_tensor(out=acc[:, u, :], in0=bk(5 + 2 * (e % 2)), scalar=rt[:, 6, e:e + 1], in1=acc[:, u, :],
                                             op0=ALU.mult, op1=ALU.add).then_inc(mix_done, 1)

                def kT_copy(p, b):
                    for gp in range(2):
                        dve.wait_ge(kT_hi_ready, p * 4 + (2 * b + gp + 1))
                        dve.tensor_tensor(kT_lo[:, b, gp, :], bk(KBANKS[b][gp])[:, 0:KEYS], kT_hi[:, b, gp, :].bitcast(F32),
                                          ALU.subtract).then_inc(kT_ready, 1)

                def qT_copy(p):
                    dve.wait_ge(qT_hi_ready, p * 2 + 2)
                    for gp in range(2):
                        dve.tensor_tensor(qT_lo[:, gp, :, :, :].rearrange("p b h t -> p h b t"),
                                          bk(6)[:, gp * T // 2:(gp + 1) * T // 2].rearrange("p (h b t) -> p h b t", h=2, b=2),
                                          qT_hi[:, gp, :, :, :].rearrange("p b h t -> p h b t").bitcast(F32),
                                          ALU.subtract).then_inc(qT_ready, 1)

                def make_mask(p, b):
                    first = thr[:, bass.ds(p * 2 + b, 1)].to_broadcast([P, KEYS])
                    dve.tensor_tensor(mask[:, b, :], jrow[:, :], first, ALU.is_lt).then_inc(mask_step, 1)
                    dve.wait_ge(mask_step, p * 4 + (2 * b + 1))
                    dve.scalar_tensor_tensor(out=mask[:, b, :], in0=mask[:, b, :], scalar=MASKED, in1=band[:, :],
                                             op0=ALU.mult, op1=ALU.add).then_inc(mask_step, 1)

                def route(p):
                    n = Count()

                    def step(ins):
                        ins.then_inc(route_step, 1)
                        dve.wait_ge(route_step, p * ROUTE_STEPS + n.next())

                    dve.wait_ge(lg_ps, p + 1)
                    dve.tensor_scalar(lg[:, :], bk(3)[:, 0:E], 50.0, -50.0, ALU.min, ALU.max).then_inc(lg_read, 1)
                    dve.wait_ge(lg_read, p + 1)
                    step(dve.tensor_reduce(rt[:, 0, 0:1], lg[:, :], AX, ALU.max))
                    dve.tensor_scalar(rt[:, 1, 0:1], rt[:, 0, 0:1], -1.0, None, ALU.mult).then_inc(lg_negmax, 1)
                    other = lg[:, :].unsqueeze(1).to_broadcast([P, E, E])
                    own = lg[:, :].unsqueeze(2).to_broadcast([P, E, E])
                    step(dve.tensor_tensor(gtr[:, :, :], other, own, ALU.is_gt))
                    step(dve.tensor_tensor(eqr[:, :, :], other, own, ALU.is_equal))
                    step(dve.tensor_tensor(eqr[:, :, :], eqr[:, :, :], before[:, :, :], ALU.mult))
                    step(dve.tensor_tensor(gtr[:, :, :], gtr[:, :, :], eqr[:, :, :], ALU.add))
                    step(dve.tensor_reduce(rt[:, 3, :], gtr[:, :, :], AX, ALU.add))
                    step(dve.tensor_scalar(rt[:, 3, :], rt[:, 3, :], 2.0, None, ALU.is_lt))
                    dve.wait_ge(lg_exp, p + 1)
                    step(dve.tensor_tensor(rt[:, 4, :], rt[:, 3, :], rt[:, 2, :], ALU.mult))
                    step(dve.tensor_reduce(rt[:, 5, 0:1], rt[:, 4, :], AX, ALU.add))
                    step(dve.reciprocal(rt[:, 5, 1:2], rt[:, 5, 0:1]))
                    step(dve.tensor_scalar(rt[:, 6, :], rt[:, 4, :], rt[:, 5, 1:2], None, ALU.mult))
                    assert n.n == ROUTE_STEPS, n.n

                def low_parts(s):
                    for piece in range(2 * s, 2 * s + 2):
                        k, r = piece // PIECES, piece % PIECES
                        dve.wait_ge(piece_hi, piece + 1)
                        at = slice(r * PIECE, (r + 1) * PIECE)
                        dve.tensor_tensor(experts_lo[EARLY + k][:, :, at], stage[:, piece % STAGES, :, :].rearrange("p r e -> p e r"),
                                          experts_hi[EARLY + k][:, :, at].bitcast(F32), ALU.subtract).then_inc(experts_ready, 1)

                def pair(p, u, mix, nxt):
                    def finish(s):
                        b = s // 4
                        if s % 4 == 3:
                            dve.wait_ge(prob_ready, p * 8 + (s + 1))
                            dve.reciprocal(rinv[:, 4 * b:4 * b + 4], rsum[:, 4 * b:4 * b + 4]).then_inc(rinv_step, 1)
                        if mix is not None:
                            if s == 0:
                                dve.wait_ge(acc_loaded[1 - u], (mix - (1 - u)) * 8 + 16)
                            mix_add(mix, 1 - u, s)
                        if s % 4 == 3:
                            dve.wait_ge(rinv_step, p * 2 + (b + 1))
                            dve.wait_ge(o_ps, p * 2 + (b + 5))
                            dve.tensor_tensor(o_sb[:, b, :].rearrange("p (g d) -> p g d", g=G),
                                              bk(2 if b else 6)[:, 0:G * HD].rearrange("p (g d) -> p g d", g=G),
                                              rinv[:, 4 * b:4 * b + 4].unsqueeze(2).to_broadcast([P, G, HD]), ALU.mult).then_inc(o_ready, 1)

                    dve.wait_ge(mask_step, p * 4 + 4)
                    for s in range(8):
                        dve.wait_ge(score_ps, p * 8 + (s + 1))
                        dve.wait_ge(pT_ps, p * 8 + (s + 1))
                        dve.sem_inc(score_taken, 1)
                        dve.tensor_tensor_reduce(prob[:, s % 2, :], bk(s % 2)[:, 0:KEYS], mask[:, s // 4, :], 1.0, MASKED,
                                                 ALU.add, ALU.max, mx[:, s:s + 1]).then_inc(sm_ready, 1)
                        dve.wait_ge(sm_ready, p * 8 + (s + 3))
                        dve.tensor_scalar(nmx[:, s:s + 1], mx[:, s:s + 1], -SCALE, None, ALU.mult).then_inc(nmx_ready, 1)
                        if s == 1 and mix is not None:
                            route(mix)
                        if s >= 1:
                            finish(s - 1)
                        if 1 <= s < 7 and mix is None:
                            low_parts(s - 1)
                        if s == 5 and nxt is not None:
                            make_mask(nxt[0], 0)
                    if nxt is not None:
                        make_mask(nxt[0], 1)
                    finish(7)
                    if mix is None:
                        low_parts(6)
                        low_parts(7)
                    if nxt is not None:
                        kT_copy(nxt[0], 0)
                        qT_copy(nxt[0])
                    dve.wait_ge(yT_ready, p * 2 + 1)
                    dve.tensor_tensor(yT_lo[:, :, :], bk(2).rearrange("p (k n) -> p k n", n=P), yT_hi[:, :, :].bitcast(F32),
                                      ALU.subtract).then_inc(yT_ready, 1)
                    if nxt is not None:
                        kT_copy(nxt[0], 1)

                dve.tensor_copy(route_hi[:, :, :], route_w[:, :, :]).then_inc(route_split, 1)
                dve.wait_ge(route_split, 1)
                dve.tensor_tensor(route_lo[:, :, :], route_w[:, :, :], route_hi[:, :, :].bitcast(F32), ALU.subtract).then_inc(route_split, 1)
                make_mask(0, 0)
                make_mask(0, 1)
                qT_copy(0)
                kT_copy(0, 0)
                kT_copy(0, 1)
                each_pair(dve, pair)
                route(PAIRS - 1)
                dve.wait_ge(acc_loaded[1], 16 * (PAIRS // 2))
                for e in range(E):
                    mix_add(PAIRS - 1, 1, e)



def _arrays(inputs):
    i = {k: np.asarray(v) for k, v in inputs.items()}
    heads = [(2 * gp + g) * 2 + h2 for gp in range(2) for h2 in range(2) for g in range(2)]
    wq = i["L1_cond_Wq"].reshape(H, HD, T)[heads].reshape(H * HD, T)
    wo = i["L1_cond_Wo"].reshape(T, H, HD)[:, heads].reshape(T, H * HD)
    kc, vc = (i[f"L1_cond_{n}_blocks"].transpose(0, 2, 1, 3).reshape(POOL_ROWS, G * HD) for n in "kv")
    half = np.arange(HALF, dtype=np.float32) / np.float32(HALF)
    return {
        "x": i["x"].reshape(TOK, T),
        "kv_lens": i["itok_B_37_3939"],
        "subjects": i["itok_B_0_7"].reshape(1, B),
        "tables": i["itok_Bx257_0_4111"].reshape(B * NBLK),
        "cond_w": i["L0_cond_weights"],
        "gate_t": i["L0_ffn_gate_w"].T,
        "up_t": i["L0_ffn_up_w"].T,
        "down_t": i["L0_ffn_down_w"].T,
        "gate_s": i["L0_ffn_gate_s"].reshape(IT, P).T,
        "up_s": i["L0_ffn_up_s"].reshape(IT, P).T,
        "down_s": i["L0_ffn_down_s"].reshape(1, T),
        "wqkv_t": np.concatenate([wq, i["L1_cond_Wk"], i["L1_cond_Wv"]]).T,
        "wo_t": wo.T,
        "q_norm": i["L1_cond_q_norm_scale"].reshape(1, HD),
        "k_norm": i["L1_cond_k_norm_scale"].reshape(1, HD),
        "kv_cache": np.concatenate([kc, vc], axis=1),
        "inv_freq": (np.float32(1.0) / np.float32(10000.0) ** half).reshape(1, HALF),
        "route_t": i["L1_ffn_gate_w"].T,
        "w_t": i["L1_ffn_W"].T,
        "atoms": i["L1_ffn_atoms"].reshape(A, P, SCH).transpose(0, 2, 1),
        "expert_atom": i["L1_ffn_expert_atom_weights"],
        "importance": i["L1_ffn_importance"].T.reshape(P, SCH, E),
        "mask_col": i["L1_ffn_mask_idx"].reshape(P, SCH),
        "mask_row": i["L1_ffn_mask_idx"].reshape(P, SCH).T,
    }


def kernel(**inputs):
    import numpy as _np
    import concourse.bacc as _bacc
    from concourse import mybir as _mybir
    from concourse.bass_utils import run_bass_kernel_spmd as _run

    nc = _bacc.Bacc("TRN2", target_bir_lowering=False, num_devices=1)
    arrays, args = {}, {}
    for name, a in _arrays(inputs).items():
        a = _np.ascontiguousarray(a)
        arrays[f"in_{name}"] = a
        args[name] = nc.dram_tensor(f"in_{name}", a.shape, _mybir.dt.from_np(a.dtype), kind="ExternalInput").ap()
    args["out"] = nc.dram_tensor("out_dram", (TOK, T), F32, kind="ExternalOutput").ap()
    bass_adaln_ffn_kernel(nc, **args)
    r = _run(nc, [arrays], core_ids=[0])
    return r.results[0]["out_dram"].reshape(B, C, T)
```
